# Optimizing a Trainium2 kernel written in Bass

```python
import numpy as np
import jax
import jax.numpy as jnp

def _softmax(x, axis=-1):
    return jax.nn.softmax(x, axis=axis)

def _gelu(x):
    return jax.nn.gelu(x, approximate=True)

def _silu(x):
    return jax.nn.silu(x)

def _sigmoid(x):
    return jax.nn.sigmoid(x)

def _layernorm(x, axis=-1, eps=1e-05):
    m = jnp.mean(x, axis=axis, keepdims=True)
    v = jnp.var(x, axis=axis, keepdims=True)
    return (x - m) / jnp.sqrt(v + eps)

def _scatter_add(tgt, idx, src, axis=0):
    return tgt.at[idx].add(src)

def _segment_sum(src, seg, n):
    return jax.ops.segment_sum(src, seg, n)
kernel_name = 'mk_early_fusion_embed_d1_tok_img768_r4_079c2a'

def setup_inputs(seed: int=0):
    np.random.seed(seed)
    _w = jnp.asarray

    def _rec_inputs():
        import jax
        import jax.numpy as jnp
        _rk = jax.random.key(seed)
        x = -0.000348323 + 0.999952 * jax.random.normal(jax.random.fold_in(_rk, 1), (32, 3, 224, 224), jnp.float32)
        x_txt = jax.random.randint(jax.random.fold_in(_rk, 51), (32, 77), 0, 31993, jnp.int32)
        return (x, x_txt)
    x, x_txt = _rec_inputs()

    def _L0_tok_setup():
        import jax, jax.numpy as jnp
        import numpy as np
        PATCH = 16

        def _shifted_concat(x):
            B, C, H, W = x.shape
            xp = jnp.pad(x, ((0, 0), (0, 0), (1, 1), (1, 1)))
            right = xp[:, :, 1:1 + H, 0:W]
            left = xp[:, :, 1:1 + H, 2:2 + W]
            down = xp[:, :, 0:H, 1:1 + W]
            up = xp[:, :, 2:2 + H, 1:1 + W]
            return jnp.concatenate([x, right, left, down, up], axis=1)

        def _patchify(x, p):
            B, C, H, W = x.shape
            h, w = (H // p, W // p)
            x = x.reshape(B, C, h, p, w, p)
            x = x.transpose(0, 2, 4, 3, 5, 1)
            return x.reshape(B, h * w, p * p * C)

        def _layernorm(x, gamma, beta, eps=1e-05):
            mu = jnp.mean(x, axis=-1, keepdims=True)
            var = jnp.var(x, axis=-1, keepdims=True)
            return (x - mu) * jax.lax.rsqrt(var + eps) * gamma + beta
        key = jax.random.key(seed)
        k1, k2 = jax.random.split(key)
        B, H, W = (32, 96, 96)
        patch_dim = PATCH * PATCH * 15
        d_hidn = 192
        x = jax.random.normal(k1, (B, 3, H, W), dtype=jnp.float32)
        gamma = jnp.ones((patch_dim,), dtype=jnp.float32)
        beta = jnp.zeros((patch_dim,), dtype=jnp.float32)
        W_ = jax.random.normal(k2, (patch_dim, d_hidn), dtype=jnp.float32) * patch_dim ** (-0.5)
        b = jnp.zeros((d_hidn,), dtype=jnp.float32)
        return {'x': x, 'gamma': gamma, 'beta': beta, 'W': W_, 'b': b}
    _L0_tok_all = _L0_tok_setup()
    _L0_tok_in = {k: v for k, v in _L0_tok_all.items() if k in ('gamma', 'beta', 'W', 'b')}
    del _L0_tok_all

    def _L0_txt_setup():
        import jax, jax.numpy as jnp
        import numpy as np
        NUM_HEADS = 12
        EPS = 1e-05

        def _layer_norm(x, gamma, beta):
            mean = jnp.mean(x, axis=-1, keepdims=True)
            std = jnp.sqrt(jnp.mean((x - mean) ** 2, axis=-1, keepdims=True))
            return (x - mean) / (std + EPS) * gamma + beta

        def _pos_encoding(L, D, dtype):
            pos = jnp.arange(L, dtype=dtype)[:, None]
            i = jnp.arange(D, dtype=dtype)[None, :]
            ang = pos / jnp.power(jnp.asarray(10000.0, dtype), 2.0 * i / D)
            even = jnp.arange(D) % 2 == 0
            return jnp.where(even[None, :], jnp.cos(ang), jnp.sin(ang))
        key = jax.random.key(seed)
        ks = jax.random.split(key, 12)
        B, L, D, F, V = (4, 512, 192, 768, 8000)
        s = lambda d: 1.0 / np.sqrt(d)
        return {'tokens': jax.random.randint(ks[0], (B, L), 0, V, dtype=jnp.int32), 'emb': jax.random.normal(ks[1], (V, D), jnp.float32) * 0.02, 'wq': jax.random.normal(ks[2], (D, D), jnp.float32) * s(D), 'bq': jnp.zeros((D,), jnp.float32), 'wk': jax.random.normal(ks[3], (D, D), jnp.float32) * s(D), 'bk': jnp.zeros((D,), jnp.float32), 'wv': jax.random.normal(ks[4], (D, D), jnp.float32) * s(D), 'bv': jnp.zeros((D,), jnp.float32), 'wo': jax.random.normal(ks[5], (D, D), jnp.float32) * s(D), 'bo': jnp.zeros((D,), jnp.float32), 'w1': jax.random.normal(ks[6], (D, F), jnp.float32) * s(D), 'b1': jnp.zeros((F,), jnp.float32), 'w2': jax.random.normal(ks[7], (F, D), jnp.float32) * s(F), 'b2': jnp.zeros((D,), jnp.float32), 'gamma1': jnp.ones((D,), jnp.float32), 'beta1': jnp.zeros((D,), jnp.float32), 'gamma2': jnp.ones((D,), jnp.float32), 'beta2': jnp.zeros((D,), jnp.float32)}
    _L0_txt_all = _L0_txt_setup()
    _L0_txt_in = {k: v for k, v in _L0_txt_all.items() if k in ('emb', 'wq', 'bq', 'wk', 'bk', 'wv', 'bv', 'wo', 'bo', 'w1', 'b1', 'w2', 'b2', 'gamma1', 'beta1', 'gamma2', 'beta2')}
    del _L0_txt_all

    def _L0_attn_setup():
        import jax, jax.numpy as jnp
        import numpy as np
        NUM_HEADS = 12
        Q_BITS = 8

        def fake_quant(x, bits=Q_BITS):
            qmax = 2.0 ** (bits - 1) - 1.0
            scale = jnp.maximum(jnp.max(jnp.abs(x)) / qmax, 1e-08)
            q = jnp.clip(jnp.round(x / scale), -qmax - 1.0, qmax) * scale
            return x + jax.lax.stop_gradient(q - x)
        key = jax.random.key(seed)
        ks = jax.random.split(key, 5)
        B, N, C = (8, 256, 192)
        x = jax.random.normal(ks[0], (B, N, C), dtype=jnp.float32)
        w_qkv = jax.random.normal(ks[1], (C, 3 * C), dtype=jnp.float32) * 0.02
        b_qkv = jax.random.normal(ks[2], (3 * C,), dtype=jnp.float32) * 0.02
        w_proj = jax.random.normal(ks[3], (C, C), dtype=jnp.float32) * 0.02
        b_proj = jax.random.normal(ks[4], (C,), dtype=jnp.float32) * 0.02
        return {'x': x, 'w_qkv': w_qkv, 'b_qkv': b_qkv, 'w_proj': w_proj, 'b_proj': b_proj}
    _L0_attn_all = _L0_attn_setup()
    _L0_attn_in = {k: v for k, v in _L0_attn_all.items() if k in ('w_qkv', 'b_qkv', 'w_proj', 'b_proj')}
    del _L0_attn_all

    def _L0_ffn_setup():
        import jax, jax.numpy as jnp
        import numpy as np
        GT0 = [[0, 1, 0, 0, 1, 0], [0, 1, 0, 0, 0, 1], [0, 0, 1, 0, 1, 0], [0, 0, 1, 0, 0, 1], [0, 0, 0, 1, 1, 0], [0, 0, 0, 1, 0, 1]]
        NCLS = 6
        K = 1

        def _expert_pairs():
            pairs = []
            for i in range(NCLS):
                p = [(j - 1, k - 1) for j in range(1, 6) for k in range(1, 6) if j != k and GT0[i][j] == 1 and (GT0[i][k] == 1)]
                pairs.append(p)
            return pairs
        PAIRS = _expert_pairs()
        B, P, D, H = (64, 64, 192, 768)

        def _gelu(t):
            return jax.nn.gelu(t, approximate=False)
        key = jax.random.key(seed)
        ks = jax.random.split(key, 8)
        s = 0.02
        x = jax.random.normal(ks[0], (B, NCLS + P, D), dtype=jnp.float32)
        mids = jax.random.randint(ks[1], (B,), 0, 6)
        moe0_W1 = jax.random.normal(ks[2], (D, H), dtype=jnp.float32) * s
        moe0_b1 = jnp.zeros((H,), jnp.float32)
        moe0_W2 = jax.random.normal(ks[3], (H, D), dtype=jnp.float32) * s
        moe0_b2 = jnp.zeros((D,), jnp.float32)
        A1_W = jax.random.normal(ks[4], (5, D, H), dtype=jnp.float32) * s
        A1_b = jnp.zeros((5, H), jnp.float32)
        A2_W = jax.random.normal(ks[5], (5, H, D), dtype=jnp.float32) * s
        A2_b = jnp.zeros((5, D), jnp.float32)
        G_W = jax.random.normal(ks[6], (NCLS, D, 2), dtype=jnp.float32) * s
        return {'x': x, 'moe0_W1': moe0_W1, 'moe0_b1': moe0_b1, 'moe0_W2': moe0_W2, 'moe0_b2': moe0_b2, 'A1_W': A1_W, 'A1_b': A1_b, 'A2_W': A2_W, 'A2_b': A2_b, 'G_W': G_W, 'mids': mids}
    _L0_ffn_all = _L0_ffn_setup()
    _L0_ffn_in = {k: v for k, v in _L0_ffn_all.items() if k in ('moe0_W1', 'moe0_b1', 'moe0_W2', 'moe0_b2', 'A1_W', 'A1_b', 'A2_W', 'A2_b', 'G_W', 'mids')}
    del _L0_ffn_all
    return {'x': x, 'x_txt': x_txt, 'L0_tok_gamma': _L0_tok_in['gamma'], 'L0_tok_beta': _L0_tok_in['beta'], 'L0_tok_W': _L0_tok_in['W'], 'L0_tok_b': _L0_tok_in['b'], 'L0_txt_emb': _L0_txt_in['emb'], 'L0_txt_wq': _L0_txt_in['wq'], 'L0_txt_bq': _L0_txt_in['bq'], 'L0_txt_wk': _L0_txt_in['wk'], 'L0_txt_bk': _L0_txt_in['bk'], 'L0_txt_wv': _L0_txt_in['wv'], 'L0_txt_bv': _L0_txt_in['bv'], 'L0_txt_wo': _L0_txt_in['wo'], 'L0_txt_bo': _L0_txt_in['bo'], 'L0_txt_w1': _L0_txt_in['w1'], 'L0_txt_b1': _L0_txt_in['b1'], 'L0_txt_w2': _L0_txt_in['w2'], 'L0_txt_b2': _L0_txt_in['b2'], 'L0_txt_gamma1': _L0_txt_in['gamma1'], 'L0_txt_beta1': _L0_txt_in['beta1'], 'L0_txt_gamma2': _L0_txt_in['gamma2'], 'L0_txt_beta2': _L0_txt_in['beta2'], 'L0_attn_w_qkv': _L0_attn_in['w_qkv'], 'L0_attn_b_qkv': _L0_attn_in['b_qkv'], 'L0_attn_w_proj': _L0_attn_in['w_proj'], 'L0_attn_b_proj': _L0_attn_in['b_proj'], 'L0_ffn_moe0_W1': _L0_ffn_in['moe0_W1'], 'L0_ffn_moe0_b1': _L0_ffn_in['moe0_b1'], 'L0_ffn_moe0_W2': _L0_ffn_in['moe0_W2'], 'L0_ffn_moe0_b2': _L0_ffn_in['moe0_b2'], 'L0_ffn_A1_W': _L0_ffn_in['A1_W'], 'L0_ffn_A1_b': _L0_ffn_in['A1_b'], 'L0_ffn_A2_W': _L0_ffn_in['A2_W'], 'L0_ffn_A2_b': _L0_ffn_in['A2_b'], 'L0_ffn_G_W': _L0_ffn_in['G_W'], 'L0_ffn_mids': _L0_ffn_in['mids']}

def reference(x, x_txt, L0_tok_gamma, L0_tok_beta, L0_tok_W, L0_tok_b, L0_txt_emb, L0_txt_wq, L0_txt_bq, L0_txt_wk, L0_txt_bk, L0_txt_wv, L0_txt_bv, L0_txt_wo, L0_txt_bo, L0_txt_w1, L0_txt_b1, L0_txt_w2, L0_txt_b2, L0_txt_gamma1, L0_txt_beta1, L0_txt_gamma2, L0_txt_beta2, L0_attn_w_qkv, L0_attn_b_qkv, L0_attn_w_proj, L0_attn_b_proj, L0_ffn_moe0_W1, L0_ffn_moe0_b1, L0_ffn_moe0_W2, L0_ffn_moe0_b2, L0_ffn_A1_W, L0_ffn_A1_b, L0_ffn_A2_W, L0_ffn_A2_b, L0_ffn_G_W, L0_ffn_mids):
    import jax
    import jax.numpy as jnp

    def _L0_tok_ref(x, gamma, beta, W, b):
        import jax, jax.numpy as jnp
        import numpy as np
        PATCH = 16

        def _shifted_concat(x):
            B, C, H, W = x.shape
            xp = jnp.pad(x, ((0, 0), (0, 0), (1, 1), (1, 1)))
            right = xp[:, :, 1:1 + H, 0:W]
            left = xp[:, :, 1:1 + H, 2:2 + W]
            down = xp[:, :, 0:H, 1:1 + W]
            up = xp[:, :, 2:2 + H, 1:1 + W]
            return jnp.concatenate([x, right, left, down, up], axis=1)

        def _patchify(x, p):
            B, C, H, W = x.shape
            h, w = (H // p, W // p)
            x = x.reshape(B, C, h, p, w, p)
            x = x.transpose(0, 2, 4, 3, 5, 1)
            return x.reshape(B, h * w, p * p * C)

        def _layernorm(x, gamma, beta, eps=1e-05):
            mu = jnp.mean(x, axis=-1, keepdims=True)
            var = jnp.var(x, axis=-1, keepdims=True)
            return (x - mu) * jax.lax.rsqrt(var + eps) * gamma + beta
        xs = _shifted_concat(x)
        tokens = _patchify(xs, PATCH)
        normed = _layernorm(tokens, gamma, beta)
        return jnp.einsum('bnd,de->bne', normed, W) + b

    def _L0_txt_ref(tokens, emb, wq, bq, wk, bk, wv, bv, wo, bo, w1, b1, w2, b2, gamma1, beta1, gamma2, beta2):
        import jax, jax.numpy as jnp
        import numpy as np
        NUM_HEADS = 12
        EPS = 1e-05

        def _layer_norm(x, gamma, beta):
            mean = jnp.mean(x, axis=-1, keepdims=True)
            std = jnp.sqrt(jnp.mean((x - mean) ** 2, axis=-1, keepdims=True))
            return (x - mean) / (std + EPS) * gamma + beta

        def _pos_encoding(L, D, dtype):
            pos = jnp.arange(L, dtype=dtype)[:, None]
            i = jnp.arange(D, dtype=dtype)[None, :]
            ang = pos / jnp.power(jnp.asarray(10000.0, dtype), 2.0 * i / D)
            even = jnp.arange(D) % 2 == 0
            return jnp.where(even[None, :], jnp.cos(ang), jnp.sin(ang))
        B, L = tokens.shape
        D = emb.shape[1]
        H = NUM_HEADS
        dh = D // H
        x = emb[tokens] + _pos_encoding(L, D, emb.dtype)

        def heads(t):
            return t.reshape(B, L, H, dh).transpose(0, 2, 1, 3)
        q = heads(x @ wq + bq)
        k = heads(x @ wk + bk)
        v = heads(x @ wv + bv)
        scores = jnp.einsum('bhqd,bhkd->bhqk', q, k) / jnp.sqrt(jnp.asarray(dh, x.dtype))
        weights = jax.nn.softmax(scores, axis=-1)
        attn = jnp.einsum('bhqk,bhkd->bhqd', weights, v)
        attn = attn.transpose(0, 2, 1, 3).reshape(B, L, D)
        attn_out = attn @ wo + bo
        h1 = _layer_norm(x + attn_out, gamma1, beta1)
        ff = jax.nn.relu(h1 @ w1 + b1) @ w2 + b2
        return _layer_norm(h1 + ff, gamma2, beta2)

    def _L0_attn_ref(x, w_qkv, b_qkv, w_proj, b_proj):
        import jax, jax.numpy as jnp
        import numpy as np
        NUM_HEADS = 12
        Q_BITS = 8

        def fake_quant(x, bits=Q_BITS):
            qmax = 2.0 ** (bits - 1) - 1.0
            scale = jnp.maximum(jnp.max(jnp.abs(x)) / qmax, 1e-08)
            q = jnp.clip(jnp.round(x / scale), -qmax - 1.0, qmax) * scale
            return x + jax.lax.stop_gradient(q - x)
        B, N, C = x.shape
        H = NUM_HEADS
        hd = C // H
        scale = hd ** (-0.5)
        qkv = fake_quant(x) @ fake_quant(w_qkv) + b_qkv
        qkv = qkv.reshape(B, N, 3, H, hd).transpose(2, 0, 3, 1, 4)
        q, k, v = (qkv[0], qkv[1], qkv[2])
        attn = jnp.einsum('bhnd,bhmd->bhnm', fake_quant(q), fake_quant(k))
        attn = attn * scale
        attn = fake_quant(jax.nn.softmax(attn, axis=-1))
        out = jnp.einsum('bhnm,bhmd->bhnd', attn, fake_quant(v))
        out = out.transpose(0, 2, 1, 3).reshape(B, N, C)
        out = fake_quant(out) @ fake_quant(w_proj) + b_proj
        return out

    def _L0_ffn_ref(x, moe0_W1, moe0_b1, moe0_W2, moe0_b2, A1_W, A1_b, A2_W, A2_b, G_W, mids):
        import jax, jax.numpy as jnp
        import numpy as np
        GT0 = [[0, 1, 0, 0, 1, 0], [0, 1, 0, 0, 0, 1], [0, 0, 1, 0, 1, 0], [0, 0, 1, 0, 0, 1], [0, 0, 0, 1, 1, 0], [0, 0, 0, 1, 0, 1]]
        NCLS = 6
        K = 1

        def _expert_pairs():
            pairs = []
            for i in range(NCLS):
                p = [(j - 1, k - 1) for j in range(1, 6) for k in range(1, 6) if j != k and GT0[i][j] == 1 and (GT0[i][k] == 1)]
                pairs.append(p)
            return pairs
        PAIRS = _expert_pairs()
        B, P, D, H = (64, 64, 192, 768)

        def _gelu(t):
            return jax.nn.gelu(t, approximate=False)
        cls_tokens = x[:, :NCLS]
        patch_tokens = x[:, NCLS:]
        patch_out = _gelu(patch_tokens @ moe0_W1 + moe0_b1) @ moe0_W2 + moe0_b2
        cls_outs = []
        for i in range(NCLS):
            tok = cls_tokens[:, i]
            eouts = [_gelu(tok @ A1_W[a] + A1_b[a]) @ A2_W[c] + A2_b[c] for a, c in PAIRS[i]]
            out = jnp.stack(eouts, axis=-1)
            gate = jax.nn.softmax(tok @ G_W[i], axis=-1)
            thr = jnp.sort(gate, axis=-1)[..., -(K + 1)]
            mask = (gate > thr[..., None]).astype(gate.dtype)
            g = gate * mask
            g = g / jnp.clip(jnp.sum(g, axis=-1, keepdims=True), 1e-06)
            cls_outs.append(jnp.sum(out * g[:, None, :], axis=-1))
        cls_out = jnp.stack(cls_outs, axis=1)
        return jnp.concatenate([cls_out, patch_out], axis=1)
    h = _L0_tok_ref(x, L0_tok_gamma, L0_tok_beta, L0_tok_W, L0_tok_b)
    h = jnp.concatenate([h, _L0_txt_ref(x_txt, L0_txt_emb, L0_txt_wq, L0_txt_bq, L0_txt_wk, L0_txt_bk, L0_txt_wv, L0_txt_bv, L0_txt_wo, L0_txt_bo, L0_txt_w1, L0_txt_b1, L0_txt_w2, L0_txt_b2, L0_txt_gamma1, L0_txt_beta1, L0_txt_gamma2, L0_txt_beta2)], axis=1)
    h = h + _L0_attn_ref(_layernorm(h, axis=-1), L0_attn_w_qkv, L0_attn_b_qkv, L0_attn_w_proj, L0_attn_b_proj)
    h = h + _L0_ffn_ref(_layernorm(h, axis=-1), L0_ffn_moe0_W1, L0_ffn_moe0_b1, L0_ffn_moe0_W2, L0_ffn_moe0_b2, L0_ffn_A1_W, L0_ffn_A1_b, L0_ffn_A2_W, L0_ffn_A2_b, L0_ffn_G_W, L0_ffn_mids)
    return h

_drawn_inputs = setup_inputs


def setup_inputs(seed=0):
    import zlib

    import numpy as np

    out = dict(_drawn_inputs(seed))
    spreads = {'L0_tok_gamma': (1.0, 0.2),
     'L0_tok_beta': (0.0, 0.1),
     'L0_tok_b': (0.0, 0.1),
     'L0_txt_bq': (0.0, 0.8),
     'L0_txt_bk': (0.0, 2.0),
     'L0_txt_bv': (0.0, 0.1),
     'L0_txt_bo': (0.0, 0.1),
     'L0_txt_b1': (0.0, 0.282),
     'L0_txt_b2': (0.0, 0.1),
     'L0_txt_gamma1': (1.0, 0.2),
     'L0_txt_beta1': (0.0, 0.1),
     'L0_txt_gamma2': (1.0, 0.2),
     'L0_txt_beta2': (0.0, 0.1),
     'L0_ffn_moe0_b1': (0.0, 0.286),
     'L0_ffn_moe0_b2': (0.0, 0.1),
     'L0_ffn_A1_b': (0.0, 0.8),
     'L0_ffn_A2_b': (0.0, 0.56)}
    factors = {'L0_txt_emb': 4.37,
     'L0_txt_wq': 5.06,
     'L0_txt_wk': 4.56,
     'L0_attn_w_qkv': 2.722,
     'L0_attn_b_qkv': 8.0,
     'L0_attn_b_proj': 3.085,
     'L0_ffn_A1_W': 4.988,
     'L0_ffn_A2_W': 4.575,
     'L0_ffn_G_W': 4.33}
    for name, (base, spread) in spreads.items():
        noise = np.random.default_rng([zlib.crc32(name.encode()), seed]).standard_normal(out[name].shape)
        drawn = base * np.exp(spread * noise) if base else spread * noise
        out[name] = jnp.asarray(drawn.astype(out[name].dtype))
    for name, factor in factors.items():
        out[name] = (out[name] * factor).astype(out[name].dtype)
    return out
```

```python
from contextlib import ExitStack

import numpy as np

import concourse.bass as bass
from concourse import mybir

F32 = mybir.dt.float32
BF16 = mybir.dt.bfloat16
I32 = mybir.dt.int32
U32 = mybir.dt.uint32
ALU = mybir.AluOpType
ACT = mybir.ActivationFunctionType
AX = mybir.AxisListType
RMAX = bass.bass_isa.ReduceOp.max

B = 32
IMG, PATCH, CH = 224, 16, 3
GRID = IMG // PATCH
NIMG = GRID * GRID
NTXT = 77
N = NIMG + NTXT
D = 192
D2 = D - 128
HEADS, DH = 12, 16
F = 768
FT = F // 128
VOCAB = 8000
NCLS = 6
TOKENS = B * N
FEAT = PATCH * PATCH * 5 * CH
EPS = 1e-5
QMAX = 127.0
SCALE_FLOOR = 1e-8
ROUND = 1.5 * 2.0 ** 23

KP, KT = 120, 8
STEPS = 7
TILES = 7
IPT = 128 // B

TG = 4
TGROUPS = B // TG

NE = N + 1
SX, SW, SWP = 0, 1, 2
ISX, ISW, ISWP = 3, 4, 5
SXW, ISXW = 6, 7
SQKV, IQKV = 8, 11
AQKV = 14
ALPHA, IALPHA = 17, 18
SP_, LNSP, SO_IN = 19, 20, 21
SOUT, ISOUT, AOUT, HOUT = 22, 23, 24, 25
TMP = 26
NSC = 40


def counts():
    pix = []
    for y in range(-1, PATCH + 1):
        for x in range(-1, PATCH + 1):
            src = []
            for dy, dx in ((0, 0), (0, 1), (0, -1), (1, 0), (-1, 0)):
                py, px = y + dy, x + dx
                ok = 0 <= py < PATCH and 0 <= px < PATCH
                src.append(py * PATCH + px if ok else -1)
            n = sum(s >= 0 for s in src)
            if n:
                pix.append((n, y, x, src))
    five = [p for p in pix if p[0] == 5]
    four = [p for p in pix if p[0] == 4]
    three = [p for p in pix if p[0] == 3]
    one = [p for p in pix if p[0] == 1]
    return five + three + four + one


class Mem:

    def __init__(self, nc, ctx, tag):
        self.nc, self.ctx, self.tag, self.sems = nc, ctx, tag, []
        ctx.callback(self.clear)

    def clear(self):
        if self.sems:
            self.nc.clear_and_free_semaphores(self.sems)
            self.nc.all_engine_barrier()

    def sb(self, name, shape, dt=F32):
        return self.ctx.enter_context(self.nc.sbuf_tensor(f"{self.tag}_{name}", shape, dt))

    def ps(self, name, shape, dt=F32):
        return self.ctx.enter_context(self.nc.psum_tensor(f"{self.tag}_{name}", shape, dt))

    def sem(self, name):
        self.sems.append(self.nc.alloc_semaphore(f"{self.tag}_{name}"))
        return self.sems[-1]


class Chain:

    def __init__(self, eng, sem):
        self.eng, self.sem, self.base, self.step, self.per, self.k = eng, sem, 0, None, 0, 0

    def loop(self, step, per):
        self.step, self.per, self.k, self.start = step, per, 0, self.base

    def end(self, count):
        assert self.k == self.per, (self.k, self.per)
        self.base, self.step, self.k = self.start + self.per * count, None, 0

    def __call__(self, ins):
        ins.then_inc(self.sem, 1)
        if self.step is None:
            self.base += 1
            self.eng.wait_ge(self.sem, self.base)
        else:
            self.k += 1
            self.eng.wait_ge(self.sem, self.step * self.per + (self.start + self.k))


def pool_copy(pool, out, src, one):
    while len(one.shape) < len(src.shape):
        one = one.unsqueeze(len(one.shape))
    return pool.tensor_tensor(out, src, one.to_broadcast(list(src.shape)), ALU.mult)


def image_phase(nc, T, C):
    LAG = 3
    with ExitStack() as ctx:
        m = Mem(nc, ctx, "im")
        wsh = m.sb("wsh", [KP, KT, 5, D])
        gsh = m.sb("gsh", [KP, KT, 5])
        bsh = m.sb("bsh", [KP, KT, 5])
        cntw = m.sb("cntw", [KP, KT])
        rootw = m.sb("rootw", [KP, KT])
        weff = m.sb("weff", [KP, KT, D + 1])
        brow = m.sb("brow", [128, D])
        gsum = m.sb("gsum", [128, D])
        bias = m.sb("bias", [128, D])
        ones = m.sb("ones", [KP, 128])
        xt = m.sb("xt", [KP, TILES, KT, 128])
        sq = m.sb("sq", [KP, TILES, KT, 128])
        sqs = m.sb("sqs", [KP, TILES, 128])
        u = m.sb("u", [128, TILES, D + 2])
        mean2 = m.sb("mean2", [128, TILES])
        var = m.sb("var", [128, TILES])
        rstd = m.sb("rstd", [128, TILES])
        nmean = m.sb("nmean", [128, TILES])
        z = m.sb("z", [128, TILES, D])
        h = m.sb("h", [128, TILES, D])
        bn = m.sb("bn", [128, TILES, 6])
        mv = m.sb("mv", [128, TILES, 2])
        hvar = m.sb("hvar", [128, TILES])
        hrstd = m.sb("hrstd", [128, TILES])
        y = m.sb("y", [128, TILES, D])
        ymx = m.sb("ymx", [128, 1])
        gap = m.sb("gap", [1, 1])
        psx = [m.ps(f"psx{i}", [128, 512]) for i in range(TILES)]
        psb = m.ps("psb", [128, 2, 256])

        w_loaded = m.sem("w_loaded")
        x_loaded = [m.sem(f"x_loaded{s}") for s in range(TILES)]
        taken = [m.sem(f"taken{s}") for s in range(TILES)]
        ones_set = m.sem("ones_set")
        weff_done = m.sem("weff_done")
        rows_done = m.sem("rows_done")
        bias_set = m.sem("bias_set")
        squared = m.sem("squared")
        sq_summed = m.sem("sq_summed")
        projected = m.sem("projected")
        var_done = m.sem("var_done")
        rstd_done = m.sem("rstd_done")
        u_used = m.sem("u_used")
        h_done = m.sem("h_done")
        hvar_done = m.sem("hvar_done")
        hrstd_done = m.sem("hrstd_done")
        y_done = m.sem("y_done")
        h_stored = m.sem("h_stored")
        y_stored = m.sem("y_stored")
        vchain = m.sem("vchain")

        with nc.Block() as block:

            @block.sync
            def _(sp):
                sp.dma_start(gsh[:, :, :], T["gsh"]).then_inc(w_loaded, 16)
                sp.dma_start(bsh[:, :, :], T["bsh"]).then_inc(w_loaded, 16)
                sp.dma_start(cntw[:, :], T["cntw"]).then_inc(w_loaded, 16)
                sp.dma_start(rootw[:, :], T["rootw"]).then_inc(w_loaded, 16)
                sp.dma_start(wsh[:, :, :, :], T["wsh"]).then_inc(w_loaded, 16)
                sp.dma_start(brow[:, :], T["rows"][0, 0:D].partition_broadcast(128)).then_inc(w_loaded, 16)

                def load(it):
                    for s in range(TILES):
                        sp.wait_ge(taken[s], it)
                        sp.dma_start(xt[:, s, :, :], T["xcol"][bass.ts(it * TILES + s, KP), :]
                                     ).then_inc(x_loaded[s], 16)

                def store(it):
                    for t, name, done, stored in ((h, "H", h_done, h_stored), (y, "Y", y_done, y_stored)):
                        sp.wait_ge(done, it + 1)
                        sp.dma_start(T[name].rearrange("(b n) d -> b n d", b=B)[:, bass.ds(it * (TILES * IPT), TILES * IPT), :]
                                     .rearrange("b (i s) d -> b i (s d)", i=IPT),
                                     t[:, :, :].rearrange("p s d -> p (s d)")).then_inc(stored, 16)

                load(0)
                with sp.Fori(0, STEPS - 1) as it:
                    load(it + 1)
                    store(it)
                store(STEPS - 1)
                sp.wait_ge(h_stored, 16 * STEPS)
                sp.wait_ge(y_stored, 16 * STEPS)

            @block.gpsimd
            def _(pool):
                pool.memset(ones[:, :], 1.0).then_inc(ones_set, 1)
                with pool.Fori(0, STEPS) as it:
                    pool.wait_ge(var_done, it + 1)
                    pool.tensor_tensor(rstd[:, :], var[:, :], C["nhalf"][:, 0:TILES], ALU.pow).then_inc(rstd_done, 1)
                    pool.wait_ge(hvar_done, it + 1)
                    pool.tensor_tensor(hrstd[:, :], hvar[:, :], C["nhalf"][:, 0:TILES], ALU.pow).then_inc(hrstd_done, 1)

            @block.scalar
            def _(act):
                act.preload_act_table(ACT.Square)
                act.wait_ge(w_loaded, 96)
                r5, r4, r1 = (float(np.sqrt(k / FEAT)) for k in (5.0, 4.0, 1.0))
                with act.Fori(0, STEPS) as it:

                    def take(s):
                        act.wait_ge(projected, it * TILES + (s + 1))
                        if s == 0:
                            act.wait_ge(u_used, it)
                        act.activation(u[:, s, :], psx[s][:, 0:D + 2], ACT.Copy).then_inc(taken[s], 1)

                    for s in range(TILES):
                        act.wait_ge(x_loaded[s], it * 16 + 16)
                        if s == 0:
                            act.wait_ge(sq_summed, it * TILES)
                        act.activation(sq[:, s, 0:4, :], xt[:, s, 0:4, :], ACT.Square, scale=r5)
                        act.activation(sq[:, s, 4, :], xt[:, s, 4, :], ACT.Square, scale=rootw[:, 4:5])
                        act.activation(sq[:, s, 5, :], xt[:, s, 5, :], ACT.Square, scale=r4)
                        act.activation(sq[:, s, 6, :], xt[:, s, 6, :], ACT.Square, scale=rootw[:, 6:7])
                        act.activation(sq[:, s, 7, :], xt[:, s, 7, :], ACT.Square, scale=r1).then_inc(squared, 1)
                        if s >= LAG:
                            take(s - LAG)
                    for s in range(TILES - LAG, TILES):
                        take(s)

            @block.tensor
            def _(pe):
                pe.wait_ge(ones_set, 1)
                pe.wait_ge(w_loaded, 96)
                for k in range(KT):
                    for s in range(5):
                        pe.matmul(psb[:, 1, 0:D], bsh[:, k, s:s + 1].to_broadcast([KP, 128]), wsh[:, k, s, :],
                                  start=(k == 0 and s == 0), stop=(k == KT - 1 and s == 4), skip_group_check=True)
                for k in range(KT):
                    pe.wait_ge(weff_done, k + 1)
                    last = pe.matmul(psx[0][:, 0:D], ones[:, :], weff[:, k, 0:D], start=(k == 0), stop=(k == KT - 1))
                last.then_inc(rows_done, 1)
                pe.wait_ge(bias_set, 2)
                with pe.Fori(0, STEPS) as it:

                    def mean_square(s):
                        pe.wait_ge(sq_summed, it * TILES + (s + 1))
                        pe.matmul(psx[s][:, D + 1:D + 2], sqs[:, s, :], ones[:, 0:1], start=False, stop=True,
                                  skip_group_check=True).then_inc(projected, 1)

                    for s in range(TILES):
                        pe.wait_ge(x_loaded[s], it * 16 + 16)
                        pe.wait_ge(taken[s], it)
                        for k in range(KT):
                            pe.matmul(psx[s][:, 0:D + 1], xt[:, s, k, :], weff[:, k, :], start=(k == 0), stop=(k == KT - 1))
                        if s >= LAG:
                            mean_square(s - LAG)
                    for s in range(TILES - LAG, TILES):
                        mean_square(s)

            @block.vector
            def _(v):
                chain = Chain(v, vchain)
                v.wait_ge(w_loaded, 96)
                chain(v.tensor_copy(weff[:, :, D:D + 1], cntw[:, :].unsqueeze(2)))
                for k in range(KT):
                    ins = v.tensor_scalar(weff[:, k, 0:D], wsh[:, k, 0, :], gsh[:, k, 0:1], None, ALU.mult)
                    for s in range(1, 5):
                        chain(ins)
                        ins = v.scalar_tensor_tensor(out=weff[:, k, 0:D], in0=wsh[:, k, s, :], scalar=gsh[:, k, s:s + 1],
                                                     in1=weff[:, k, 0:D], op0=ALU.mult, op1=ALU.add)
                    ins.then_inc(weff_done, 1)
                v.wait_ge(rows_done, 1)
                v.tensor_copy(gsum[:, :], psx[0][:, 0:D]).then_inc(bias_set, 1)
                v.tensor_tensor(bias[:, :], psb[:, 1, 0:D], brow[:, :], ALU.add).then_inc(bias_set, 1)
                chain(v.memset(C["ymax_img"][:, :], 0.0))
                v.wait_ge(bias_set, 2)
                with v.Fori(0, STEPS) as it:
                    chain.loop(it, 6)
                    for s in range(TILES):
                        v.wait_ge(squared, it * TILES + (s + 1))
                        v.tensor_reduce(sqs[:, s, :], sq[:, s, :, :].rearrange("p k n -> p n k"), AX.X, ALU.add
                                        ).then_inc(sq_summed, 1)
                    for s in range(TILES):
                        v.wait_ge(taken[s], it + 1)
                    v.tensor_scalar(nmean[:, :], u[:, :, D], -1.0, None, ALU.mult)
                    chain(v.tensor_tensor(mean2[:, :], u[:, :, D], u[:, :, D], ALU.mult))
                    chain(v.tensor_tensor(var[:, :], u[:, :, D + 1], mean2[:, :], ALU.subtract))
                    v.tensor_scalar(var[:, :], var[:, :], 0.0, EPS, ALU.max, ALU.add).then_inc(var_done, 1)
                    for s in range(TILES):
                        ins = v.scalar_tensor_tensor(out=z[:, s, :], in0=gsum[:, :], scalar=nmean[:, s:s + 1],
                                                     in1=u[:, s, 0:D], op0=ALU.mult, op1=ALU.add)
                    ins.then_inc(u_used, 1)
                    v.wait_ge(u_used, it + 1)
                    v.wait_ge(rstd_done, it + 1)
                    v.wait_ge(h_stored, it * 16)
                    for s in range(TILES):
                        ins = v.scalar_tensor_tensor(out=h[:, s, :], in0=z[:, s, :], scalar=rstd[:, s:s + 1],
                                                     in1=bias[:, :], op0=ALU.mult, op1=ALU.add)
                    ins.then_inc(h_done, 1)
                    v.wait_ge(h_done, it + 1)
                    for s in range(TILES):
                        ins = v.bn_stats(bn[:, s, :], h[:, s, :])
                    chain(ins)
                    v.memset(gap[:, :], 0.0)
                    for s in range(TILES):
                        ins = v.bn_aggr(mv[:, s, :], bn[:, s, :])
                    chain(ins)
                    v.tensor_scalar(hvar[:, :], mv[:, :, 1], EPS, None, ALU.add).then_inc(hvar_done, 1)
                    v.wait_ge(hrstd_done, it + 1)
                    v.wait_ge(y_stored, it * 16)
                    for s in range(TILES):
                        ins = v.tensor_scalar(y[:, s, :], h[:, s, :], mv[:, s, 0:1], hrstd[:, s:s + 1],
                                              ALU.subtract, ALU.mult)
                    ins.then_inc(y_done, 1)
                    v.wait_ge(y_done, it + 1)
                    chain(v.tensor_reduce(ymx[:, :], y[:, :, :].rearrange("p s d -> p (s d)"), AX.X, ALU.max, apply_absolute_value=True))
                    chain(v.tensor_tensor(C["ymax_img"][:, :], C["ymax_img"][:, :], ymx[:, :], ALU.max))
                chain.end(STEPS)


def text_phase(nc, T, C):
    W = TG * NTXT
    U = 2 * 3
    SCALE = float(DH) ** -0.5
    with ExitStack() as ctx:
        m = Mem(nc, ctx, "tx")
        wqk = m.sb("wqk", [128, 2, 2, 384])
        bqk = m.sb("bqk", [128, 6])
        wv = m.sb("wv", [128, 2, D])
        wo = m.sb("wo", [128, 2, D])
        w1 = m.sb("w1", [128, 2, F])
        b1 = m.sb("b1", [128, FT])
        w2 = m.sb("w2", [128, FT, D])
        rows = m.sb("rows", [NTXT, 8, D])
        bv, bo, gam1, bet1, b2, gam2, bet2 = (rows[:, i, :] for i in range(1, 8))
        pos = m.sb("pos", [NTXT, D])
        xg = m.sb("xg", [NTXT, TG, D])
        xbo = m.sb("xbo", [NTXT, TG, D])
        xT = m.sb("xT", [128, 2, W])
        qT = m.sb("qT", [128, 6, W])
        v = m.sb("v", [NTXT, TG, D])
        mx = m.sb("mx", [NTXT, 2, 4, U])
        e = m.sb("e", [NTXT, 2, 4, U, NTXT])
        zs = m.sb("zs", [NTXT, 2, 4, U])
        rz = m.sb("rz", [NTXT, 2, 4, U])
        pT = m.sb("pT", [NTXT, 2, 4, U * NTXT])
        attn = m.sb("attn", [NTXT, TG, D])
        aT = m.sb("aT", [128, 2, W])
        r1 = m.sb("r1", [NTXT, TG, D])
        bn = m.sb("bn", [NTXT, TG, 6])
        mv = m.sb("mv", [NTXT, TG, 2])
        std = m.sb("std", [NTXT, TG])
        dn = m.sb("dn", [NTXT, TG])
        rs = m.sb("rs", [NTXT, TG])
        h1n = m.sb("h1n", [NTXT, TG, D])
        h1 = m.sb("h1", [NTXT, TG, D])
        h1T = m.sb("h1T", [128, 2, W])
        fT = m.sb("fT", [128, FT, W])
        ho = m.sb("ho", [NTXT, TG, D])
        yo = m.sb("yo", [NTXT, TG, D])
        ymx = m.sb("ymx", [NTXT, 1])
        gap = m.sb("gap", [1, 1])
        ps = m.ps("ps", [128, 8, 512])

        w_loaded = m.sem("w_loaded")
        x_ready = m.sem("x_ready")
        xbo_ready = m.sem("xbo_ready")
        x_turned = m.sem("x_turned")
        xT_ready = m.sem("xT_ready")
        qk_mm = m.sem("qk_mm")
        qk_ready = m.sem("qk_ready")
        v_mm = m.sem("v_mm")
        v_ready = m.sem("v_ready")
        s_mm = m.sem("s_mm")
        s_less_max = m.sem("s_less_max")
        exp_done = m.sem("exp_done")
        p_turned = m.sem("p_turned")
        pT_ready = m.sem("pT_ready")
        pv_mm = m.sem("pv_mm")
        attn_ready = m.sem("attn_ready")
        a_turned = m.sem("a_turned")
        aT_ready = m.sem("aT_ready")
        wo_mm = m.sem("wo_mm")
        var_ready = m.sem("var_ready")
        std_ready = m.sem("std_ready")
        h1_ready = m.sem("h1_ready")
        h1_turned = m.sem("h1_turned")
        h1T_ready = m.sem("h1T_ready")
        f1_mm = m.sem("f1_mm")
        fT_ready = m.sem("fT_ready")
        f2_mm = m.sem("f2_mm")
        f2_used = m.sem("f2_used")
        h_ready = m.sem("h_ready")
        y_ready = m.sem("y_ready")
        h_stored = m.sem("h_stored")
        y_stored = m.sem("y_stored")
        vchain = m.sem("vchain")
        NLOAD = 9

        with nc.Block() as block:

            @block.sync
            def _(sp):
                for t, name in ((wqk, "wqk"), (wv, "wv"), (wo, "wo"), (w1, "w1")):
                    sp.dma_start(t[:, :, :, :] if len(t.shape) == 4 else t[:, :, :], T[name]).then_inc(w_loaded, 16)
                sp.dma_start(bqk[:, :], T["bqk"]).then_inc(w_loaded, 16)
                sp.dma_start(b1[:, :], T["b1"]).then_inc(w_loaded, 16)
                sp.dma_start(w2[:, :, :], T["w2"].rearrange("(k p) d -> p k d", p=128)).then_inc(w_loaded, 16)
                sp.dma_start(rows[:, :, :].rearrange("p r d -> p (r d)"),
                             T["rows"][0, 0:8 * D].partition_broadcast(NTXT)).then_inc(w_loaded, 16)
                sp.dma_start(pos[:, :], T["pos"]).then_inc(w_loaded, 16)
                with sp.Fori(0, TGROUPS) as it:
                    for b in range(TG):
                        h_out = T["H"].rearrange("(b n) d -> b n d", b=B)[bass.ds(it * TG + b, 1), NIMG:N, :]
                        if b == 0:
                            sp.wait_ge(h_ready, it + 1)
                        sp.dma_start(h_out.rearrange("o n d -> (o n) d"), ho[:, b, :]).then_inc(h_stored, 16)
                    for b in range(TG):
                        y_out = T["Y"].rearrange("(b n) d -> b n d", b=B)[bass.ds(it * TG + b, 1), NIMG:N, :]
                        if b == 0:
                            sp.wait_ge(y_ready, it + 1)
                        sp.dma_start(y_out.rearrange("o n d -> (o n) d"), yo[:, b, :]).then_inc(y_stored, 16)
                sp.wait_ge(h_stored, 16 * B)
                sp.wait_ge(y_stored, 16 * B)

            @block.gpsimd
            def _(pool):
                pool.wait_ge(w_loaded, 16 * NLOAD)
                with pool.Fori(0, TGROUPS) as it:
                    pool.wait_ge(x_ready, it + 1)
                    pool.tensor_tensor(xbo[:, :, :], xg[:, :, :], bo.unsqueeze(1).to_broadcast([NTXT, TG, D]), ALU.add
                                       ).then_inc(xbo_ready, 1)
                    pool.wait_ge(var_ready, it * 3 + 1)
                    pool.tensor_tensor(std[:, :], mv[:, :, 1], C["half"][0:NTXT, 0:TG], ALU.pow).then_inc(std_ready, 1)
                    pool.wait_ge(var_ready, it * 3 + 2)
                    pool.tensor_tensor(std[:, :], mv[:, :, 1], C["half"][0:NTXT, 0:TG], ALU.pow).then_inc(std_ready, 1)
                    pool.wait_ge(var_ready, it * 3 + 3)
                    pool.tensor_tensor(rs[:, :], dn[:, :], C["nhalf"][0:NTXT, 0:TG], ALU.pow).then_inc(std_ready, 1)

            @block.scalar
            def _(act):
                act.preload_act_table(ACT.Exp)
                act.wait_ge(w_loaded, 16 * NLOAD)
                with act.Fori(0, TGROUPS) as it:
                    act.wait_ge(x_turned, it + 1)
                    act.activation(xT[:, 0, :], ps[:, 2, 0:W], ACT.Copy)
                    act.activation(xT[0:D2, 1, :], ps[0:D2, 3, 0:W], ACT.Copy).then_inc(xT_ready, 1)
                    for k in range(6):
                        act.wait_ge(qk_mm, it * 6 + (k + 1))
                        act.activation(qT[:, k, :], ps[:, (4 + k) % 8, 0:W], ACT.Identity, bias=bqk[:, k:k + 1]
                                       ).then_inc(qk_ready, 1)
                    for un in range(2):
                        act.wait_ge(s_less_max, it * 2 + (un + 1))
                        act.activation(e[:, un, :, :, :], e[:, un, :, :, :], ACT.Exp, scale=SCALE).then_inc(exp_done, 1)
                    for un in range(2):
                        act.wait_ge(p_turned, it * 2 + (un + 1))
                        act.activation(pT[:, un, :, :], ps[0:NTXT, 4 * un:4 * un + 4, 0:U * NTXT], ACT.Copy
                                       ).then_inc(pT_ready, 1)
                    act.wait_ge(a_turned, it + 1)
                    act.activation(aT[:, 0, :], ps[:, 2, 0:W], ACT.Copy)
                    act.activation(aT[0:D2, 1, :], ps[0:D2, 3, 0:W], ACT.Copy).then_inc(aT_ready, 1)
                    act.wait_ge(h1_turned, it + 1)
                    act.activation(h1T[:, 0, :], ps[:, 0, 0:W], ACT.Copy)
                    act.activation(h1T[0:D2, 1, :], ps[0:D2, 1, 0:W], ACT.Copy).then_inc(h1T_ready, 1)
                    for k in range(FT):
                        act.wait_ge(f1_mm, it * FT + (k + 1))
                        act.activation(fT[:, k, :], ps[:, 2 + k, 0:W], ACT.Relu, bias=b1[:, k:k + 1]).then_inc(fT_ready, 1)

            @block.tensor
            def _(pe):
                ident = C["ident"]
                pe.wait_ge(w_loaded, 16 * NLOAD)

                def turn(src, lo, hi, done):
                    for b in range(TG):
                        pe.transpose(ps[:, lo, b * NTXT:(b + 1) * NTXT], src[:, b, 0:128], ident[0:NTXT, 0:NTXT])
                    for b in range(TG):
                        last = pe.transpose(ps[0:D2, hi, b * NTXT:(b + 1) * NTXT], src[:, b, 128:D], ident[0:NTXT, 0:NTXT])
                    last.then_inc(done, 1)

                def project(srcT, w, bank, b):
                    for k in range(2):
                        K = (128, D2)[k]
                        ins = pe.matmul(ps[0:NTXT, bank, (b % 2) * D:(b % 2) * D + D], srcT[0:K, k, b * NTXT:(b + 1) * NTXT],
                                        w[0:K, k, :], start=(k == 0), stop=(k == 1), skip_group_check=True)
                    return ins

                with pe.Fori(0, TGROUPS) as it:
                    pe.wait_ge(x_ready, it + 1)
                    pe.wait_ge(fT_ready, it * FT)
                    turn(xg, 2, 3, x_turned)
                    pe.wait_ge(xT_ready, it + 1)
                    pe.wait_ge(f2_used, it)
                    for n in range(6):
                        for k in range(2):
                            K = (128, D2)[k]
                            last = pe.matmul(ps[:, (4 + n) % 8, 0:W], wqk[0:K, k, n // 3, (n % 3) * 128:(n % 3) * 128 + 128],
                                             xT[0:K, k, :], start=(k == 0), stop=(k == 1))
                        last.then_inc(qk_mm, 1)
                    for b in range(TG):
                        last = project(xT, wv, 2 + b // 2, b)
                    last.then_inc(v_mm, 1)
                    pe.wait_ge(qk_ready, it * 6 + 6)
                    pe.wait_ge(v_ready, it + 1)
                    for un in range(2):
                        for j in range(4):
                            for b in range(2):
                                at = (2 * un + b) * NTXT
                                for g in range(3):
                                    c = (b * 3 + g) * NTXT
                                    last = pe.matmul(ps[0:NTXT, 4 * un + j, c:c + NTXT],
                                                     qT[32 * j:32 * j + 32, g, at:at + NTXT],
                                                     qT[32 * j:32 * j + 32, 3 + g, at:at + NTXT],
                                                     start=True, stop=True, skip_group_check=True)
                        last.then_inc(s_mm, 1)
                    for un in range(2):
                        pe.wait_ge(exp_done, it * 2 + (un + 1))
                        for j in range(4):
                            for c in range(U):
                                last = pe.transpose(ps[0:NTXT, 4 * un + j, c * NTXT:(c + 1) * NTXT], e[:, un, j, c, :],
                                                    ident[0:NTXT, 0:NTXT])
                        last.then_inc(p_turned, 1)
                    for un in range(2):
                        pe.wait_ge(pT_ready, it * 2 + (un + 1))
                        for b in range(2):
                            for h in range(HEADS):
                                c = (b * 3 + h // 4) * NTXT
                                last = pe.matmul(ps[0:NTXT, 4 * un, b * D + h * DH:b * D + (h + 1) * DH],
                                                 pT[:, un, h % 4, c:c + NTXT], v[:, 2 * un + b, h * DH:(h + 1) * DH],
                                                 start=True, stop=True, skip_group_check=True)
                        last.then_inc(pv_mm, 1)
                    pe.wait_ge(attn_ready, it * 2 + 2)
                    turn(attn, 2, 3, a_turned)
                    pe.wait_ge(aT_ready, it + 1)
                    for b in range(TG):
                        last = project(aT, wo, 5 + b // 2, b)
                    last.then_inc(wo_mm, 1)
                    pe.wait_ge(h1_ready, it + 1)
                    turn(h1, 0, 1, h1_turned)
                    pe.wait_ge(h1T_ready, it + 1)
                    for n in range(FT):
                        for k in range(2):
                            K = (128, D2)[k]
                            last = pe.matmul(ps[:, 2 + n, 0:W], w1[0:K, k, n * 128:(n + 1) * 128], h1T[0:K, k, :],
                                             start=(k == 0), stop=(k == 1))
                        last.then_inc(f1_mm, 1)
                    pe.wait_ge(fT_ready, it * FT + FT)
                    for b in range(TG):
                        for k in range(FT):
                            last = pe.matmul(ps[0:NTXT, b // 2, (b % 2) * D:(b % 2) * D + D],
                                             fT[:, k, b * NTXT:(b + 1) * NTXT], w2[:, k, :],
                                             start=(k == 0), stop=(k == FT - 1), skip_group_check=True)
                    last.then_inc(f2_mm, 1)

            @block.vector
            def _(ve):
                chain = Chain(ve, vchain)
                two = lambda bank: ps[0:NTXT, bank:bank + 2, 0:2 * D].rearrange("p k (b d) -> p k b d", b=2)
                by2 = lambda t: t[:, :, :].rearrange("p (k b) d -> p k b d", b=2)
                wide = lambda r: r.unsqueeze(1).to_broadcast([NTXT, TG, D])
                chain(ve.memset(C["ymax_txt"][:, :], 0.0))
                ve.wait_ge(w_loaded, 16 * NLOAD)

                with ve.Fori(0, TGROUPS) as it:
                    chain.loop(it, 22)

                    def layer_norm(src, nth, gam, bet, norm, out):
                        for b in range(TG):
                            ins = ve.bn_stats(bn[:, b, :], src[:, b, :])
                        chain(ins)
                        ve.memset(gap[:, :], 0.0)
                        for b in range(TG):
                            ins = ve.bn_aggr(mv[:, b, :], bn[:, b, :])
                        ins.then_inc(var_ready, 1)
                        ve.wait_ge(std_ready, it * 3 + nth)
                        chain(ve.tensor_scalar(dn[:, :], std[:, :], EPS, None, ALU.add))
                        chain(ve.reciprocal(rs[:, :], dn[:, :]))
                        for b in range(TG):
                            ins = ve.tensor_scalar(norm[:, b, :], src[:, b, :], mv[:, b, 0:1], rs[:, b:b + 1],
                                                   ALU.subtract, ALU.mult)
                        chain(ins)
                        chain(ve.tensor_tensor(norm[:, :, :], norm[:, :, :], wide(gam), ALU.mult))
                        return ve.tensor_tensor(out[:, :, :], norm[:, :, :], wide(bet), ALU.add)

                    ve.tensor_tensor(xg[:, :, :], C["emb"][:, bass.ds(it * TG, TG), :], wide(pos[:, :]), ALU.add
                                     ).then_inc(x_ready, 1)
                    ve.wait_ge(v_mm, it + 1)
                    for k in range(2):
                        ins = ve.tensor_tensor(v[:, 2 * k:2 * k + 2, :],
                                               ps[0:NTXT, 2 + k, 0:2 * D].rearrange("p (b d) -> p b d", b=2),
                                               bv.unsqueeze(1).to_broadcast([NTXT, 2, D]), ALU.add)
                    ins.then_inc(v_ready, 1)
                    for un in range(2):
                        s = ps[0:NTXT, 4 * un:4 * un + 4, 0:U * NTXT].rearrange("p j (c k) -> p j c k", c=U)
                        ve.wait_ge(s_mm, it * 2 + (un + 1))
                        chain(ve.tensor_reduce(mx[:, un, :, :], s, AX.X, ALU.max))
                        for j in range(4):
                            ins = ve.tensor_tensor(e[:, un, j, :, :], s[:, j, :, :],
                                                   mx[:, un, j, :].unsqueeze(2).to_broadcast([NTXT, U, NTXT]), ALU.subtract)
                        ins.then_inc(s_less_max, 1)
                    for un in range(2):
                        ve.wait_ge(exp_done, it * 2 + (un + 1))
                        chain(ve.tensor_reduce(zs[:, un, :, :], e[:, un, :, :, :], AX.X, ALU.add))
                        chain(ve.reciprocal(rz[:, un, :, :], zs[:, un, :, :]))
                    for un in range(2):
                        ve.wait_ge(pv_mm, it * 2 + (un + 1))
                        for b in range(2):
                            r = rz[:, un, :, 3 * b:3 * b + 3].rearrange("p j g -> p g j").unsqueeze(3)
                            ins = ve.tensor_tensor(attn[:, 2 * un + b, :].rearrange("p (g j d) -> p g j d", g=3, j=4),
                                                   ps[0:NTXT, 4 * un, b * D:(b + 1) * D].rearrange("p (g j d) -> p g j d", g=3, j=4),
                                                   r.to_broadcast([NTXT, 3, 4, DH]), ALU.mult)
                        ins.then_inc(attn_ready, 1)
                    ve.wait_ge(wo_mm, it + 1)
                    ve.wait_ge(xbo_ready, it + 1)
                    for k in range(2):
                        ins = ve.tensor_tensor(r1[:, 2 * k:2 * k + 2, :],
                                               ps[0:NTXT, 5 + k, 0:2 * D].rearrange("p (b d) -> p b d", b=2),
                                               xbo[:, 2 * k:2 * k + 2, :], ALU.add)
                    chain(ins)
                    layer_norm(r1, 1, gam1, bet1, h1n, h1).then_inc(h1_ready, 1)
                    ve.wait_ge(f2_mm, it + 1)
                    for k in range(2):
                        ins = ve.tensor_tensor(r1[:, 2 * k:2 * k + 2, :],
                                               ps[0:NTXT, k, 0:2 * D].rearrange("p (b d) -> p b d", b=2),
                                               b2.unsqueeze(1).to_broadcast([NTXT, 2, D]), ALU.add)
                    ins.then_inc(f2_used, 1)
                    ve.wait_ge(f2_used, it + 1)
                    chain(ve.tensor_tensor(r1[:, :, :], r1[:, :, :], h1[:, :, :], ALU.add))
                    ve.wait_ge(h_stored, it * (16 * TG))
                    layer_norm(r1, 2, gam2, bet2, h1n, ho).then_inc(h_ready, 1)
                    ve.wait_ge(h_ready, it + 1)
                    for b in range(TG):
                        ins = ve.bn_stats(bn[:, b, :], ho[:, b, :])
                    chain(ins)
                    ve.memset(gap[:, :], 0.0)
                    for b in range(TG):
                        ins = ve.bn_aggr(mv[:, b, :], bn[:, b, :])
                    chain(ins)
                    ve.tensor_scalar(dn[:, :], mv[:, :, 1], EPS, None, ALU.add).then_inc(var_ready, 1)
                    ve.wait_ge(std_ready, it * 3 + 3)
                    ve.wait_ge(y_stored, it * (16 * TG))
                    for b in range(TG):
                        ins = ve.tensor_scalar(yo[:, b, :], ho[:, b, :], mv[:, b, 0:1], rs[:, b:b + 1],
                                               ALU.subtract, ALU.mult)
                    ins.then_inc(y_ready, 1)
                    ve.wait_ge(y_ready, it + 1)
                    chain(ve.tensor_reduce(ymx[:, :], yo[:, :, :], AX.XY, ALU.max, apply_absolute_value=True))
                    chain(ve.tensor_tensor(C["ymax_txt"][0:NTXT, :], C["ymax_txt"][0:NTXT, :], ymx[:, :], ALU.max))
                chain.end(TGROUPS)


def scales(nc, T, C):
    sc, wint, wqk, wpi = C["sc"], C["wint"], C["wqkp"], C["wpint"]
    with ExitStack() as ctx:
        m = Mem(nc, ctx, "qs")
        wf = m.sb("wf", [128, 2, 3 * D])
        wpf = m.sb("wpf", [128, 2, D])
        big = m.sb("big", [128, 2, 3 * D])
        bigp = m.sb("bigp", [128, 2, D])
        brow = m.sb("brow", [1, 3 * D])
        rest = m.sb("rest", [1, 2, 3 * D])
        parts = m.sb("parts", [1, 3, 3 * D], BF16)
        mx = m.sb("mx", [128, 3])
        gx = m.sb("gx", [128, 3])
        loaded = m.sem("loaded")
        mx_ready = m.sem("mx_ready")
        gx_ready = m.sem("gx_ready")
        parts_ready = m.sem("parts_ready")
        parts_placed = m.sem("parts_placed")
        zeroed = m.sem("zeroed")
        vchain = m.sem("vchain")
        with nc.Block() as block:

            @block.sync
            def _(sp):
                sp.dma_start(wf[:, :, :], T["wqkv"]).then_inc(loaded, 16)
                sp.dma_start(wpf[:, :, :], T["wproj"]).then_inc(loaded, 16)
                sp.dma_start(brow[:, :], T["bqkv"]).then_inc(loaded, 16)
                sp.wait_ge(parts_ready, 1)
                sp.dma_start(wint[D2:D2 + 3, 1, :], parts[:, :, :].rearrange("o r n -> o (r n)")).then_inc(parts_placed, 16)
                sp.wait_ge(parts_placed, 16)

            @block.gpsimd
            def _(pool):
                pool.memset(wqk[:, :, :, :], 0.0).then_inc(zeroed, 1)
                pool.wait_ge(mx_ready, 1)
                pool.partition_all_reduce(gx[:, :], mx[:, :], 128, RMAX).then_inc(gx_ready, 1)

            @block.vector
            def _(v):
                chain = Chain(v, vchain)
                v.wait_ge(loaded, 48)
                v.tensor_tensor(mx[:, 0:1], C["ymax_img"][:, :], C["ymax_txt"][:, :], ALU.max)
                v.tensor_reduce(mx[:, 1:2], wf[:, :, :], AX.XY, ALU.max, apply_absolute_value=True)
                v.tensor_reduce(mx[:, 2:3], wpf[:, :, :], AX.XY, ALU.max, apply_absolute_value=True).then_inc(mx_ready, 1)
                v.wait_ge(gx_ready, 1)
                chain(v.tensor_scalar(sc[:, SX:SX + 3], gx[:, :], 1.0 / QMAX, SCALE_FLOOR, ALU.mult, ALU.max))
                chain(v.reciprocal(sc[:, ISX:ISX + 3], sc[:, SX:SX + 3]))
                v.tensor_tensor(sc[:, SXW:SXW + 1], sc[:, SX:SX + 1], sc[:, SX + 1:SX + 2], ALU.mult)
                v.tensor_scalar(big[:, :, :], wf[:, :, :], sc[:, ISX + 1:ISX + 2], ROUND, ALU.mult, ALU.add)
                v.tensor_scalar(bigp[:, :, :], wpf[:, :, :], sc[:, ISX + 2:ISX + 3], ROUND, ALU.mult, ALU.add)
                chain(v.tensor_tensor(sc[:, ISXW:ISXW + 1], sc[:, ISX:ISX + 1], sc[:, ISX + 1:ISX + 2], ALU.mult))
                v.tensor_scalar(wint[:, :, :], big[:, :, :], ROUND, None, ALU.subtract)
                v.tensor_scalar(wpi[:, :, :], bigp[:, :, :], ROUND, None, ALU.subtract)
                chain(v.tensor_scalar(rest[:, 0, :], brow[:, :], sc[0:1, ISXW:ISXW + 1], None, ALU.mult))
                chain(v.tensor_copy(parts[:, 0, :], rest[:, 0, :]))
                chain(v.tensor_tensor(rest[:, 1, :], rest[:, 0, :], parts[:, 0, :], ALU.subtract))
                chain(v.tensor_copy(parts[:, 1, :], rest[:, 1, :]))
                v.tensor_tensor(parts[:, 2, :], rest[:, 1, :], parts[:, 1, :], ALU.subtract).then_inc(parts_ready, 1)
                v.wait_ge(parts_placed, 16)
                v.wait_ge(zeroed, 1)
                chain(v.tensor_copy(wqk[:, :, :, 0:DH], wint[:, :, 0:2 * D].rearrange("p k (h d) -> p k h d", d=DH)))


def quantize_phase(nc, T, C):
    NT = N // 3
    PAD = NT + 1
    sc, wint = C["sc"], C["wint"]
    with ExitStack() as ctx:
        m = Mem(nc, ctx, "qz")
        yt = m.sb("yt", [NT, 2, 3, D])
        big = m.sb("big", [NT, 2, 3, D])
        yq = m.sb("yq", [NT, 2, 3, D], BF16)
        yT = m.sb("yT", [128, 2, 2, NE], BF16)
        tile_max = m.sb("tile_max", [NT, 6, 3])
        run_max = m.sb("run_max", [NT, 6, 3])
        pt = [m.ps(f"pt{s}", [128, 2, 3, PAD], BF16) for s in range(2)]
        pj = m.ps("pj", [128, 6, 512])
        y_loaded = [m.sem(f"y_loaded{s}") for s in range(2)]
        yq_ready = [m.sem(f"yq_ready{s}") for s in range(2)]
        turned = [m.sem(f"turned{s}") for s in range(2)]
        yT_ready = [m.sem(f"yT_ready{s}") for s in range(2)]
        rounded = [m.sem(f"rounded{s}") for s in range(2)]
        stored = [m.sem(f"stored{s}") for s in range(2)]
        product = m.sem("product")
        reduced = m.sem("reduced")
        ones_set = m.sem("ones_set")
        vchain = m.sem("vchain")
        with nc.Block() as block:

            @block.sync
            def _(sp):

                def load(it, s):
                    sp.wait_ge(yq_ready[s], it)
                    sp.dma_start(yt[:, s, :, :].rearrange("p i d -> p (i d)"),
                                 T["Y"].rearrange("(r i) d -> r (i d)", i=3)[bass.ts(it * 2 + s, NT), :]
                                 ).then_inc(y_loaded[s], 16)

                def store(it, s):
                    sp.wait_ge(yT_ready[s], it + 1)
                    sp.dma_start(T["YQ"][bass.ds((it * 2 + s) * D, 128), :], yT[:, s, 0, :]).then_inc(stored[s], 16)
                    sp.dma_start(T["YQ"][bass.ds((it * 2 + s) * D + 128, D2), :], yT[0:D2, s, 1, :]).then_inc(stored[s], 16)

                for s in range(2):
                    load(0, s)
                with sp.Fori(0, B // 2 - 1) as it:
                    for s in range(2):
                        load(it + 1, s)
                    for s in range(2):
                        store(it, s)
                for s in range(2):
                    store(B // 2 - 1, s)
                for s in range(2):
                    sp.wait_ge(stored[s], 16 * B)

            @block.vector
            def _(v):
                chain = Chain(v, vchain)
                v.memset(run_max[:, :, :], 0.0)
                v.memset(yT[:, :, :, :], 0.0)
                chain(v.memset(C["qkvmax"][:, :], 0.0))
                v.memset(yT[D2:D2 + 3, :, 1, :], 1.0).then_inc(ones_set, 1)
                with v.Fori(0, B // 2) as it:
                    chain.loop(it, 1)
                    for s in range(2):
                        v.wait_ge(y_loaded[s], it * 16 + 16)
                        v.tensor_scalar(big[:, s, :, :], yt[:, s, :, :], sc[0:NT, ISX:ISX + 1], ROUND, ALU.mult, ALU.add
                                        ).then_inc(rounded[s], 1)
                        v.wait_ge(rounded[s], it + 1)
                        v.wait_ge(turned[s], it)
                        v.tensor_scalar(yq[:, s, :, :], big[:, s, :, :], ROUND, None, ALU.subtract).then_inc(yq_ready[s], 1)
                    for t in range(6):
                        v.wait_ge(product, it * 6 + (t + 1))
                        ins = v.tensor_reduce(tile_max[:, t, :], pj[0:NT, 3 * (t % 2):3 * (t % 2) + 3, 0:D], AX.X, ALU.max,
                                              apply_absolute_value=True)
                        ins.then_inc(reduced, 1)
                    v.wait_ge(reduced, it * 6 + 6)
                    chain(v.tensor_tensor(run_max[:, :, :], run_max[:, :, :], tile_max[:, :, :], ALU.max))
                chain.end(B // 2)
                chain(v.tensor_reduce(C["qkvmax"][0:NT, :], run_max[:, :, :].rearrange("p t c -> p c t"), AX.X, ALU.max))

            @block.scalar
            def _(act):
                act.preload_act_table(ACT.Copy)
                act.wait_ge(ones_set, 1)
                with act.Fori(0, B // 2) as it:
                    for s in range(2):
                        act.wait_ge(turned[s], it + 1)
                        act.wait_ge(product, it * 6)
                        act.wait_ge(stored[s], it * 32)
                        for k in range(2):
                            K = (128, D2)[k]
                            ins = act.activation(yT[0:K, s, k, 0:N].rearrange("c (p i) -> c i p", i=3),
                                                 pt[s][0:K, k, :, 0:NT], ACT.Copy)
                        ins.then_inc(yT_ready[s], 1)

            @block.tensor
            def _(pe):
                with pe.Fori(0, B // 2) as it:
                    for s in range(2):
                        pe.wait_ge(yq_ready[s], it + 1)
                        pe.wait_ge(yT_ready[s], it)
                        for k in range(2):
                            K = (128, D2)[k]
                            for i in range(3):
                                ins = pe.transpose(pt[s][0:K, k, i, 0:NT], yq[:, s, i, 128 * k:128 * k + K],
                                                   C["identb"][0:NT, 0:NT])
                        ins.then_inc(turned[s], 1)
                    for s in range(2):
                        pe.wait_ge(yT_ready[s], it + 1)
                        for i in range(3):
                            t = 3 * s + i
                            if t >= 2:
                                pe.wait_ge(reduced, it * 6 + (t - 1))
                            else:
                                pe.wait_ge(reduced, it * 6)
                            for c in range(3):
                                for k in range(2):
                                    K = (128, D2 + 3)[k]
                                    ins = pe.matmul(pj[0:NT, 3 * (t % 2) + c, 0:D], yT[0:K, s, k, i * NT:(i + 1) * NT],
                                                    wint[0:K, k, c * D:(c + 1) * D], start=(k == 0), stop=(k == 1))
                            ins.then_inc(product, 1)


def head_scales(nc, T, C):
    sc = C["sc"]
    with ExitStack() as ctx:
        m = Mem(nc, ctx, "hs")
        gx = m.sb("gx", [128, 3])
        gx_ready = m.sem("gx_ready")
        vchain = m.sem("vchain")
        with nc.Block() as block:

            @block.gpsimd
            def _(pool):
                pool.partition_all_reduce(gx[:, :], C["qkvmax"][:, :], 128, RMAX).then_inc(gx_ready, 1)

            @block.vector
            def _(v):
                chain = Chain(v, vchain)
                one = lambda i: sc[:, i:i + 1]
                three = lambda i: sc[:, i:i + 3]
                v.wait_ge(gx_ready, 1)
                chain(v.tensor_scalar(three(TMP), gx[:, :], one(SXW), None, ALU.mult))
                chain(v.tensor_scalar(three(SQKV), three(TMP), 1.0 / QMAX, SCALE_FLOOR, ALU.mult, ALU.max))
                chain(v.reciprocal(three(IQKV), three(SQKV)))
                v.tensor_scalar(three(AQKV), three(IQKV), one(SXW), None, ALU.mult)
                chain(v.tensor_scalar(one(ALPHA), one(SQKV), one(SQKV + 1), float(DH) ** -0.5, ALU.mult, ALU.mult))
                v.reciprocal(one(IALPHA), one(ALPHA))


def qkv_phase(nc, T, C):
    L = N - 256
    sc, wint, wqk = C["sc"], C["wint"], C["wqkp"]
    with ExitStack() as ctx:
        m = Mem(nc, ctx, "qk")
        yT = m.sb("yT", [128, 2, 2, NE], BF16)
        yL = m.sb("yL", [128, 2, 2, 4, 32], BF16)
        qkb = m.sb("qkb", [128, 2, 2, 3, N])
        qko = m.sb("qko", [128, 2, 2, 3, NE], BF16)
        vb = m.sb("vb", [128, 2, 3, D])
        vo = m.sb("vo", [128, 2, 3, D], BF16)
        kround = m.sb("kround", [128, 1])
        rounding = m.sb("rounding", [128, 1])
        ps = m.ps("ps", [128, 8, 512])
        loaded = [m.sem(f"loaded{s}") for s in range(2)]
        left_ready = [m.sem(f"left_ready{s}") for s in range(2)]
        q_mm, k_mm = m.sem("q_mm"), m.sem("k_mm")
        v_mm = [m.sem(f"v_mm{s}") for s in range(2)]
        q_out, k_out, v_out = m.sem("q_out"), m.sem("k_out"), m.sem("v_out")
        qk_ready = [m.sem(f"qk_ready{s}") for s in range(2)]
        v_ready = [m.sem(f"v_ready{s}") for s in range(2)]
        qk_stored = [m.sem(f"qk_stored{s}") for s in range(2)]
        v_stored = [m.sem(f"v_stored{s}") for s in range(2)]
        const_set = m.sem("const_set")
        ones_set = m.sem("ones_set")
        k_loaded = m.sem("k_loaded")
        with nc.Block() as block:

            @block.sync
            def _(sp):
                sp.dma_start(kround[:, :], T["kround"]).then_inc(k_loaded, 16)
                sp.wait_ge(ones_set, 1)

                def load(it, s):
                    sp.wait_ge(v_mm[s], it)
                    sp.dma_start(yT[:, s, 0, :], T["YQ"][bass.ds((it * 2 + s) * D, 128), :]).then_inc(loaded[s], 16)
                    sp.dma_start(yT[0:D2, s, 1, :], T["YQ"][bass.ds((it * 2 + s) * D + 128, D2), :]).then_inc(loaded[s], 16)

                def store(it, s):
                    sp.wait_ge(qk_ready[s], it * 2 + 2)
                    sp.dma_start(T["QK"][:, :, bass.ds((it * 2 + s) * (3 * NE), 3 * NE)].rearrange("a p n -> p a n"),
                                 qko[:, s, :, :, :].rearrange("p a g n -> p a (g n)")).then_inc(qk_stored[s], 16)
                    sp.wait_ge(v_ready[s], it + 1)
                    sp.dma_start(T["V"][bass.ts(it * 2 + s, 128), :], vo[:, s, :, :].rearrange("p t d -> p (t d)")
                                 ).then_inc(v_stored[s], 16)

                for s in range(2):
                    load(0, s)
                with sp.Fori(0, B // 2 - 1) as it:
                    for s in range(2):
                        load(it + 1, s)
                        store(it, s)
                for s in range(2):
                    store(B // 2 - 1, s)
                for s in range(2):
                    sp.wait_ge(qk_stored[s], 8 * B)
                    sp.wait_ge(v_stored[s], 8 * B)

            @block.gpsimd
            def _(pool):
                pool.memset(yL[:, :, :, :, :], 0.0).then_inc(const_set, 1)
                pool.wait_ge(const_set, 4)
                with pool.Fori(0, B // 2) as it:
                    for s in range(2):
                        pool.wait_ge(loaded[s], it * 32 + 32)
                        pool.wait_ge(v_mm[s], it)
                        pool_copy(pool, yL[:, s, :, :, 0:L], yT[:, s, :, 256:N].unsqueeze(2).to_broadcast([128, 2, 4, L]), C["one"][:, :]
                                         ).then_inc(left_ready[s], 1)

            @block.scalar
            def _(act):
                aq, ak = act.alloc_register("scale_q"), act.alloc_register("scale_k")
                act.reg_load(aq, sc[0:1, AQKV:AQKV + 1].bitcast(U32))
                act.reg_load(ak, sc[0:1, AQKV + 1:AQKV + 2].bitcast(U32))
                act.preload_act_table(ACT.Identity)
                act.wait_ge(const_set, 4)
                with act.Fori(0, B // 2) as it:
                    for s in range(2):
                        act.wait_ge(qk_ready[s], it * 2)
                        for a, (mm, out, r) in enumerate(((q_mm, q_out, aq), (k_mm, k_out, ak))):
                            act.wait_ge(mm, it * 2 + (s + 1))
                            act.activation(qkb[:, s, a, :, :], ps[:, 3 * a:3 * a + 3, 0:N], ACT.Identity,
                                           scale=r, bias=rounding[:, 0:1]).then_inc(out, 1)

            @block.vector
            def _(v):
                v.memset(rounding[:, :], ROUND).then_inc(const_set, 1)
                v.memset(qko[:, :, :, :, :], 0.0).then_inc(const_set, 1)
                v.memset(yT[:, :, :, :], 0.0).then_inc(const_set, 1)
                v.wait_ge(const_set, 4)
                v.memset(yT[D2:D2 + 3, :, 1, :], 1.0).then_inc(ones_set, 1)
                v.wait_ge(k_loaded, 16)
                with v.Fori(0, B // 2) as it:
                    for s in range(2):
                        v.wait_ge(qk_stored[s], it * 16)
                        v.wait_ge(q_out, it * 2 + (s + 1))
                        v.tensor_scalar(qko[:, s, 0, :, 0:N], qkb[:, s, 0, :, :], ROUND, None, ALU.subtract
                                        ).then_inc(qk_ready[s], 1)
                        v.wait_ge(k_out, it * 2 + (s + 1))
                        v.tensor_scalar(qko[:, s, 1, :, 0:N], qkb[:, s, 1, :, :], kround[:, 0:1], None, ALU.subtract
                                        ).then_inc(qk_ready[s], 1)
                        v.wait_ge(v_mm[s], it + 1)
                        v.tensor_scalar(vb[:, s, 0:2, :], ps[:, 6, 0:2 * D].rearrange("p (t d) -> p t d", t=2),
                                        sc[:, AQKV + 2:AQKV + 3], ROUND, ALU.mult, ALU.add)
                        v.tensor_scalar(vb[:, s, 2, :], ps[:, 7, 0:D], sc[:, AQKV + 2:AQKV + 3], ROUND, ALU.mult, ALU.add
                                        ).then_inc(v_out, 1)
                        v.wait_ge(v_out, it * 2 + (s + 1))
                        v.wait_ge(v_stored[s], it * 16)
                        v.tensor_scalar(vo[:, s, :, :], vb[:, s, :, :], ROUND, None, ALU.subtract).then_inc(v_ready[s], 1)

            @block.tensor
            def _(pe):
                pe.wait_ge(ones_set, 1)
                with pe.Fori(0, B // 2) as it:
                    for s in range(2):
                        pe.wait_ge(loaded[s], it * 32 + 32)
                        for a, (mm, out) in enumerate(((q_mm, q_out), (k_mm, k_out))):
                            pe.wait_ge(out, it * 2 + s)
                            for g in range(3):
                                for k in range(2):
                                    K = (128, D2 + 3)[k]
                                    ins = pe.matmul(ps[:, 3 * a + g, 0:N],
                                                    wqk[0:K, k, 12 * a + 4 * g:12 * a + 4 * g + 4, :].rearrange("c j n -> c (j n)"),
                                                    yT[0:K, s, k, 0:N], start=(k == 0), stop=(k == 1))
                            ins.then_inc(mm, 1)
                        pe.wait_ge(v_out, it * 2 + s)
                        pe.wait_ge(left_ready[s], it + 1)
                        for t in range(3):
                            for k in range(2):
                                K = (128, D2 + 3)[k]
                                lhsT = (yT[0:K, s, k, t * 128:(t + 1) * 128] if t < 2 else
                                        yL[0:K, s, k, :, :].rearrange("c j n -> c (j n)"))
                                ins = pe.matmul(ps[:, 6 + t // 2, (t % 2) * D:(t % 2) * D + D], lhsT,
                                                wint[0:K, k, 2 * D:3 * D], start=(k == 0), stop=(k == 1),
                                                skip_group_check=True)
                        ins.then_inc(v_mm[s], 1)


def tiles_of_sample():
    pairs = [[(g, t, j), (g, t, j + 1)] for g in range(3) for t in range(2) for j in (0, 2)]
    return pairs + [[(0, 2, 0), (1, 2, 0)], [(2, 2, 0)]]


def row_phase(nc, T, C):
    L = N - 256
    sc = C["sc"]
    PAIRS = tiles_of_sample()
    NP = len(PAIRS)
    col = lambda g, t, j: g * 9 + t * 4 + j
    with ExitStack() as ctx:
        m = Mem(nc, ctx, "rw")
        qk = m.sb("qk", [128, 2, 2, 3, NE], BF16)
        qL = m.sb("qL", [128, 2, 3, 4, 32], BF16)
        nm = m.sb("nm", [128, 2, 27])
        nb = m.sb("nb", [128, 2, 27])
        zz = m.sb("zz", [128, 2, 27])
        ps = m.ps("ps", [128, 8, 512])
        loaded = [m.sem(f"loaded{s}") for s in range(2)]
        left_ready = [m.sem(f"left_ready{s}") for s in range(2)]
        scored = [m.sem(f"scored{n}") for n in range(4)]
        maxed = m.sem("maxed")
        biased = m.sem("biased")
        summed = [m.sem(f"summed{n}") for n in range(4)]
        pchain = m.sem("pchain")
        kept = [m.sem(f"kept{s}") for s in range(2)]
        zeroed = m.sem("zeroed")
        with nc.Block() as block:

            @block.sync
            def _(sp):
                with sp.Fori(0, B // 2) as it:
                    for s in range(2):
                        sp.wait_ge(kept[s], it * 2)
                        sp.dma_start(qk[:, s, :, :, :].rearrange("p a g n -> p a (g n)"),
                                     T["QK"][:, :, bass.ds((it * 2 + s) * (3 * NE), 3 * NE)].rearrange("a p n -> p a n")
                                     ).then_inc(loaded[s], 16)

            @block.gpsimd
            def _(pool):
                pool.memset(qL[:, :, :, :, :], 0.0).then_inc(zeroed, 1)
                pool.wait_ge(zeroed, 1)
                chain = Chain(pool, pchain)
                with pool.Fori(0, B // 2) as it:
                    chain.loop(it, 6)
                    for s in range(2):
                        pool.wait_ge(loaded[s], it * 16 + 16)
                        for j in range(4):
                            ins = pool_copy(pool, qL[32 * j:32 * j + 32, s, :, j, 0:L], qk[32 * j:32 * j + 32, s, 0, :, 256:N],
                                            C["one"][32 * j:32 * j + 32, :])
                            if j < 3:
                                chain(ins)
                        ins.then_inc(left_ready[s], 1)
                        pool.wait_ge(left_ready[s], it + 1)
                    for s in range(2):
                        n = 14 * s + 13
                        pool.wait_ge(summed[n % 4], it * 7 + (n // 4 + 1))
                        pool_copy(pool, C["nmax"][:, bass.ds((it * 2 + s) * 27, 27)], nm[:, s, :], C["one"][:, :]).then_inc(kept[s], 1)
                        pool_copy(pool, C["zsum"][:, bass.ds((it * 2 + s) * 27, 27)], zz[:, s, :], C["one"][:, :]).then_inc(kept[s], 1)
                chain.end(B // 2)

            @block.tensor
            def _(pe):
                with pe.Fori(0, B // 2) as it:
                    for s in range(2):
                        for p, pair in enumerate(PAIRS):
                            n = NP * s + p
                            bank = 2 * (n % 4)
                            if p == 0:
                                pe.wait_ge(loaded[s], it * 16 + 16)
                            if p == 12:
                                pe.wait_ge(left_ready[s], it + 1)
                            pe.wait_ge(summed[n % 4], it * 7 + n // 4)
                            for c, (g, t, j) in enumerate(pair):
                                if t < 2:
                                    r = slice(32 * j, 32 * j + 32)
                                    ins = pe.matmul(ps[:, bank + c, 0:N], qk[r, s, 0, g, t * 128:(t + 1) * 128],
                                                    qk[r, s, 1, g, 0:N], start=True, stop=True)
                                else:
                                    ins = pe.matmul(ps[:, bank + c, 0:N], qL[:, s, g, :, :].rearrange("p j n -> p (j n)"),
                                                    qk[:, s, 1, g, 0:N], start=True, stop=True)
                            ins.then_inc(scored[n % 4], 1)

            @block.vector
            def _(v):
                with v.Fori(0, B // 2) as it:
                    for s in range(2):
                        v.wait_ge(kept[s], it * 2)
                        for p, pair in enumerate(PAIRS):
                            n = NP * s + p
                            bank = 2 * (n % 4)
                            c0, w = col(*pair[0]), len(pair)
                            at = slice(c0, c0 + 1) if w == 1 else slice(c0, col(*pair[1]) + 1, col(*pair[1]) - c0)
                            v.wait_ge(scored[n % 4], it * 7 + (n // 4 + 1))
                            v.tensor_reduce(nm[:, s, at], ps[:, bank:bank + w, 0:N], AX.X, ALU.max, negate=True
                                            ).then_inc(maxed, 1)
                            v.wait_ge(maxed, it * 28 + (n + 1))
                            v.tensor_scalar(nb[:, s, at], nm[:, s, at], sc[:, ALPHA:ALPHA + 1], None, ALU.mult
                                            ).then_inc(biased, 1)

            @block.scalar
            def _(act):
                alpha = act.alloc_register("alpha1")
                act.reg_load(alpha, sc[0:1, ALPHA:ALPHA + 1].bitcast(U32))
                act.preload_act_table(ACT.Exp)
                with act.Fori(0, B // 2) as it:
                    for s in range(2):
                        act.wait_ge(kept[s], it * 2)
                        for p, pair in enumerate(PAIRS):
                            n = NP * s + p
                            bank = 2 * (n % 4)
                            act.wait_ge(biased, it * 28 + (n + 1))
                            for c, t in enumerate(pair):
                                i = col(*t)
                                ins = act.activation(ps[:, bank + c, 0:N], ps[:, bank + c, 0:N], ACT.Exp,
                                                     bias=nb[:, s, i:i + 1], scale=alpha, accum_out=zz[:, s, i:i + 1])
                            ins.then_inc(summed[n % 4], 1)


def row_offsets(nc, T, C):
    L = N - 256
    GROUP = 108
    NG = B * 27 // GROUP
    sc = C["sc"]
    one = lambda i: sc[:, i:i + 1]
    with ExitStack() as ctx:
        m = Mem(nc, ctx, "ro")
        zmin = m.sb("zmin", [128, 1])
        gx = m.sb("gx", [128, 1])
        lnz = m.sb("lnz", [128, B * 27])
        off = m.sb("off", [128, B * 27])
        rest = m.sb("rest", [GROUP, 2, NG, 128])
        parts = m.sb("parts", [GROUP, NG, 3, 128], BF16)
        ps = m.ps("ps", [128, 2, 4, 128])
        zmin_ready = m.sem("zmin_ready")
        gx_ready = m.sem("gx_ready")
        scale_ready = m.sem("scale_ready")
        ln_ready = m.sem("ln_ready")
        off_ready = m.sem("off_ready")
        turned = m.sem("turned")
        parts_ready = m.sem("parts_ready")
        staged = m.sem("staged")
        placed = m.sem("placed")
        vchain = m.sem("vchain")
        with nc.Block() as block:

            @block.gpsimd
            def _(pool):
                pool.wait_ge(zmin_ready, 1)
                pool.partition_all_reduce(gx[:, :], zmin[:, :], 128, RMAX).then_inc(gx_ready, 1)

            @block.scalar
            def _(act):
                act.activation(lnz[:, :], C["zsum"][:, :], ACT.Ln).then_inc(ln_ready, 1)
                act.wait_ge(scale_ready, 1)
                act.activation(one(LNSP), one(SP_), ACT.Ln).then_inc(ln_ready, 1)

            @block.vector
            def _(v):
                chain = Chain(v, vchain)
                chain(v.tensor_reduce(gx[:, :], C["zsum"][:, :], AX.X, ALU.min))
                v.tensor_scalar(zmin[:, :], gx[:, :], -1.0, None, ALU.mult).then_inc(zmin_ready, 1)
                v.wait_ge(gx_ready, 1)
                chain(v.tensor_scalar(one(TMP), gx[:, :], -1.0, None, ALU.mult))
                chain(v.reciprocal(one(TMP + 1), one(TMP)))
                chain(v.tensor_scalar(one(SP_), one(TMP + 1), 1.0 / QMAX, SCALE_FLOOR, ALU.mult, ALU.max))
                v.tensor_scalar(one(TMP + 2), one(IALPHA), -1.0, None, ALU.mult)
                v.tensor_tensor(one(SO_IN), one(SP_), one(SQKV + 2), ALU.mult).then_inc(scale_ready, 1)
                v.wait_ge(ln_ready, 2)
                v.wait_ge(scale_ready, 1)
                chain(v.tensor_scalar(lnz[:, :], lnz[:, :], one(LNSP), one(TMP + 2), ALU.add, ALU.mult))
                v.tensor_tensor(off[:, :], lnz[:, :], C["nmax"][:, :], ALU.add).then_inc(off_ready, 1)
                v.wait_ge(turned, 1)
                t = ps[0:GROUP, :, :, :].rearrange("p a b n -> p (a b) n")
                chain(v.tensor_copy(parts[:, :, 0, :], t))
                chain(v.tensor_tensor(rest[:, 0, :, :], t, parts[:, :, 0, :], ALU.subtract))
                chain(v.tensor_copy(parts[:, :, 1, :], rest[:, 0, :, :]))
                v.tensor_tensor(parts[:, :, 2, :], rest[:, 0, :, :], parts[:, :, 1, :], ALU.subtract
                                ).then_inc(parts_ready, 1)

            @block.tensor
            def _(pe):
                pe.wait_ge(off_ready, 1)
                for g in range(NG):
                    ins = pe.transpose(ps[0:GROUP, g // 4, g % 4, :], off[:, g * GROUP:(g + 1) * GROUP], C["ident"][:, :])
                ins.then_inc(turned, 1)

            @block.sync
            def _(sp):
                sp.wait_ge(parts_ready, 1)
                sp.dma_start(T["OFF"].rearrange("(g p) r n -> p g (r n)", p=GROUP),
                             parts[:, :, :, :].rearrange("p g r n -> p g (r n)")).then_inc(staged, 16)
                sp.wait_ge(staged, 16)
                src = T["OFF"].rearrange("(m c) r n -> c r m n", c=9)
                for j in range(4):
                    rows = T["QK"][0, 32 * j + DH:32 * j + DH + 3, :].rearrange("r (m n) -> r m n", n=NE)
                    for t in range(2):
                        sp.dma_start(rows[:, :, t * 128:(t + 1) * 128], src[t * 4 + j]).then_inc(placed, 16)
                    sp.dma_start(rows[:, :, 256:N], src[8, :, :, 32 * j:32 * j + L]).then_inc(placed, 16)
                sp.wait_ge(placed, 16 * 12)


def product_phase(nc, T, C):
    L = N - 256
    sc = C["sc"]
    tiles = [(g, t, j) for g in range(3) for t in (0, 1, 2) for j in (range(4) if t < 2 else [0])]
    UNITS = len(tiles) // 3
    A_LAST = UNITS * 2 // 3 - 1
    LAST = B // 2 - 1
    with ExitStack() as ctx:
        m = Mem(nc, ctx, "pr")
        qk = m.sb("qk", [128, 2, 2, 3, NE], BF16)
        kL = m.sb("kL", [128, 2, 3, 4, 32], BF16)
        vt = m.sb("vt", [128, 2, 3, D], BF16)
        va = m.sb("va", [128, 2, 2, 8 * (128 + DH)], BF16)
        vb = m.sb("vb", [128, 2, 2, 4 * (64 + DH)], BF16)
        vL = m.sb("vL", [128, 2, 3 * 192], BF16)
        e = m.sb("e", [128, 2, 3, N])
        p = m.sb("p", [128, 2, 3, NE], BF16)
        o = m.sb("o", [128, 2, 2, N])
        mx = m.sb("mx", [128, 2, 2])
        ps = m.ps("ps", [128, 8, 512])
        qk_loaded = [m.sem(f"qk_loaded{s}") for s in range(2)]
        v_loaded = [m.sem(f"v_loaded{s}") for s in range(2)]
        kL_ready = [m.sem(f"kL_ready{s}") for s in range(2)]
        v_ready = [m.sem(f"v_ready{s}") for s in range(2)]
        scored = [m.sem(f"scored{n}") for n in range(2)]
        exp_done = [m.sem(f"exp_done{n}") for n in range(2)]
        rounded = [m.sem(f"rounded{n}") for n in range(2)]
        used = [m.sem(f"used{n}") for n in range(2)]
        a_taken = m.sem("a_taken")
        b_taken = [m.sem(f"b_taken{s}") for s in range(2)]
        cls_kept = [m.sem(f"cls_kept{s}") for s in range(2)]
        o_stored = [m.sem(f"o_stored{s}") for s in range(2)]
        zeroed = m.sem("zeroed")
        pchain, vchain = m.sem("pchain"), m.sem("vchain")
        before = lambda it, w: it * UNITS + w // 2
        with nc.Block() as block:

            @block.sync
            def _(sp):

                def load(it, s):
                    sp.dma_start(qk[:, s, :, :, :].rearrange("p a g n -> p a (g n)"),
                                 T["QK"][:, :, bass.ds((it * 2 + s) * (3 * NE), 3 * NE)].rearrange("a p n -> p a n")
                                 ).then_inc(qk_loaded[s], 16)
                    sp.dma_start(vt[:, s, :, :].rearrange("p t d -> p (t d)"), T["V"][bass.ts(it * 2 + s, 128), :]
                                 ).then_inc(v_loaded[s], 16)

                def store(it, s):
                    sp.wait_ge(b_taken[s], it + 1)
                    sp.dma_start(T["OT"][0:128, bass.ts(it * 2 + s, N)], o[:, s, 0, :]).then_inc(o_stored[s], 16)
                    sp.dma_start(T["OT"][128:D, bass.ts(it * 2 + s, N)], o[0:D2, s, 1, :]).then_inc(o_stored[s], 16)

                for s in range(2):
                    load(0, s)
                with sp.Fori(0, LAST) as it:
                    for s in range(2):
                        store(it, s)
                        load(it + 1, s)
                for s in range(2):
                    store(LAST, s)
                for s in range(2):
                    sp.wait_ge(o_stored[s], 16 * B)

            @block.gpsimd
            def _(pool):
                chain = Chain(pool, pchain)
                chain(pool.memset(kL[:, :, :, :, :], 0.0))
                chain(pool.memset(va[:, :, :, :], 0.0))
                chain(pool.memset(vb[:, :, :, :], 0.0))
                pool.memset(vL[:, :, :], 0.0).then_inc(zeroed, 1)
                pool.wait_ge(zeroed, 1)

                def build(it, s):
                    pool.wait_ge(qk_loaded[s], it * 16 + 16)
                    for j in range(4):
                        r = slice(32 * j, 32 * j + 32)
                        ins = pool_copy(pool, kL[r, s, :, j, 0:L], qk[r, s, 1, :, 256:N], C["one"][r, :])
                        if j < 3:
                            chain(ins)
                    ins.then_inc(kL_ready[s], 1)
                    pool.wait_ge(kL_ready[s], it + 1)
                    pool.wait_ge(v_loaded[s], it * 16 + 16)
                    chain(pool_copy(pool, va[:, s, :, :].rearrange("p t (h c) -> p t h c", h=8)[:, :, :, 0:DH],
                                           vt[:, s, 0:2, 0:128].rearrange("p t (h d) -> p t h d", d=DH), C["one"][:, :]))
                    chain(pool_copy(pool, vb[:, s, :, :].rearrange("p t (h c) -> p t h c", h=4)[:, :, :, 0:DH],
                                           vt[:, s, 0:2, 128:D].rearrange("p t (h d) -> p t h d", d=DH), C["one"][:, :]))
                    for j in range(4):
                        r = slice(32 * j, 32 * j + 32)
                        ins = pool_copy(pool, vL[r, s, :].rearrange("p (g c) -> p g c", g=3)[:, :, 16 * j:16 * j + DH],
                                               vt[r, s, 2, :].rearrange("p (g j d) -> p g j d", g=3, j=4)[:, :, j, :], C["one"][r, :])
                        if j < 3:
                            chain(ins)
                    ins.then_inc(v_ready[s], 1)
                    pool.wait_ge(v_ready[s], it + 1)

                def keep_cls(it, s):
                    pool.wait_ge(b_taken[s], it + 1)
                    pool_copy(pool, C["ocls"][:, :, :, bass.ds(it * 2 + s, 1)], o[:, s, :, 0:NCLS].unsqueeze(3), C["one"][:, :]
                                     ).then_inc(cls_kept[s], 1)
                    pool.wait_ge(cls_kept[s], it + 1)

                for s in range(2):
                    build(0, s)
                with pool.Fori(0, LAST) as it:
                    chain.loop(it, 2 * 8)
                    for s in range(2):
                        keep_cls(it, s)
                        build(it + 1, s)
                chain.end(LAST)
                for s in range(2):
                    keep_cls(LAST, s)

            @block.tensor
            def _(pe):

                def score(it, w):
                    if w >= 2 * UNITS:
                        it, w = it + 1, w - 2 * UNITS
                    s, u = w // UNITS, w % UNITS
                    if u == 0:
                        pe.wait_ge(qk_loaded[s], it * 16 + 16)
                    if u == 2:
                        pe.wait_ge(kL_ready[s], it + 1)
                    pe.wait_ge(exp_done[w % 2], before(it, w))
                    for c in range(3):
                        g, t, j = tiles[3 * u + c]
                        out = ps[:, 3 * (w % 2) + c, 0:N]
                        if t < 2:
                            r = slice(32 * j, 32 * j + 32)
                            ins = pe.matmul(out, qk[r, s, 1, g, t * 128:(t + 1) * 128], qk[r, s, 0, g, 0:N],
                                            start=True, stop=True)
                        else:
                            ins = pe.matmul(out, kL[:, s, g, :, :].rearrange("p j n -> p (j n)"), qk[:, s, 0, g, 0:N],
                                            start=True, stop=True)
                    ins.then_inc(scored[w % 2], 1)

                def times_v(it, w):
                    s, u = w // UNITS, w % UNITS
                    if u == 0:
                        pe.wait_ge(v_ready[s], it + 1)
                        pe.wait_ge(a_taken, it * 2 + s)
                    if u == A_LAST + 1:
                        pe.wait_ge(b_taken[1 - s], it + s)
                    pe.wait_ge(rounded[w % 2], before(it, w) + 1)
                    for c in range(3):
                        n = 3 * u + c
                        g, t, j = tiles[n]
                        probs = p[:, w % 2, c, 0:N]
                        if g < 2:
                            h = 4 * g + j
                            v = va[:, s, t, 128 * h:128 * h + 128] if t < 2 else vL[:, s, 128 * g:128 * g + 128]
                            ins = pe.matmul(ps[:, 6, 0:N], v, probs, start=(n == 0), stop=(n == 3 * A_LAST + 2))
                        else:
                            v = vb[:, s, t, 64 * j:64 * j + 64] if t < 2 else vL[:, s, 384:448]
                            ins = pe.matmul(ps[0:64, 7, 0:N], v, probs, start=(n == 3 * A_LAST + 3),
                                            stop=(n == len(tiles) - 1))
                    ins.then_inc(used[w % 2], 1)

                def step(it, last):
                    for w in range(2 * UNITS):
                        if not (last and w + 2 >= 2 * UNITS):
                            score(it, w + 2)
                        times_v(it, w)

                score(0, 0)
                score(0, 1)
                with pe.Fori(0, LAST) as it:
                    step(it, False)
                step(LAST, True)

            @block.scalar
            def _(act):
                alpha = act.alloc_register("alpha2")
                act.reg_load(alpha, sc[0:1, ALPHA:ALPHA + 1].bitcast(U32))
                act.preload_act_table(ACT.Exp)
                with act.Fori(0, B // 2) as it:
                    for w in range(2 * UNITS):
                        at = w % 2
                        act.wait_ge(scored[at], before(it, w) + 1)
                        act.wait_ge(rounded[at], before(it, w))
                        act.activation(e[:, at, :, :], ps[:, 3 * at:3 * at + 3, 0:N], ACT.Exp, scale=alpha
                                       ).then_inc(exp_done[at], 1)

            @block.vector
            def _(v):
                chain = Chain(v, vchain)
                chain(v.memset(o[D2:128, :, 1, :], 0.0))
                chain(v.memset(mx[:, :, :], 0.0))
                chain(v.memset(C["omax"][:, :], 0.0))
                with v.Fori(0, B // 2) as it:
                    chain.loop(it, 2)
                    for w in range(2 * UNITS):
                        at, s, u = w % 2, w // UNITS, w % UNITS
                        v.wait_ge(exp_done[at], before(it, w) + 1)
                        v.wait_ge(used[at], before(it, w))
                        v.tensor_scalar(p[:, at, :, 0:N], e[:, at, :, :], ROUND, ROUND, ALU.add, ALU.subtract
                                        ).then_inc(rounded[at], 1)
                        if u == A_LAST + 1:
                            v.wait_ge(used[1 - at], before(it, w - 1) + 1)
                            v.wait_ge(o_stored[s], it * 32)
                            v.wait_ge(cls_kept[s], it)
                            v.tensor_reduce(mx[:, s, 0:1], ps[:, 6, 0:N], AX.X, ALU.max, apply_absolute_value=True)
                            v.tensor_copy(o[:, s, 0, :], ps[:, 6, 0:N]).then_inc(a_taken, 1)
                        if u == UNITS - 1:
                            v.wait_ge(used[at], before(it, w) + 1)
                            v.tensor_reduce(mx[0:64, s, 1:2], ps[0:64, 7, 0:N], AX.X, ALU.max, apply_absolute_value=True)
                            v.tensor_copy(o[0:64, s, 1, :], ps[0:64, 7, 0:N]).then_inc(b_taken[s], 1)
                            v.wait_ge(b_taken[s], it + 1)
                            chain(v.tensor_tensor(C["omax"][:, :], C["omax"][:, :], mx[:, s, :], ALU.max))
                chain.end(B // 2)


GROUP_TOKENS = 336
GP = GROUP_TOKENS // 3
GROUPS = TOKENS // GROUP_TOKENS


def output_scales(nc, T, C):
    sc = C["sc"]
    one = lambda i: sc[:, i:i + 1]
    with ExitStack() as ctx:
        m = Mem(nc, ctx, "os")
        mx = m.sb("mx", [128, 1])
        gx = m.sb("gx", [128, 1])
        mx_ready = m.sem("mx_ready")
        gx_ready = m.sem("gx_ready")
        vchain = m.sem("vchain")
        with nc.Block() as block:

            @block.gpsimd
            def _(pool):
                pool.wait_ge(mx_ready, 1)
                pool.partition_all_reduce(gx[:, :], mx[:, :], 128, RMAX).then_inc(gx_ready, 1)

            @block.vector
            def _(v):
                chain = Chain(v, vchain)
                v.tensor_reduce(mx[:, :], C["omax"][:, :], AX.X, ALU.max).then_inc(mx_ready, 1)
                v.wait_ge(gx_ready, 1)
                chain(v.tensor_scalar(one(TMP), gx[:, :], one(SO_IN), None, ALU.mult))
                chain(v.tensor_scalar(one(SOUT), one(TMP), 1.0 / QMAX, SCALE_FLOOR, ALU.mult, ALU.max))
                chain(v.reciprocal(one(ISOUT), one(SOUT)))
                v.tensor_tensor(one(HOUT), one(SOUT), one(SX + 2), ALU.mult)
                v.tensor_tensor(one(AOUT), one(ISOUT), one(SO_IN), ALU.mult)


def output_phase(nc, T, C):
    sc = C["sc"]
    G = GROUP_TOKENS
    LOOP = (GROUPS - 4) // 2
    with ExitStack() as ctx:
        m = Mem(nc, ctx, "out")
        w1 = m.sb("w1", [128, 2, F])
        b1 = m.sb("b1", [128, FT])
        w2 = m.sb("w2", [128, FT, D])
        rows = m.sb("rows", [GP, 2, D])
        rounding = m.sb("rounding", [128, 1])
        ot = m.sb("ot", [128, 2, 2, G])
        big = m.sb("big", [128, 2, 3, GP])
        oq = m.sb("oq", [128, 2, 2, 3, GP], BF16)
        hin = m.sb("hin", [GP, 2, 3, D])
        hb = m.sb("hb", [GP, 2, 3, D])
        h2 = m.sb("h2", [GP, 2, 3, D])
        h2b = m.sb("h2b", [GP, 2, 3, D])
        bn = m.sb("bn", [GP, 3, 6])
        mv = m.sb("mv", [GP, 3, 2])
        var = m.sb("var", [GP, 3])
        rstd = m.sb("rstd", [GP, 3])
        y = m.sb("y", [GP, 3, D])
        yT = m.sb("yT", [128, 2, G])
        act_out = m.sb("act_out", [128, FT, G])
        gap = m.sb("gap", [1, 1])
        out = m.sb("out", [GP, 2, 3, D])
        ps = m.ps("ps", [128, 8, 512])
        w_loaded = m.sem("w_loaded")
        ot_loaded = [m.sem(f"ot_loaded{s}") for s in range(2)]
        hin_loaded = [m.sem(f"hin_loaded{s}") for s in range(2)]
        const_set = m.sem("const_set")
        big_done = m.sem("big_done")
        oq_ready = m.sem("oq_ready")
        proj_mm = m.sem("proj_mm")
        hb_ready = m.sem("hb_ready")
        h2_done = m.sem("h2_done")
        h2b_ready = m.sem("h2b_ready")
        var_ready = m.sem("var_ready")
        rstd_ready = m.sem("rstd_ready")
        y_ready = m.sem("y_ready")
        turned = m.sem("turned")
        yT_ready = m.sem("yT_ready")
        fc1_mm = m.sem("fc1_mm")
        gelu_done = m.sem("gelu_done")
        fc2_mm = m.sem("fc2_mm")
        out_done = m.sem("out_done")
        stored = [m.sem(f"stored{s}") for s in range(2)]
        vchain = m.sem("vchain")

        def exists(it, s, k):
            return not isinstance(it, int) or 2 * it + s + k < GROUPS

        def steps(eng, body):
            with eng.Fori(0, LOOP) as it:
                for s in range(2):
                    body(it, s)
            for it in range(LOOP, GROUPS // 2):
                for s in range(2):
                    body(it, s)

        with nc.Block() as block:

            @block.sync
            def _(sp):
                sp.dma_start(w1[:, :, :], T["mw1"]).then_inc(w_loaded, 16)
                sp.dma_start(b1[:, :], T["mb1"]).then_inc(w_loaded, 16)
                sp.dma_start(w2[:, :, :], T["mw2"].rearrange("(k p) d -> p k d", p=128)).then_inc(w_loaded, 16)
                sp.dma_start(rows[:, :, :].rearrange("p r d -> p (r d)"),
                             T["rows"][0, 8 * D:10 * D].partition_broadcast(GP)).then_inc(w_loaded, 16)

                def load(it, s, k):
                    q, m = (s + k) % 2, it * 2 + (s + k)
                    if not (isinstance(m, int) and m < 2):
                        sp.wait_ge(big_done, m - 1)
                        sp.wait_ge(hb_ready, m - 1)
                    sp.dma_start(ot[:, q, 0, :], T["OT"][0:128, bass.ts(m, G)]).then_inc(ot_loaded[q], 16)
                    sp.dma_start(ot[0:D2, q, 1, :], T["OT"][128:D, bass.ts(m, G)]).then_inc(ot_loaded[q], 16)
                    sp.dma_start(hin[:, q, :, :].rearrange("p i d -> p (i d)"),
                                 T["H"].rearrange("(r i) d -> r (i d)", i=3)[bass.ts(m, GP), :]).then_inc(hin_loaded[q], 16)

                sp.wait_ge(const_set, 2)
                for k in range(2):
                    load(0, 0, k)
                sp.dma_start(C["a1"][:, :, :], T["a1"]).then_inc(C["experts_loaded"], 16)
                sp.dma_start(C["a2"][:, :, :], T["a2"].rearrange("(k p) d -> p k d", p=128)).then_inc(C["experts_loaded"], 16)
                for k in range(2, 4):
                    load(0, 0, k)

                def body(it, s):
                    if exists(it, s, 4):
                        load(it, s, 4)
                    sp.wait_ge(out_done, it * 2 + (s + 1))
                    sp.dma_start(T["out"].rearrange("(r i) d -> r (i d)", i=3)[bass.ts(it * 2 + s, GP), :],
                                 out[:, s, :, :].rearrange("p i d -> p (i d)")).then_inc(stored[s], 16)

                steps(sp, body)
                for s in range(2):
                    sp.wait_ge(stored[s], 8 * GROUPS)
                sp.wait_ge(C["experts_loaded"], 32)

            @block.gpsimd
            def _(pool):
                pool.wait_ge(w_loaded, 64)

                def with_bias(it, s, k):
                    q, m = (s + k) % 2, it * 2 + (s + k)
                    pool.wait_ge(hin_loaded[q], it * 16 + (s + k) // 2 * 16 + 16)
                    if not (isinstance(m, int) and m < 2):
                        pool.wait_ge(h2_done, m - 1)
                    pool.tensor_tensor(hb[:, q, :, :], hin[:, q, :, :],
                                       rows[:, 0:1, :].to_broadcast([GP, 3, D]), ALU.add).then_inc(hb_ready, 1)

                def norm(it, s, k):
                    q, m = (s + k) % 2, it * 2 + (s + k)
                    pool.wait_ge(var_ready, m + 1)
                    pool.tensor_tensor(rstd[:, :], var[:, :], C["nhalf"][0:GP, 0:3], ALU.pow).then_inc(rstd_ready, 1)
                    if not (isinstance(m, int) and m < 2):
                        pool.wait_ge(out_done, m - 1)
                    pool.tensor_tensor(h2b[:, q, :, :], h2[:, q, :, :], rows[:, 1:2, :].to_broadcast([GP, 3, D]), ALU.add
                                       ).then_inc(h2b_ready, 1)

                with_bias(0, 0, 0)
                with_bias(0, 0, 1)
                norm(0, 0, 0)

                def body(it, s):
                    if exists(it, s, 1):
                        norm(it, s, 1)
                    if exists(it, s, 2):
                        with_bias(it, s, 2)

                steps(pool, body)

            @block.scalar
            def _(act):
                aout = act.alloc_register("scale_out")
                act.reg_load(aout, sc[0:1, AOUT:AOUT + 1].bitcast(U32))
                act.preload_act_table(ACT.Gelu)
                act.wait_ge(w_loaded, 64)
                act.wait_ge(const_set, 2)

                def enlarge(it, s, k):
                    q, m = (s + k) % 2, it * 2 + (s + k)
                    act.wait_ge(ot_loaded[q], it * 32 + (s + k) // 2 * 32 + 32)
                    if not (isinstance(m, int) and m < 1):
                        act.wait_ge(oq_ready, m)
                    for kk in range(2):
                        ins = act.activation(big[:, kk, :, :], ot[:, q, kk, :].rearrange("c (p i) -> c i p", i=3),
                                             ACT.Identity, scale=aout, bias=rounding[:, 0:1])
                    ins.then_inc(big_done, 1)

                def take_turned(it, s, k):
                    act.wait_ge(turned, it * 2 + (s + k + 1))
                    act.activation(yT[:, 0, :], ps[:, 2, 0:G], ACT.Copy)
                    act.activation(yT[0:D2, 1, :], ps[0:D2, 3, 0:G], ACT.Copy).then_inc(yT_ready, 1)

                enlarge(0, 0, 0)
                enlarge(0, 0, 1)
                take_turned(0, 0, 0)

                def body(it, s):
                    if exists(it, s, 2):
                        enlarge(it, s, 2)
                    act.wait_ge(fc2_mm, it * 2 + s)
                    for f in range(FT):
                        act.wait_ge(fc1_mm, it * (2 * FT) + (s * FT + f + 1))
                        act.activation(act_out[:, f, :], ps[:, 4 + f % 2, 0:G], ACT.Gelu, bias=b1[:, f:f + 1]
                                       ).then_inc(gelu_done, 1)
                    if exists(it, s, 1):
                        take_turned(it, s, 1)

                steps(act, body)

            @block.tensor
            def _(pe):
                pe.wait_ge(w_loaded, 64)
                place = lambda first, i: ps[0:GP, first + i // 2, (i % 2) * D:(i % 2) * D + D]

                def project(it, s, k):
                    q, m = (s + k) % 2, it * 2 + (s + k)
                    pe.wait_ge(oq_ready, m + 1)
                    if not (isinstance(m, int) and m < 1):
                        pe.wait_ge(h2_done, m)
                    for i in range(3):
                        for kk in range(2):
                            K = (128, D2)[kk]
                            ins = pe.matmul(place(0, i), oq[0:K, q, kk, i, :], C["wpint"][0:K, kk, :],
                                            start=(kk == 0), stop=(kk == 1), skip_group_check=True)
                    ins.then_inc(proj_mm, 1)

                def turn(it, s, k):
                    m = it * 2 + (s + k)
                    pe.wait_ge(y_ready, m + 1)
                    if not (isinstance(m, int) and m < 1):
                        pe.wait_ge(yT_ready, m)
                    for kk in range(2):
                        K = (128, D2)[kk]
                        for i in range(3):
                            ins = pe.transpose(ps[0:K, 2 + kk, i * GP:(i + 1) * GP], y[:, i, 128 * kk:128 * kk + K],
                                               C["ident"][0:GP, 0:GP])
                    ins.then_inc(turned, 1)

                project(0, 0, 0)
                turn(0, 0, 0)

                def body(it, s):
                    n = it * 2 + s
                    if exists(it, s, 1):
                        project(it, s, 1)
                    pe.wait_ge(yT_ready, n + 1)
                    for f in range(FT):
                        if f >= 2:
                            pe.wait_ge(gelu_done, it * (2 * FT) + (s * FT + f - 1))
                        for kk in range(2):
                            K = (128, D2)[kk]
                            ins = pe.matmul(ps[:, 4 + f % 2, 0:G], w1[0:K, kk, f * 128:(f + 1) * 128], yT[0:K, kk, :],
                                            start=(kk == 0), stop=(kk == 1))
                        ins.then_inc(fc1_mm, 1)
                    if exists(it, s, 1):
                        turn(it, s, 1)
                    pe.wait_ge(gelu_done, it * (2 * FT) + (s * FT + FT))
                    pe.wait_ge(out_done, n)
                    for i in range(3):
                        for f in range(FT):
                            ins = pe.matmul(place(6, i), act_out[:, f, i * GP:(i + 1) * GP], w2[:, f, :],
                                            start=(f == 0), stop=(f == FT - 1), skip_group_check=True)
                    ins.then_inc(fc2_mm, 1)

                steps(pe, body)

            @block.vector
            def _(v):
                chain = Chain(v, vchain)
                v.memset(rounding[:, :], ROUND).then_inc(const_set, 1)
                v.memset(ot[:, :, :, :], 0.0).then_inc(const_set, 1)
                v.wait_ge(w_loaded, 64)

                def quantize(it, s, k):
                    q, m = (s + k) % 2, it * 2 + (s + k)
                    v.wait_ge(big_done, m + 1)
                    if not (isinstance(m, int) and m < 2):
                        v.wait_ge(proj_mm, m - 1)
                    v.tensor_scalar(oq[:, q, :, :, :], big[:, :, :, :], ROUND, None, ALU.subtract).then_inc(oq_ready, 1)

                def both(first, t, q):
                    two = ps[0:GP, first, 0:2 * D].rearrange("p (i d) -> p i d", i=2)
                    return (two, t[:, q, 0:2, :]), (ps[0:GP, first + 1:first + 2, 0:D], t[:, q, 2:3, :])

                def norm(it, s, k):
                    q, m = (s + k) % 2, it * 2 + (s + k)
                    v.wait_ge(proj_mm, m + 1)
                    v.wait_ge(hb_ready, m + 1)
                    if not (isinstance(m, int) and m < 2):
                        v.wait_ge(h2b_ready, m - 1)
                    for (src, dst), (_, add) in zip(both(0, h2, q), both(0, hb, q)):
                        ins = v.scalar_tensor_tensor(out=dst, in0=src, scalar=sc[0:GP, HOUT:HOUT + 1], in1=add,
                                                     op0=ALU.mult, op1=ALU.add)
                    ins.then_inc(h2_done, 1)
                    v.wait_ge(h2_done, m + 1)
                    for i in range(3):
                        ins = v.bn_stats(bn[:, i, :], h2[:, q, i, :])
                    chain(ins)
                    v.memset(gap[:, :], 0.0)
                    for i in range(3):
                        ins = v.bn_aggr(mv[:, i, :], bn[:, i, :])
                    chain(ins)
                    v.tensor_scalar(var[:, :], mv[:, :, 1], EPS, None, ALU.add).then_inc(var_ready, 1)
                    if not (isinstance(m, int) and m < 1):
                        v.wait_ge(turned, m)
                    v.wait_ge(rstd_ready, m + 1)
                    for i in range(3):
                        ins = v.tensor_scalar(y[:, i, :], h2[:, q, i, :], mv[:, i, 0:1], rstd[:, i:i + 1],
                                              ALU.subtract, ALU.mult)
                    ins.then_inc(y_ready, 1)

                quantize(0, 0, 0)
                quantize(0, 0, 1)
                norm(0, 0, 0)

                def body(it, s):
                    if exists(it, s, 1):
                        norm(it, s, 1)
                    if exists(it, s, 2):
                        quantize(it, s, 2)
                    n = it * 2 + s
                    v.wait_ge(fc2_mm, n + 1)
                    v.wait_ge(h2b_ready, n + 1)
                    v.wait_ge(stored[s], it * 16)
                    for (src, dst), (_, add) in zip(both(6, out, s), both(6, h2b, s)):
                        ins = v.tensor_tensor(dst, src, add, ALU.add)
                    ins.then_inc(out_done, 1)

                with v.Fori(0, LOOP) as it:
                    chain.loop(it, 4)
                    for s in range(2):
                        body(it, s)
                chain.end(LOOP)
                for it in range(LOOP, GROUPS // 2):
                    for s in range(2):
                        body(it, s)


def class_phase(nc, T, C):
    sc = C["sc"]
    P, E, A = 3 * B, 2, 3
    with ExitStack() as ctx:
        m = Mem(nc, ctx, "cl")
        b1 = m.sb("b1", [128, 5 * FT])
        gw = m.sb("gw", [128, 2, 2 * NCLS])
        a2b = m.sb("a2b", [P, 2, E, D])
        bp = m.sb("bp", [P, D])
        hin = m.sb("hin", [P, E, D])
        hb = m.sb("hb", [P, E, D])
        rounding = m.sb("rounding", [128, 1])
        big = m.sb("big", [128, 2, E * P])
        oq = m.sb("oq", [128, 2, E * P], BF16)
        h2 = m.sb("h2", [P, E, D])
        bn = m.sb("bn", [P, E, 6])
        mv = m.sb("mv", [P, E, 2])
        var = m.sb("var", [P, E])
        rstd = m.sb("rstd", [P, E])
        y = m.sb("y", [P, E, D])
        yT = m.sb("yT", [128, 2, E * P])
        hid = m.sb("hid", [128, 2, FT, E * P])
        lg = m.sb("lg", [P, E, 2])
        lx = m.sb("lx", [P, E, 2])
        le = m.sb("le", [P, E, 2])
        gate = m.sb("gate", [P, E, 2])
        kept = m.sb("kept", [P, E, 2])
        final = m.sb("final", [P, E, 2])
        mask = m.sb("mask", [P, E, 2])
        r1 = m.sb("r1", [P, 4, E])
        res = m.sb("res", [P, 2, E, D])
        out = m.sb("out", [P, 2, E, D])
        ps = m.ps("ps", [128, 8, 512])
        loaded = m.sem("loaded")
        const_set = m.sem("const_set")
        big_done = m.sem("big_done")
        oq_ready = m.sem("oq_ready")
        proj_mm = m.sem("proj_mm")
        var_ready = m.sem("var_ready")
        rstd_ready = m.sem("rstd_ready")
        y_ready = m.sem("y_ready")
        turned = m.sem("turned")
        yT_ready = m.sem("yT_ready")
        gates_mm = m.sem("gates_mm")
        gates_out = m.sem("gates_out")
        less_max = m.sem("less_max")
        gate_exp = m.sem("gate_exp")
        fc1_mm = m.sem("fc1_mm")
        gelu_done = m.sem("gelu_done")
        fc2_mm = m.sem("fc2_mm")
        out_ready = m.sem("out_ready")
        stored = m.sem("stored")
        vchain = m.sem("vchain")
        by_sample = lambda t: t.rearrange("(b n) d -> b n d", b=B)
        NLOAD = 3 + 2 + 3 * E + NCLS
        with nc.Block() as block:

            @block.sync
            def _(sp):
                for a in range(A):
                    for e in range(E):
                        sp.dma_start(hin[B * a:B * a + B, e, :], by_sample(T["H"])[:, 2 * a + e, :]).then_inc(loaded, 16)
                sp.dma_start(b1[:, :], T["a1b"]).then_inc(loaded, 16)
                sp.dma_start(gw[:, :, :], T["gw"]).then_inc(loaded, 16)
                sp.dma_start(bp[:, :], T["rows"][0, 8 * D:9 * D].partition_broadcast(P)).then_inc(loaded, 16)
                for e in range(E):
                    sp.dma_start(a2b[:, 0, e, :], T["a2b"][3 + e, :].partition_broadcast(P)).then_inc(loaded, 16)
                    for a in range(A):
                        sp.dma_start(a2b[B * a:B * a + B, 1, e, :], T["a2b"][a, :].partition_broadcast(B)).then_inc(loaded, 16)
                sp.wait_ge(out_ready, 1)
                for a in range(A):
                    for e in range(E):
                        sp.dma_start(by_sample(T["out"])[:, 2 * a + e, :], out[B * a:B * a + B, 1, e, :]).then_inc(stored, 16)
                sp.wait_ge(stored, 16 * NCLS)

            @block.gpsimd
            def _(pool):
                pool.wait_ge(var_ready, 1)
                pool.tensor_tensor(rstd[:, :], var[:, :], C["nhalf"][0:P, 0:E], ALU.pow).then_inc(rstd_ready, 1)

            @block.scalar
            def _(act):
                aout = act.alloc_register("scale_out_c")
                act.reg_load(aout, sc[0:1, AOUT:AOUT + 1].bitcast(U32))
                act.preload_act_table(ACT.Gelu)
                act.wait_ge(const_set, 1)
                act.wait_ge(loaded, 16 * NLOAD)
                for e in range(E):
                    ins = act.activation(big[:, :, e * P:(e + 1) * P].rearrange("p k (a b) -> p k a b", a=A),
                                         C["ocls"][:, :, :, :].rearrange("p k (a e) b -> p k e a b", e=E)[:, :, e, :, :],
                                         ACT.Identity, scale=aout, bias=rounding[:, 0:1])
                ins.then_inc(big_done, 1)
                act.wait_ge(turned, 1)
                act.activation(yT[:, 0, :], ps[:, 2, 0:E * P], ACT.Copy)
                act.activation(yT[0:D2, 1, :], ps[0:D2, 3, 0:E * P], ACT.Copy).then_inc(yT_ready, 1)
                act.wait_ge(less_max, 1)
                act.activation(le[:, :, :], lx[:, :, :], ACT.Exp).then_inc(gate_exp, 1)
                act.preload_act_table(ACT.Gelu)
                for f in range(FT):
                    for pair in range(2):
                        n = 2 * f + pair
                        act.wait_ge(fc1_mm, n + 1)
                        src, dst = ps[:, 4 + n % 4, 0:E * P], hid[:, pair, f, :]
                        if pair == 0:
                            split = lambda t: t.rearrange("p (e a b) -> p a e b", e=E, a=A)
                            for a in range(A):
                                ins = act.activation(split(dst)[:, a, :, :], split(src)[:, a, :, :], ACT.Gelu,
                                                     bias=b1[:, a * FT + f:a * FT + f + 1])
                        else:
                            for e in range(E):
                                x = (3 + e) * FT + f
                                ins = act.activation(dst[:, e * P:(e + 1) * P], src[:, e * P:(e + 1) * P], ACT.Gelu,
                                                     bias=b1[:, x:x + 1])
                        ins.then_inc(gelu_done, 1)

            @block.tensor
            def _(pe):
                pe.wait_ge(loaded, 16 * NLOAD)
                pe.wait_ge(oq_ready, 1)
                for e in range(E):
                    for k in range(2):
                        K = (128, D2)[k]
                        ins = pe.matmul(ps[0:P, 0, e * D:(e + 1) * D], oq[0:K, k, e * P:(e + 1) * P], C["wpint"][0:K, k, :],
                                        start=(k == 0), stop=(k == 1), skip_group_check=True)
                ins.then_inc(proj_mm, 1)
                pe.wait_ge(y_ready, 1)
                for k in range(2):
                    K = (128, D2)[k]
                    for e in range(E):
                        ins = pe.transpose(ps[0:K, 2 + k, e * P:(e + 1) * P], y[:, e, 128 * k:128 * k + K], C["ident"][0:P, 0:P])
                ins.then_inc(turned, 1)
                pe.wait_ge(yT_ready, 1)
                for e in range(E):
                    for k in range(2):
                        K = (128, D2)[k]
                        ins = pe.matmul(ps[0:P, 1, 16 * e:16 * e + 2 * NCLS], yT[0:K, k, e * P:(e + 1) * P], gw[0:K, k, :],
                                        start=(k == 0), stop=(k == 1), skip_group_check=True)
                ins.then_inc(gates_mm, 1)
                for f in range(FT):
                    for pair in range(2):
                        n = 2 * f + pair
                        if n >= 4:
                            pe.wait_ge(gelu_done, n - 3)
                        out4 = ps[:, 4 + n % 4, 0:E * P]
                        split = lambda t: t.rearrange("p (e a b) -> p a e b", e=E, a=A)
                        for x in range(A if pair == 0 else E):
                            ex = x if pair == 0 else 3 + x
                            for k in range(2):
                                K = (128, D2)[k]
                                w = C["a1"][0:K, k, ex * F + f * 128:ex * F + (f + 1) * 128]
                                if pair == 0:
                                    dst, src = split(out4)[:, x, :, :], split(yT[0:K, k, :])[:, x, :, :]
                                else:
                                    dst, src = out4[:, x * P:(x + 1) * P], yT[0:K, k, x * P:(x + 1) * P]
                                ins = pe.matmul(dst, w, src, start=(k == 0), stop=(k == 1), skip_group_check=True)
                        ins.then_inc(fc1_mm, 1)
                pe.wait_ge(gelu_done, 2 * FT)
                pe.wait_ge(gates_out, 1)
                for e in range(E):
                    for f in range(FT):
                        ins = pe.matmul(ps[0:P, 0, e * D:(e + 1) * D], hid[:, 0, f, e * P:(e + 1) * P],
                                        C["a2"][:, (3 + e) * FT + f, :], start=(f == 0), stop=(f == FT - 1), skip_group_check=True)
                for a in range(A):
                    for e in range(E):
                        for f in range(FT):
                            ins = pe.matmul(ps[0:P, 1 + a, e * D:(e + 1) * D], hid[:, 1, f, e * P:(e + 1) * P],
                                            C["a2"][:, a * FT + f, :], start=(f == 0), stop=(f == FT - 1), skip_group_check=True)
                ins.then_inc(fc2_mm, 1)

            @block.vector
            def _(v):
                chain = Chain(v, vchain)
                v.memset(rounding[:, :], ROUND).then_inc(const_set, 1)
                v.wait_ge(loaded, 16 * NLOAD)
                two = ps[0:P, 0, 0:E * D].rearrange("p (e d) -> p e d", e=E)
                chain(v.tensor_tensor(hb[:, :, :], hin[:, :, :], bp[:, :].unsqueeze(1).to_broadcast([P, E, D]), ALU.add))
                v.wait_ge(big_done, 1)
                v.tensor_scalar(oq[:, :, :], big[:, :, :], ROUND, None, ALU.subtract).then_inc(oq_ready, 1)
                v.wait_ge(proj_mm, 1)
                chain(v.scalar_tensor_tensor(out=h2[:, :, :], in0=two, scalar=sc[0:P, HOUT:HOUT + 1], in1=hb[:, :, :],
                                             op0=ALU.mult, op1=ALU.add))
                for e in range(E):
                    ins = v.bn_stats(bn[:, e, :], h2[:, e, :])
                chain(ins)
                for e in range(E):
                    ins = v.bn_aggr(mv[:, e, :], bn[:, e, :])
                chain(ins)
                v.tensor_scalar(var[:, :], mv[:, :, 1], EPS, None, ALU.add).then_inc(var_ready, 1)
                v.wait_ge(rstd_ready, 1)
                for e in range(E):
                    ins = v.tensor_scalar(y[:, e, :], h2[:, e, :], mv[:, e, 0:1], rstd[:, e:e + 1], ALU.subtract, ALU.mult)
                ins.then_inc(y_ready, 1)
                v.wait_ge(gates_mm, 1)
                for a in range(A):
                    r = slice(B * a, B * a + B)
                    ins = v.tensor_copy(lg[r, :, :], ps[r, 1, 0:36].rearrange("p (e x) -> p e x", x=18)[:, :, 4 * a:4 * a + 2])
                ins.then_inc(gates_out, 1)
                v.wait_ge(gates_out, 1)
                wide = lambda i: r1[:, i, :].unsqueeze(2).to_broadcast([P, E, 2])
                chain(v.tensor_reduce(r1[:, 0, :], lg[:, :, :], AX.X, ALU.max))
                v.tensor_tensor(lx[:, :, :], lg[:, :, :], wide(0), ALU.subtract).then_inc(less_max, 1)
                v.wait_ge(gate_exp, 1)
                chain(v.tensor_reduce(r1[:, 1, :], le[:, :, :], AX.X, ALU.add))
                chain(v.reciprocal(r1[:, 2, :], r1[:, 1, :]))
                chain(v.tensor_tensor(gate[:, :, :], le[:, :, :], wide(2), ALU.mult))
                chain(v.tensor_reduce(r1[:, 3, :], gate[:, :, :], AX.X, ALU.min))
                chain(v.tensor_tensor(mask[:, :, :], gate[:, :, :], wide(3), ALU.is_gt))
                chain(v.tensor_tensor(kept[:, :, :], gate[:, :, :], mask[:, :, :], ALU.mult))
                chain(v.tensor_reduce(r1[:, 0, :], kept[:, :, :], AX.X, ALU.add))
                chain(v.tensor_scalar(r1[:, 1, :], r1[:, 0, :], 1e-6, None, ALU.max))
                chain(v.reciprocal(r1[:, 2, :], r1[:, 1, :]))
                chain(v.tensor_tensor(final[:, :, :], kept[:, :, :], wide(2), ALU.mult))
                v.wait_ge(fc2_mm, 1)
                v.tensor_tensor(res[:, 0, :, :], two, a2b[:, 0, :, :], ALU.add)
                for a in range(A):
                    r = slice(B * a, B * a + B)
                    ins = v.tensor_tensor(res[r, 1, :, :], ps[r, 1 + a, 0:E * D].rearrange("p (e d) -> p e d", e=E),
                                          a2b[r, 1, :, :], ALU.add)
                chain(ins)
                for pair in range(2):
                    for e in range(E):
                        add = h2[:, e, :] if pair == 0 else out[:, 0, e, :]
                        ins = v.scalar_tensor_tensor(out=out[:, pair, e, :], in0=res[:, pair, e, :],
                                                     scalar=final[:, e, pair:pair + 1], in1=add, op0=ALU.mult, op1=ALU.add)
                    if pair == 0:
                        chain(ins)
                ins.then_inc(out_ready, 1)


def final_phases(nc, T, C):
    with ExitStack() as ctx:
        m = Mem(nc, ctx, "fin")
        C["a1"] = m.sb("a1", [128, 2, 5 * F])
        C["a2"] = m.sb("a2", [128, 5 * FT, D])
        C["experts_loaded"] = m.sem("experts_loaded")
        output_scales(nc, T, C)
        output_phase(nc, T, C)
        class_phase(nc, T, C)


def setup(nc, T, C):
    with ExitStack() as ctx:
        m = Mem(nc, ctx, "se")
        tok = m.sb("tok", [NTXT, B], I32)
        tf = m.sb("tf", [NTXT, B])
        below = m.sb("below", [NTXT, B])
        tw = m.sb("tw", [NTXT, B])
        idx = m.sb("idx", [NTXT, B], I32)
        loaded = m.sem("loaded")
        idx_ready = m.sem("idx_ready")
        gathered = m.sem("gathered")
        vchain = m.sem("vchain")
        with nc.Block() as block:

            @block.sync
            def _(sp):
                sp.dma_start(tok[:, :], T["tok"]).then_inc(loaded, 16)
                sp.dma_start(C["ident"][:, :], T["ident"]).then_inc(loaded, 16)
                sp.wait_ge(loaded, 32)

            @block.gpsimd
            def _(pool):
                pool.wait_ge(idx_ready, 1)
                for b in range(B):
                    pool.indirect_dma_start(out=C["emb"][:, b, :], out_offset=None, in_=T["emb"],
                                            in_offset=bass.IndirectOffsetOnAxis(ap=idx[:, b:b + 1], axis=0)
                                            ).then_inc(gathered, 16)
                pool.wait_ge(gathered, 16 * B)

            @block.vector
            def _(v):
                chain = Chain(v, vchain)
                v.memset(C["nhalf"][:, :], -0.5)
                v.memset(C["one"][:, :], 1.0)
                v.memset(C["half"][:, :], 0.5)
                v.memset(C["ymax_txt"][:, :], 0.0)
                v.wait_ge(loaded, 32)
                v.tensor_copy(C["identb"][:, :], C["ident"][:, :])
                chain(v.tensor_copy(tf[:, :], tok[:, :]))
                chain(v.tensor_scalar(below[:, :], tf[:, :], 0.0, float(VOCAB), ALU.is_lt, ALU.mult))
                chain(v.tensor_tensor(tw[:, :], tf[:, :], below[:, :], ALU.add))
                chain(v.tensor_scalar(tf[:, :], tw[:, :], 0.0, float(VOCAB - 1), ALU.max, ALU.min))
                v.tensor_copy(idx[:, :], tf[:, :]).then_inc(idx_ready, 1)


def program(nc, T):
    with ExitStack() as ctx:
        m = Mem(nc, ctx, "c")
        C = {}
        C["nhalf"], C["half"] = m.sb("nhalf", [128, 96]), m.sb("half", [128, 96])
        C["one"] = m.sb("one", [128, 1])
        C["ident"], C["identb"] = m.sb("ident", [128, 128]), m.sb("identb", [128, 128], BF16)
        C["ymax_img"], C["ymax_txt"] = m.sb("ymax_img", [128, 1]), m.sb("ymax_txt", [128, 1])
        C["sc"] = m.sb("sc", [128, NSC])
        C["qkvmax"], C["omax"] = m.sb("qkvmax", [128, 3]), m.sb("omax", [128, 2])
        C["wint"], C["wpint"] = m.sb("wint", [128, 2, 3 * D], BF16), m.sb("wpint", [128, 2, D], BF16)
        C["wqkp"] = m.sb("wqkp", [128, 2, 2 * HEADS, 32], BF16)
        C["nmax"], C["zsum"] = m.sb("nmax", [128, B * 27]), m.sb("zsum", [128, B * 27])
        C["ocls"] = m.sb("ocls", [128, 2, NCLS, B])
        with ExitStack() as first:
            C["emb"] = Mem(nc, first, "c").sb("emb", [NTXT, B, D])
            setup(nc, T, C)
            image_phase(nc, T, C)
            text_phase(nc, T, C)
        scales(nc, T, C)
        quantize_phase(nc, T, C)
        head_scales(nc, T, C)
        qkv_phase(nc, T, C)
        row_phase(nc, T, C)
        row_offsets(nc, T, C)
        product_phase(nc, T, C)
        final_phases(nc, T, C)


SCRATCH = {"H": ((TOKENS, D), F32),
           "Y": ((TOKENS, D), F32),
           "YQ": ((B * D, NE), BF16),
           "QK": ((2, 128, B * 3 * NE), BF16),
           "V": ((B * 128, 3 * D), BF16),
           "OFF": ((B * 27, 3, 128), BF16),
           "OT": ((D, TOKENS), F32)}


def lay_out(np, inputs):
    take = lambda n: np.asarray(inputs[n])
    out = {}
    x = take("x")
    pix = counts()
    npix = len(pix)
    ys, xs = np.array([p[1] for p in pix]), np.array([p[2] for p in pix])
    xp = np.zeros((B, CH, IMG + 2, IMG + 2), x.dtype)
    xp[:, :, 1:-1, 1:-1] = x
    at = np.arange(GRID) * PATCH + 1
    cols = xp[:, :, at[:, None, None] + ys, at[None, :, None] + xs]
    cols = cols.reshape(B, CH, STEPS, IPT, TILES, npix).transpose(2, 4, 5, 1, 0, 3)
    cols = cols.reshape(STEPS * TILES, KT, KP, 128).transpose(0, 2, 1, 3)
    out["xcol"] = np.ascontiguousarray(cols).reshape(STEPS * TILES * KP, KT * 128)
    src = np.array([p[3] for p in pix])
    feat = np.where(src[:, None, :] >= 0, src[:, None, :] * 15 + np.arange(5) * CH + np.arange(CH)[:, None], FEAT)
    feat = feat.reshape(KT, KP, 5).transpose(1, 0, 2)
    pad = lambda a: np.concatenate([a, np.zeros((1,) + a.shape[1:], a.dtype)])
    out["wsh"] = pad(take("L0_tok_W"))[feat]
    out["gsh"] = pad(take("L0_tok_gamma"))[feat]
    out["bsh"] = pad(take("L0_tok_beta"))[feat]
    cnt = np.repeat([p[0] for p in pix], CH).reshape(KT, KP).T
    out["cntw"] = (cnt / FEAT).astype(np.float32)
    out["rootw"] = np.sqrt(cnt / FEAT).astype(np.float32)
    rows = ["L0_tok_b", "L0_txt_bv", "L0_txt_bo", "L0_txt_gamma1", "L0_txt_beta1", "L0_txt_b2", "L0_txt_gamma2",
            "L0_txt_beta2", "L0_attn_b_proj", "L0_ffn_moe0_b2"]
    out["rows"] = np.concatenate([take(r) for r in rows])[None, :]
    def two(a):
        t = np.zeros((2, 128, a.shape[1]), a.dtype)
        t[0], t[1, :D2] = a[:128], a[128:]
        return t.transpose(1, 0, 2)

    def spread(a):
        t = np.zeros(a.shape[:-1] + (3, 4, 32), a.dtype)
        t[..., :DH] = a.reshape(a.shape[:-1] + (3, 4, DH))
        return t.reshape(a.shape[:-1] + (384,))

    out["tok"] = take("x_txt").T
    out["emb"] = take("L0_txt_emb")
    wqk = np.stack([two(spread(take("L0_txt_wq"))), two(spread(take("L0_txt_wk")))], axis=2)
    out["wqk"] = wqk
    out["bqk"] = np.concatenate([spread(take("L0_txt_bq")).reshape(3, 128), spread(take("L0_txt_bk")).reshape(3, 128)]).T
    out["wv"], out["wo"], out["w1"] = two(take("L0_txt_wv")), two(take("L0_txt_wo")), two(take("L0_txt_w1"))
    out["b1"] = take("L0_txt_b1").reshape(FT, 128).T
    out["w2"] = take("L0_txt_w2")
    out["wqkv"], out["wproj"] = two(take("L0_attn_w_qkv")), two(take("L0_attn_w_proj"))
    out["bqkv"] = take("L0_attn_b_qkv")[None, :]
    t = np.full((4, 32), ROUND, np.float32)
    t[:, DH:DH + 3] -= 1.0
    out["kround"] = t.reshape(128, 1)
    place = np.arange(NTXT, dtype=np.float32)[:, None]
    i = np.arange(D, dtype=np.float32)[None, :]
    power = np.power(10000.0, (np.float32(2.0) * i / np.float32(D)).astype(np.float64)).astype(np.float32)
    ang = (place / power).astype(np.float64)
    out["pos"] = np.where(np.arange(D)[None, :] % 2 == 0, np.cos(ang), np.sin(ang)).astype(np.float32)
    out["ident"] = np.eye(128, dtype=np.float32)
    out["mw1"], out["mw2"] = two(take("L0_ffn_moe0_W1")), take("L0_ffn_moe0_W2")
    out["mb1"] = take("L0_ffn_moe0_b1").reshape(FT, 128).T
    out["a1"] = two(take("L0_ffn_A1_W").transpose(1, 0, 2).reshape(D, 5 * F))
    out["a1b"] = take("L0_ffn_A1_b").reshape(5 * FT, 128).T
    out["a2"], out["a2b"] = take("L0_ffn_A2_W").reshape(5 * F, D), take("L0_ffn_A2_b")
    out["gw"] = two(take("L0_ffn_G_W").transpose(1, 0, 2).reshape(D, 2 * NCLS))
    return {k: np.ascontiguousarray(a) for k, a in out.items()}


def kernel(**inputs):
    import numpy as np
    import concourse.bacc as bacc
    from concourse import mybir
    from concourse.bass_utils import run_bass_kernel_spmd

    nc = bacc.Bacc("TRN2", target_bir_lowering=False, num_devices=1)
    T, arrays = {}, {}
    for name, a in lay_out(np, inputs).items():
        arrays["in_" + name] = a
        T[name] = nc.dram_tensor("in_" + name, a.shape, mybir.dt.from_np(a.dtype), kind="ExternalInput").ap()
    for name, (shape, dtype) in SCRATCH.items():
        T[name] = nc.dram_tensor("kept_" + name, shape, dtype).ap()
    T["out"] = nc.dram_tensor("out_0", (TOKENS, D), F32, kind="ExternalOutput").ap()
    program(nc, T)
    r = run_bass_kernel_spmd(nc, [arrays], core_ids=[0])
    return r.results[0]["out_0"].reshape(B, N, D)
```

```python
from contextlib import ExitStack

import numpy as np

import concourse.bass as bass
from concourse import mybir

F32 = mybir.dt.float32
BF16 = mybir.dt.bfloat16
F16 = mybir.dt.float16
I32 = mybir.dt.int32
U32 = mybir.dt.uint32
ALU = mybir.AluOpType
ACT = mybir.ActivationFunctionType
AX = mybir.AxisListType
RMAX = bass.bass_isa.ReduceOp.max

B = 32
IMG, PATCH, CH = 224, 16, 3
GRID = IMG // PATCH
NIMG = GRID * GRID
NTXT = 77
N = NIMG + NTXT
D = 192
D2 = D - 128
HEADS, DH = 12, 16
F = 768
FT = F // 128
VOCAB = 8000
NCLS = 6
TOKENS = B * N
FEAT = PATCH * PATCH * 5 * CH
EPS = 1e-5
QMAX = 127.0
SCALE_FLOOR = 1e-8
ROUND = 1.5 * 2.0 ** 23

KP, KT = 120, 8
STEPS = 7
TILES = 7
IPT = 128 // B

TG = 4
TGROUPS = B // TG

NE = N + 1
SX, SW, SWP = 0, 1, 2
ISX, ISW, ISWP = 3, 4, 5
SXW, ISXW = 6, 7
SQKV, IQKV = 8, 11
AQKV = 14
ALPHA, IALPHA = 17, 18
SP_, LNSP, SO_IN = 19, 20, 21
SOUT, ISOUT, AOUT, HOUT = 22, 23, 24, 25
TMP = 26
SW1, SHID, SW2 = 29, 30, 31
UW1, UW2 = 32, 33
NSC = 40


def counts():
    pix = []
    for y in range(-1, PATCH + 1):
        for x in range(-1, PATCH + 1):
            src = []
            for dy, dx in ((0, 0), (0, 1), (0, -1), (1, 0), (-1, 0)):
                py, px = y + dy, x + dx
                ok = 0 <= py < PATCH and 0 <= px < PATCH
                src.append(py * PATCH + px if ok else -1)
            n = sum(s >= 0 for s in src)
            if n:
                pix.append((n, y, x, src))
    five = [p for p in pix if p[0] == 5]
    four = [p for p in pix if p[0] == 4]
    three = [p for p in pix if p[0] == 3]
    one = [p for p in pix if p[0] == 1]
    return five + three + four + one


class Mem:

    def __init__(self, nc, ctx, tag):
        self.nc, self.ctx, self.tag, self.sems = nc, ctx, tag, []
        ctx.callback(self.clear)

    def clear(self):
        if self.sems:
            self.nc.clear_and_free_semaphores(self.sems)
            self.nc.all_engine_barrier()

    def sb(self, name, shape, dt=F32):
        return self.ctx.enter_context(self.nc.sbuf_tensor(f"{self.tag}_{name}", shape, dt))

    def ps(self, name, shape, dt=F32):
        return self.ctx.enter_context(self.nc.psum_tensor(f"{self.tag}_{name}", shape, dt))

    def sem(self, name):
        self.sems.append(self.nc.alloc_semaphore(f"{self.tag}_{name}"))
        return self.sems[-1]


class Chain:

    def __init__(self, eng, sem):
        self.eng, self.sem, self.base, self.step, self.per, self.k = eng, sem, 0, None, 0, 0

    def loop(self, step, per):
        self.step, self.per, self.k, self.start = step, per, 0, self.base

    def end(self, count):
        assert self.k == self.per, (self.k, self.per)
        self.base, self.step, self.k = self.start + self.per * count, None, 0

    def __call__(self, ins):
        ins.then_inc(self.sem, 1)
        if self.step is None:
            self.base += 1
            self.eng.wait_ge(self.sem, self.base)
        else:
            self.k += 1
            self.eng.wait_ge(self.sem, self.step * self.per + (self.start + self.k))


def pool_copy(pool, out, src, one):
    while len(one.shape) < len(src.shape):
        one = one.unsqueeze(len(one.shape))
    return pool.tensor_tensor(out, src, one.to_broadcast(list(src.shape)), ALU.mult)


def image_phase(nc, T, C):
    LAG = TILES - 1
    with ExitStack() as ctx:
        m = Mem(nc, ctx, "im")
        wsh = m.sb("wsh", [KP, KT, 5, D])
        gsh = m.sb("gsh", [KP, KT, 5])
        bsh = m.sb("bsh", [KP, KT, 5])
        cntw = m.sb("cntw", [KP, KT])
        rootw = m.sb("rootw", [KP, KT])
        weff = m.sb("weff", [KP, KT, D + 1])
        brow = m.sb("brow", [128, D])
        gsum = m.sb("gsum", [128, D])
        bias = m.sb("bias", [128, D])
        ones = m.sb("ones", [KP, 128])
        xt = m.sb("xt", [KP, TILES, KT, 128])
        sq = m.sb("sq", [KP, TILES, KT, 128])
        sqs = m.sb("sqs", [KP, TILES, 128])
        u = m.sb("u", [128, TILES, D + 2])
        mean2 = m.sb("mean2", [128, TILES])
        var = m.sb("var", [128, TILES])
        rstd = m.sb("rstd", [128, TILES])
        nmean = m.sb("nmean", [128, TILES])
        z = m.sb("z", [128, TILES, D])
        h = m.sb("h", [128, TILES, D])
        bn = m.sb("bn", [128, TILES, 6])
        mv = m.sb("mv", [128, TILES, 2])
        hvar = m.sb("hvar", [128, TILES])
        hrstd = m.sb("hrstd", [128, TILES])
        y = m.sb("y", [128, TILES, D])
        ymx = m.sb("ymx", [128, 1])
        gap = m.sb("gap", [1, 1])
        psx = [m.ps(f"psx{i}", [128, 512]) for i in range(TILES)]
        psb = m.ps("psb", [128, 2, 256])

        w_loaded = m.sem("w_loaded")
        x_loaded = [m.sem(f"x_loaded{s}") for s in range(TILES)]
        taken = [m.sem(f"taken{s}") for s in range(TILES)]
        ones_set = m.sem("ones_set")
        weff_done = m.sem("weff_done")
        rows_done = m.sem("rows_done")
        bias_set = m.sem("bias_set")
        squared = m.sem("squared")
        sq_summed = m.sem("sq_summed")
        projected = m.sem("projected")
        var_done = m.sem("var_done")
        rstd_done = m.sem("rstd_done")
        u_used = m.sem("u_used")
        h_done = m.sem("h_done")
        hvar_done = m.sem("hvar_done")
        hrstd_done = m.sem("hrstd_done")
        y_done = m.sem("y_done")
        h_stored = m.sem("h_stored")
        y_stored = m.sem("y_stored")
        gathered = m.sem("gathered")
        vchain = m.sem("vchain")

        with nc.Block() as block:

            @block.sync
            def _(sp):
                sp.dma_start(gsh[:, :, :], T["gsh"]).then_inc(w_loaded, 16)
                sp.dma_start(bsh[:, :, :], T["bsh"]).then_inc(w_loaded, 16)
                sp.dma_start(cntw[:, :], T["cntw"]).then_inc(w_loaded, 16)
                sp.dma_start(rootw[:, :], T["rootw"]).then_inc(w_loaded, 16)
                sp.dma_start(wsh[:, :, :, :], T["wsh"]).then_inc(w_loaded, 16)
                sp.dma_start(brow[:, :], T["rows"][0, 0:D].partition_broadcast(128)).then_inc(w_loaded, 16)

                def load(it):
                    for s in range(TILES):
                        sp.wait_ge(taken[s], it)
                        sp.dma_start(xt[:, s, :, :], T["xcol"][bass.ts(it * TILES + s, KP), :]
                                     ).then_inc(x_loaded[s], 16)

                def store(it):
                    for t, name, done, stored in ((h, "H", h_done, h_stored), (y, "Y", y_done, y_stored)):
                        sp.wait_ge(done, it + 1)
                        sp.dma_start(T[name].rearrange("(b n) d -> b n d", b=B)[:, bass.ds(it * (TILES * IPT), TILES * IPT), :]
                                     .rearrange("b (i s) d -> b i (s d)", i=IPT),
                                     t[:, :, :].rearrange("p s d -> p (s d)")).then_inc(stored, 16)

                load(0)
                with sp.Fori(0, STEPS - 1) as it:
                    load(it + 1)
                    store(it)
                store(STEPS - 1)
                sp.wait_ge(h_stored, 16 * STEPS)
                sp.wait_ge(y_stored, 16 * STEPS)

            @block.gpsimd
            def _(pool):
                pool.memset(ones[:, :], 1.0).then_inc(ones_set, 1)
                for b in range(B):
                    pool.indirect_dma_start(out=C["emb"][:, b, :], out_offset=None, in_=T["emb"],
                                            in_offset=bass.IndirectOffsetOnAxis(ap=C["idx"][:, b:b + 1], axis=0)
                                            ).then_inc(gathered, 16)
                with pool.Fori(0, STEPS) as it:
                    pool.wait_ge(var_done, it + 1)
                    pool.tensor_tensor(rstd[:, :], var[:, :], C["nhalf"][:, 0:TILES], ALU.pow).then_inc(rstd_done, 1)
                    pool.wait_ge(hvar_done, it + 1)
                    pool.tensor_tensor(hrstd[:, :], hvar[:, :], C["nhalf"][:, 0:TILES], ALU.pow).then_inc(hrstd_done, 1)
                pool.wait_ge(gathered, 16 * B)

            @block.scalar
            def _(act):
                act.preload_act_table(ACT.Square)
                act.wait_ge(w_loaded, 96)
                r5, r4, r1 = (float(np.sqrt(k / FEAT)) for k in (5.0, 4.0, 1.0))
                with act.Fori(0, STEPS) as it:

                    def take(s):
                        act.wait_ge(projected, it * TILES + (s + 1))
                        if s == 0:
                            act.wait_ge(u_used, it)
                        act.activation(u[:, s, :], psx[s][:, 0:D + 2], ACT.Copy).then_inc(taken[s], 1)

                    for s in range(TILES):
                        act.wait_ge(x_loaded[s], it * 16 + 16)
                        if s == 0:
                            act.wait_ge(sq_summed, it * TILES)
                        act.activation(sq[:, s, 0:4, :], xt[:, s, 0:4, :], ACT.Square, scale=r5)
                        act.activation(sq[:, s, 4, :], xt[:, s, 4, :], ACT.Square, scale=rootw[:, 4:5])
                        act.activation(sq[:, s, 5, :], xt[:, s, 5, :], ACT.Square, scale=r4)
                        act.activation(sq[:, s, 6, :], xt[:, s, 6, :], ACT.Square, scale=rootw[:, 6:7])
                        act.activation(sq[:, s, 7, :], xt[:, s, 7, :], ACT.Square, scale=r1).then_inc(squared, 1)
                        if s >= LAG:
                            take(s - LAG)
                    for s in range(TILES - LAG, TILES):
                        take(s)

            @block.tensor
            def _(pe):
                pe.wait_ge(ones_set, 1)
                pe.wait_ge(w_loaded, 96)
                for k in range(KT):
                    for s in range(5):
                        pe.matmul(psb[:, 1, 0:D], bsh[:, k, s:s + 1].to_broadcast([KP, 128]), wsh[:, k, s, :],
                                  start=(k == 0 and s == 0), stop=(k == KT - 1 and s == 4), skip_group_check=True)
                for k in range(KT):
                    pe.wait_ge(weff_done, k + 1)
                    last = pe.matmul(psx[0][:, 0:D], ones[:, :], weff[:, k, 0:D], start=(k == 0), stop=(k == KT - 1))
                last.then_inc(rows_done, 1)
                pe.wait_ge(bias_set, 2)
                with pe.Fori(0, STEPS) as it:

                    def mean_square(s):
                        pe.wait_ge(sq_summed, it * TILES + (s + 1))
                        pe.matmul(psx[s][:, D + 1:D + 2], sqs[:, s, :], ones[:, 0:1], start=False, stop=True,
                                  skip_group_check=True).then_inc(projected, 1)

                    for s in range(TILES):
                        pe.wait_ge(x_loaded[s], it * 16 + 16)
                        pe.wait_ge(taken[s], it)
                        for k in range(KT):
                            pe.matmul(psx[s][:, 0:D + 1], xt[:, s, k, :], weff[:, k, :], start=(k == 0), stop=(k == KT - 1))
                        if s >= LAG:
                            mean_square(s - LAG)
                    for s in range(TILES - LAG, TILES):
                        mean_square(s)

            @block.vector
            def _(v):
                chain = Chain(v, vchain)
                v.wait_ge(w_loaded, 96)
                chain(v.tensor_copy(weff[:, :, D:D + 1], cntw[:, :].unsqueeze(2)))
                for k in range(KT):
                    ins = v.tensor_scalar(weff[:, k, 0:D], wsh[:, k, 0, :], gsh[:, k, 0:1], None, ALU.mult)
                    for s in range(1, 5):
                        chain(ins)
                        ins = v.scalar_tensor_tensor(out=weff[:, k, 0:D], in0=wsh[:, k, s, :], scalar=gsh[:, k, s:s + 1],
                                                     in1=weff[:, k, 0:D], op0=ALU.mult, op1=ALU.add)
                    ins.then_inc(weff_done, 1)
                v.wait_ge(rows_done, 1)
                v.tensor_copy(gsum[:, :], psx[0][:, 0:D]).then_inc(bias_set, 1)
                v.tensor_tensor(bias[:, :], psb[:, 1, 0:D], brow[:, :], ALU.add).then_inc(bias_set, 1)
                chain(v.memset(C["ymax_img"][:, :], 0.0))
                v.wait_ge(bias_set, 2)
                with v.Fori(0, STEPS) as it:
                    chain.loop(it, 6)
                    for s in range(TILES):
                        v.wait_ge(squared, it * TILES + (s + 1))
                        v.tensor_reduce(sqs[:, s, :], sq[:, s, :, :].rearrange("p k n -> p n k"), AX.X, ALU.add
                                        ).then_inc(sq_summed, 1)
                    for s in range(TILES):
                        v.wait_ge(taken[s], it + 1)
                    v.tensor_scalar(nmean[:, :], u[:, :, D], -1.0, None, ALU.mult)
                    chain(v.tensor_tensor(mean2[:, :], u[:, :, D], u[:, :, D], ALU.mult))
                    chain(v.tensor_tensor(var[:, :], u[:, :, D + 1], mean2[:, :], ALU.subtract))
                    v.tensor_scalar(var[:, :], var[:, :], 0.0, EPS, ALU.max, ALU.add).then_inc(var_done, 1)
                    for s in range(TILES):
                        ins = v.scalar_tensor_tensor(out=z[:, s, :], in0=gsum[:, :], scalar=nmean[:, s:s + 1],
                                                     in1=u[:, s, 0:D], op0=ALU.mult, op1=ALU.add)
                    ins.then_inc(u_used, 1)
                    v.wait_ge(u_used, it + 1)
                    v.wait_ge(rstd_done, it + 1)
                    v.wait_ge(h_stored, it * 16)
                    for s in range(TILES):
                        ins = v.scalar_tensor_tensor(out=h[:, s, :], in0=z[:, s, :], scalar=rstd[:, s:s + 1],
                                                     in1=bias[:, :], op0=ALU.mult, op1=ALU.add)
                    ins.then_inc(h_done, 1)
                    v.wait_ge(h_done, it + 1)
                    for s in range(TILES):
                        ins = v.bn_stats(bn[:, s, :], h[:, s, :])
                    chain(ins)
                    v.memset(gap[:, :], 0.0)
                    for s in range(TILES):
                        ins = v.bn_aggr(mv[:, s, :], bn[:, s, :])
                    chain(ins)
                    v.tensor_scalar(hvar[:, :], mv[:, :, 1], EPS, None, ALU.add).then_inc(hvar_done, 1)
                    v.wait_ge(hrstd_done, it + 1)
                    v.wait_ge(y_stored, it * 16)
                    for s in range(TILES):
                        ins = v.tensor_scalar(y[:, s, :], h[:, s, :], mv[:, s, 0:1], hrstd[:, s:s + 1],
                                              ALU.subtract, ALU.mult)
                    ins.then_inc(y_done, 1)
                    v.wait_ge(y_done, it + 1)
                    chain(v.tensor_reduce(ymx[:, :], y[:, :, :].rearrange("p s d -> p (s d)"), AX.X, ALU.max, apply_absolute_value=True))
                    chain(v.tensor_tensor(C["ymax_img"][:, :], C["ymax_img"][:, :], ymx[:, :], ALU.max))
                chain.end(STEPS)


def text_phase(nc, T, C):
    W = TG * NTXT
    U = 2 * 3
    SCALE = float(DH) ** -0.5
    with ExitStack() as ctx:
        m = Mem(nc, ctx, "tx")
        wqk = m.sb("wqk", [128, 2, 2, 384])
        bqk = m.sb("bqk", [128, 6])
        wv = m.sb("wv", [128, 2, D])
        wo = m.sb("wo", [128, 2, D])
        w1 = m.sb("w1", [128, 2, F])
        b1 = m.sb("b1", [128, FT])
        w2 = m.sb("w2", [128, FT, D])
        rows = m.sb("rows", [NTXT, 8, D])
        bv, bo, gam1, bet1, b2, gam2, bet2 = (rows[:, i, :] for i in range(1, 8))
        pos = m.sb("pos", [NTXT, D])
        xg = m.sb("xg", [NTXT, TG, D])
        xbo = m.sb("xbo", [NTXT, TG, D])
        xT = m.sb("xT", [128, 2, W])
        qT = m.sb("qT", [128, 3, W])
        kT = m.sb("kT", [128, 4, 3, W])
        v = m.sb("v", [NTXT, TG, D])
        mx = m.sb("mx", [NTXT, 2, 4, U])
        e = m.sb("e", [NTXT, 2, 4, U, NTXT])
        zs = m.sb("zs", [NTXT, 2, 4, U])
        rz = m.sb("rz", [NTXT, 2, 4, U])
        pT = m.sb("pT", [NTXT, 2, 4, U * NTXT])
        attn = m.sb("attn", [NTXT, TG, D])
        aT = m.sb("aT", [128, 2, W])
        r1 = m.sb("r1", [NTXT, TG, D])
        r2 = m.sb("r2", [NTXT, TG, D])
        bn = m.sb("bn", [NTXT, TG, 6])
        mv = m.sb("mv", [NTXT, TG, 2])
        std = m.sb("std", [NTXT, TG])
        dn = m.sb("dn", [NTXT, TG])
        rs = m.sb("rs", [NTXT, TG])
        h1n = m.sb("h1n", [NTXT, TG, D])
        h1 = m.sb("h1", [NTXT, TG, D])
        h1T = m.sb("h1T", [128, 2, W])
        fT = m.sb("fT", [128, FT, W])
        ho = m.sb("ho", [NTXT, TG, D])
        yo = m.sb("yo", [NTXT, TG, D])
        ymx = m.sb("ymx", [NTXT, 1])
        gap = m.sb("gap", [1, 1])
        ps = m.ps("ps", [128, 8, 512])

        w_loaded = m.sem("w_loaded")
        kT_zeroed = m.sem("kT_zeroed")
        x_ready = m.sem("x_ready")
        xbo_ready = m.sem("xbo_ready")
        x_turned = m.sem("x_turned")
        xT_ready = m.sem("xT_ready")
        ring_mm = m.sem("ring_mm")
        ring_taken = m.sem("ring_taken")
        v_mm = m.sem("v_mm")
        v_ready = m.sem("v_ready")
        s_mm = m.sem("s_mm")
        s_less_max = m.sem("s_less_max")
        exp_done = m.sem("exp_done")
        p_turned = m.sem("p_turned")
        pT_ready = m.sem("pT_ready")
        pv_mm = m.sem("pv_mm")
        attn_ready = m.sem("attn_ready")
        a_turned = m.sem("a_turned")
        aT_ready = m.sem("aT_ready")
        wo_mm = m.sem("wo_mm")
        var_ready = m.sem("var_ready")
        std_ready = m.sem("std_ready")
        h1_ready = m.sem("h1_ready")
        h1_turned = m.sem("h1_turned")
        h1T_ready = m.sem("h1T_ready")
        f2_mm = m.sem("f2_mm")
        f2_used = m.sem("f2_used")
        h_ready = m.sem("h_ready")
        y_ready = m.sem("y_ready")
        h_stored = m.sem("h_stored")
        y_stored = m.sem("y_stored")
        vchain = m.sem("vchain")
        NLOAD = 9

        with nc.Block() as block:

            @block.sync
            def _(sp):
                for t, name in ((wqk, "wqk"), (wv, "wv"), (wo, "wo"), (w1, "w1")):
                    sp.dma_start(t[:, :, :, :] if len(t.shape) == 4 else t[:, :, :], T[name]).then_inc(w_loaded, 16)
                sp.dma_start(bqk[:, :], T["bqk"]).then_inc(w_loaded, 16)
                sp.dma_start(b1[:, :], T["b1"]).then_inc(w_loaded, 16)
                sp.dma_start(w2[:, :, :], T["w2"].rearrange("(k p) d -> p k d", p=128)).then_inc(w_loaded, 16)
                sp.dma_start(rows[:, :, :].rearrange("p r d -> p (r d)"),
                             T["rows"][0, 0:8 * D].partition_broadcast(NTXT)).then_inc(w_loaded, 16)
                sp.dma_start(pos[:, :], T["pos"]).then_inc(w_loaded, 16)
                with sp.Fori(0, TGROUPS) as it:
                    for b in range(TG):
                        h_out = T["H"].rearrange("(b n) d -> b n d", b=B)[bass.ds(it * TG + b, 1), NIMG:N, :]
                        if b == 0:
                            sp.wait_ge(h_ready, it + 1)
                        sp.dma_start(h_out.rearrange("o n d -> (o n) d"), ho[:, b, :]).then_inc(h_stored, 16)
                    for b in range(TG):
                        y_out = T["Y"].rearrange("(b n) d -> b n d", b=B)[bass.ds(it * TG + b, 1), NIMG:N, :]
                        if b == 0:
                            sp.wait_ge(y_ready, it + 1)
                        sp.dma_start(y_out.rearrange("o n d -> (o n) d"), yo[:, b, :]).then_inc(y_stored, 16)
                sp.wait_ge(h_stored, 16 * B)
                sp.wait_ge(y_stored, 16 * B)

            @block.gpsimd
            def _(pool):
                pool.memset(kT[:, :, :, :], 0.0).then_inc(kT_zeroed, 1)
                pool.wait_ge(w_loaded, 16 * NLOAD)

                def with_bo(n):
                    pool.wait_ge(x_ready, n + 1)
                    pool.tensor_tensor(xbo[:, :, :], xg[:, :, :], bo.unsqueeze(1).to_broadcast([NTXT, TG, D]), ALU.add
                                       ).then_inc(xbo_ready, 1)

                def deviation(count):
                    pool.wait_ge(var_ready, count)
                    pool.tensor_tensor(std[:, :], mv[:, :, 1], C["half"][0:NTXT, 0:TG], ALU.pow).then_inc(std_ready, 1)

                def feed_forward(count):
                    deviation(count)
                    pool.wait_ge(var_ready, count + 1)
                    pool.tensor_tensor(rs[:, :], dn[:, :], C["nhalf"][0:NTXT, 0:TG], ALU.pow).then_inc(std_ready, 1)

                with_bo(0)
                deviation(1)
                with_bo(1)
                with pool.Fori(0, TGROUPS - 2) as g:
                    deviation(g * 3 + 2)
                    with_bo(g + 2)
                    feed_forward(g * 3 + 3)
                deviation(TGROUPS * 3 - 4)
                feed_forward(TGROUPS * 3 - 3)
                feed_forward(TGROUPS * 3 - 1)

            @block.scalar
            def _(act):
                act.preload_act_table(ACT.Exp)
                act.wait_ge(w_loaded, 16 * NLOAD)
                act.wait_ge(kT_zeroed, 1)

                def take_turned(first, done, ready, dst, count):
                    act.wait_ge(done, count)
                    act.activation(dst[:, 0, :], ps[:, first, 0:W], ACT.Copy)
                    act.activation(dst[0:D2, 1, :], ps[0:D2, first + 1, 0:W], ACT.Copy).then_inc(ready, 1)

                def take_qk(base, first):
                    for k in range(6):
                        act.wait_ge(ring_mm, base + (k + 1))
                        bank = 4 + (first + k) % 4
                        if k < 3:
                            ins = act.activation(qT[:, k, :], ps[:, bank, 0:W], ACT.Identity, bias=bqk[:, k:k + 1])
                        else:
                            for j in range(4):
                                r = slice(32 * j, 32 * j + 32)
                                ins = act.activation(kT[r, j, k - 3, :], ps[r, bank, 0:W], ACT.Identity, bias=bqk[r, k:k + 1])
                        ins.then_inc(ring_taken, 1)

                def take_hidden(g):
                    take_turned(0, h1_turned, h1T_ready, h1T, g + 1)

                def relu(base, first):
                    for k in range(FT):
                        act.wait_ge(ring_mm, base + (k + 1))
                        act.activation(fT[:, k, :], ps[:, 4 + (first + k) % 4, 0:W], ACT.Relu, bias=b1[:, k:k + 1]
                                       ).then_inc(ring_taken, 1)

                def attention(n):
                    for un in range(2):
                        act.wait_ge(s_less_max, n * 2 + (un + 1))
                        act.activation(e[:, un, :, :, :], e[:, un, :, :, :], ACT.Exp, scale=SCALE).then_inc(exp_done, 1)
                    for un in range(2):
                        act.wait_ge(p_turned, n * 2 + (un + 1))
                        first = 4 - 4 * un
                        act.activation(pT[:, un, :, :], ps[0:NTXT, first:first + 4, 0:U * NTXT], ACT.Copy).then_inc(pT_ready, 1)
                    take_turned(2, a_turned, aT_ready, aT, n + 1)

                take_turned(2, x_turned, xT_ready, xT, 1)
                take_qk(0, 0)
                attention(0)
                with act.Fori(0, TGROUPS - 1) as g:
                    take_turned(2, x_turned, xT_ready, xT, g + 2)
                    take_qk(g * 12 + 6, 6)
                    take_hidden(g)
                    relu(g * 12 + 12, 12)
                    attention(g + 1)
                take_hidden(TGROUPS - 1)
                relu(TGROUPS * 12 - 6, 6)

            @block.tensor
            def _(pe):
                ident = C["ident"]
                pe.wait_ge(w_loaded, 16 * NLOAD)

                def turn(src, first, done):
                    for k in range(2):
                        K = (128, D2)[k]
                        for b in range(TG):
                            last = pe.transpose(ps[0:K, first + k, b * NTXT:(b + 1) * NTXT], src[:, b, 128 * k:128 * k + K],
                                                ident[0:NTXT, 0:NTXT])
                    last.then_inc(done, 1)

                def project(srcT, w, bank, b):
                    for k in range(2):
                        K = (128, D2)[k]
                        ins = pe.matmul(ps[0:NTXT, bank, (b % 2) * D:(b % 2) * D + D], srcT[0:K, k, b * NTXT:(b + 1) * NTXT],
                                        w[0:K, k, :], start=(k == 0), stop=(k == 1), skip_group_check=True)
                    return ins

                def ring_tile(weights, src, base, k, first):
                    if not (isinstance(base, int) and base == 0 and k < 4):
                        pe.wait_ge(ring_taken, base + (k - 3))
                    for half in range(2):
                        K = (128, D2)[half]
                        last = pe.matmul(ps[:, 4 + (first + k) % 4, 0:W], weights[half], src[0:K, half, :],
                                         start=(half == 0), stop=(half == 1))
                    last.then_inc(ring_mm, 1)

                def turn_hidden(g):
                    pe.wait_ge(h1_ready, g + 1)
                    turn(h1, 0, h1_turned)

                def hidden(g, base, first):
                    pe.wait_ge(h1T_ready, g + 1)
                    for f in range(FT):
                        ring_tile([w1[0:(128, D2)[h], h, f * 128:(f + 1) * 128] for h in range(2)], h1T, base, f, first)

                def second(taken):
                    pe.wait_ge(ring_taken, taken)
                    for b in range(TG):
                        for k in range(FT):
                            last = pe.matmul(ps[0:NTXT, b // 2, (b % 2) * D:(b % 2) * D + D],
                                             fT[:, k, b * NTXT:(b + 1) * NTXT], w2[:, k, :],
                                             start=(k == 0), stop=(k == FT - 1), skip_group_check=True)
                    last.then_inc(f2_mm, 1)

                def turn_x(n):
                    pe.wait_ge(x_ready, n + 1)
                    turn(xg, 2, x_turned)

                def qkv(n, base, first):
                    pe.wait_ge(xT_ready, n + 1)
                    for t in range(6):
                        c = (t % 3) * 128
                        ring_tile([wqk[0:(128, D2)[h], h, t // 3, c:c + 128] for h in range(2)], xT, base, t, first)
                    for b in range(TG):
                        last = project(xT, wv, 2 + b // 2, b)
                    last.then_inc(v_mm, 1)

                def scores(n, taken):
                    pe.wait_ge(ring_taken, taken)
                    pe.wait_ge(v_ready, n + 1)
                    for un in range(2):
                        for j in range(4):
                            for b in range(2):
                                at = (2 * un + b) * NTXT
                                for g in range(3):
                                    c = (b * 3 + g) * NTXT
                                    last = pe.matmul(ps[0:NTXT, 4 * un + j, c:c + NTXT],
                                                     qT[:, g, at:at + NTXT], kT[:, j, g, at:at + NTXT],
                                                     start=True, stop=True, skip_group_check=True)
                        last.then_inc(s_mm, 1)

                def attention(n):
                    for un in range(2):
                        pe.wait_ge(exp_done, n * 2 + (un + 1))
                        if un == 0:
                            pe.wait_ge(s_less_max, n * 2 + 2)
                        elif not (isinstance(n, int) and n == 0):
                            pe.wait_ge(f2_used, n)
                        for j in range(4):
                            for c in range(U):
                                last = pe.transpose(ps[0:NTXT, 4 - 4 * un + j, c * NTXT:(c + 1) * NTXT], e[:, un, j, c, :],
                                                    ident[0:NTXT, 0:NTXT])
                        last.then_inc(p_turned, 1)
                    for un in range(2):
                        pe.wait_ge(pT_ready, n * 2 + (un + 1))
                        for b in range(2):
                            for h in range(HEADS):
                                c = (b * 3 + h // 4) * NTXT
                                last = pe.matmul(ps[0:NTXT, 4 - 4 * un, b * D + h * DH:b * D + (h + 1) * DH],
                                                 pT[:, un, h % 4, c:c + NTXT], v[:, 2 * un + b, h * DH:(h + 1) * DH],
                                                 start=True, stop=True, skip_group_check=True)
                        last.then_inc(pv_mm, 1)
                    pe.wait_ge(attn_ready, n * 2 + 2)
                    turn(attn, 2, a_turned)
                    pe.wait_ge(aT_ready, n + 1)
                    for b in range(TG):
                        last = project(aT, wo, b // 2, b)
                    last.then_inc(wo_mm, 1)

                turn_x(0)
                qkv(0, 0, 0)
                scores(0, 6)
                attention(0)
                with pe.Fori(0, TGROUPS - 1) as g:
                    turn_x(g + 1)
                    qkv(g + 1, g * 12 + 6, 6)
                    turn_hidden(g)
                    hidden(g, g * 12 + 12, 12)
                    scores(g + 1, g * 12 + 18)
                    pe.wait_ge(s_less_max, g * 2 + 3)
                    second(g * 12 + 18)
                    attention(g + 1)
                turn_hidden(TGROUPS - 1)
                hidden(TGROUPS - 1, TGROUPS * 12 - 6, 6)
                second(TGROUPS * 12)

            @block.vector
            def _(ve):
                chain = Chain(ve, vchain)
                wide = lambda r: r.unsqueeze(1).to_broadcast([NTXT, TG, D])
                chain(ve.memset(C["ymax_txt"][:, :], 0.0))
                ve.wait_ge(w_loaded, 16 * NLOAD)

                def stats(src):
                    for b in range(TG):
                        ins = ve.bn_stats(bn[:, b, :], src[:, b, :])
                    chain(ins)
                    ve.memset(gap[:, :], 0.0)
                    for b in range(TG):
                        ins = ve.bn_aggr(mv[:, b, :], bn[:, b, :])
                    return ins

                def layer_norm(src, count, gam, bet, norm, out):
                    stats(src).then_inc(var_ready, 1)
                    ve.wait_ge(std_ready, count)
                    chain(ve.tensor_scalar(dn[:, :], std[:, :], EPS, None, ALU.add))
                    chain(ve.reciprocal(rs[:, :], dn[:, :]))
                    for b in range(TG):
                        ins = ve.tensor_scalar(norm[:, b, :], src[:, b, :], mv[:, b, 0:1], rs[:, b:b + 1],
                                               ALU.subtract, ALU.mult)
                    chain(ins)
                    chain(ve.tensor_tensor(norm[:, :, :], norm[:, :, :], wide(gam), ALU.mult))
                    return ve.tensor_tensor(out[:, :, :], norm[:, :, :], wide(bet), ALU.add)

                def from_banks(first, add, out):
                    for k in range(2):
                        ins = ve.tensor_tensor(out[:, 2 * k:2 * k + 2, :],
                                               ps[0:NTXT, first + k, 0:2 * D].rearrange("p (b d) -> p b d", b=2),
                                               add(k), ALU.add)
                    return ins

                row = lambda r: lambda k: r.unsqueeze(1).to_broadcast([NTXT, 2, D])

                def embed(n):
                    ve.tensor_tensor(xg[:, :, :], C["emb"][:, bass.ds(n * TG, TG), :], wide(pos[:, :]), ALU.add
                                     ).then_inc(x_ready, 1)

                def scores(n):
                    ve.wait_ge(v_mm, n + 1)
                    from_banks(2, row(bv), v).then_inc(v_ready, 1)
                    for un in range(2):
                        s = ps[0:NTXT, 4 * un:4 * un + 4, 0:U * NTXT].rearrange("p j (c k) -> p j c k", c=U)
                        ve.wait_ge(s_mm, n * 2 + (un + 1))
                        chain(ve.tensor_reduce(mx[:, un, :, :], s, AX.X, ALU.max))
                        for j in range(4):
                            ins = ve.tensor_tensor(e[:, un, j, :, :], s[:, j, :, :],
                                                   mx[:, un, j, :].unsqueeze(2).to_broadcast([NTXT, U, NTXT]), ALU.subtract)
                        ins.then_inc(s_less_max, 1)

                def sums(n):
                    for un in range(2):
                        ve.wait_ge(exp_done, n * 2 + (un + 1))
                        chain(ve.tensor_reduce(zs[:, un, :, :], e[:, un, :, :, :], AX.X, ALU.add))
                        chain(ve.reciprocal(rz[:, un, :, :], zs[:, un, :, :]))

                def attention(n, count, last):
                    for un in range(2):
                        ve.wait_ge(pv_mm, n * 2 + (un + 1))
                        for b in range(2):
                            r = rz[:, un, :, 3 * b:3 * b + 3].rearrange("p j g -> p g j").unsqueeze(3)
                            ins = ve.tensor_tensor(attn[:, 2 * un + b, :].rearrange("p (g j d) -> p g j d", g=3, j=4),
                                                   ps[0:NTXT, 4 - 4 * un, b * D:(b + 1) * D].rearrange("p (g j d) -> p g j d", g=3, j=4),
                                                   r.to_broadcast([NTXT, 3, 4, DH]), ALU.mult)
                        ins.then_inc(attn_ready, 1)
                    ve.wait_ge(xbo_ready, n + 1)
                    if not last:
                        embed(n + 1)
                    ve.wait_ge(wo_mm, n + 1)
                    chain(from_banks(0, lambda k: xbo[:, 2 * k:2 * k + 2, :], r1))
                    layer_norm(r1, count, gam1, bet1, h1n, h1).then_inc(h1_ready, 1)
                    ve.wait_ge(h1_ready, n + 1)

                def take_second(g):
                    ve.wait_ge(f2_mm, g + 1)
                    from_banks(0, row(b2), r2).then_inc(f2_used, 1)
                    ve.wait_ge(f2_used, g + 1)
                    chain(ve.tensor_tensor(r2[:, :, :], r2[:, :, :], h1[:, :, :], ALU.add))

                def output(g, count):
                    ve.wait_ge(h_stored, g * (16 * TG))
                    layer_norm(r2, count, gam2, bet2, h1n, ho).then_inc(h_ready, 1)
                    ve.wait_ge(h_ready, g + 1)
                    chain(stats(ho))
                    ve.tensor_scalar(dn[:, :], mv[:, :, 1], EPS, None, ALU.add).then_inc(var_ready, 1)
                    ve.wait_ge(std_ready, count + 1)
                    ve.wait_ge(y_stored, g * (16 * TG))
                    for b in range(TG):
                        ins = ve.tensor_scalar(yo[:, b, :], ho[:, b, :], mv[:, b, 0:1], rs[:, b:b + 1],
                                               ALU.subtract, ALU.mult)
                    ins.then_inc(y_ready, 1)
                    ve.wait_ge(y_ready, g + 1)
                    chain(ve.tensor_reduce(ymx[:, :], yo[:, :, :], AX.XY, ALU.max, apply_absolute_value=True))
                    chain(ve.tensor_tensor(C["ymax_txt"][0:NTXT, :], C["ymax_txt"][0:NTXT, :], ymx[:, :], ALU.max))

                def step(g, last):
                    scores(g + 1)
                    sums(g + 1)
                    take_second(g)
                    attention(g + 1, g * 3 + 2, last)
                    output(g, g * 3 + 3)

                embed(0)
                scores(0)
                sums(0)
                attention(0, 1, False)
                with ve.Fori(0, TGROUPS - 2) as g:
                    chain.loop(g, 22)
                    step(g, False)
                chain.end(TGROUPS - 2)
                step(TGROUPS - 2, True)
                take_second(TGROUPS - 1)
                output(TGROUPS - 1, TGROUPS * 3 - 1)


def scales(nc, T, C):
    sc, wint, wqk, wpi = C["sc"], C["wint"], C["wqkp"], C["wpint"]
    with ExitStack() as ctx:
        m = Mem(nc, ctx, "qs")
        wf = m.sb("wf", [128, 2, 3 * D])
        wpf = m.sb("wpf", [128, 2, D])
        big = m.sb("big", [128, 2, 3 * D])
        bigp = m.sb("bigp", [128, 2, D])
        brow = m.sb("brow", [1, 3 * D])
        rest = m.sb("rest", [1, 2, 3 * D])
        parts = m.sb("parts", [1, 3, 3 * D], BF16)
        mx = m.sb("mx", [128, 3])
        gx = m.sb("gx", [128, 3])
        loaded = m.sem("loaded")
        mx_ready = m.sem("mx_ready")
        gx_ready = m.sem("gx_ready")
        parts_ready = m.sem("parts_ready")
        parts_placed = m.sem("parts_placed")
        zeroed = m.sem("zeroed")
        vchain = m.sem("vchain")
        with nc.Block() as block:

            @block.sync
            def _(sp):
                sp.dma_start(wf[:, :, :], T["wqkv"]).then_inc(loaded, 16)
                sp.dma_start(wpf[:, :, :], T["wproj"]).then_inc(loaded, 16)
                sp.dma_start(brow[:, :], T["bqkv"]).then_inc(loaded, 16)
                sp.wait_ge(parts_ready, 1)
                sp.dma_start(wint[D2:D2 + 3, 1, :], parts[:, :, :].rearrange("o r n -> o (r n)")).then_inc(parts_placed, 16)
                sp.wait_ge(parts_placed, 16)

            @block.gpsimd
            def _(pool):
                pool.memset(wqk[:, :, :, :], 0.0).then_inc(zeroed, 1)
                pool.wait_ge(mx_ready, 1)
                pool.partition_all_reduce(gx[:, :], mx[:, :], 128, RMAX).then_inc(gx_ready, 1)

            @block.vector
            def _(v):
                chain = Chain(v, vchain)
                v.wait_ge(loaded, 48)
                v.tensor_tensor(mx[:, 0:1], C["ymax_img"][:, :], C["ymax_txt"][:, :], ALU.max)
                v.tensor_reduce(mx[:, 1:2], wf[:, :, :], AX.XY, ALU.max, apply_absolute_value=True)
                v.tensor_reduce(mx[:, 2:3], wpf[:, :, :], AX.XY, ALU.max, apply_absolute_value=True).then_inc(mx_ready, 1)
                v.wait_ge(gx_ready, 1)
                chain(v.tensor_scalar(sc[:, SX:SX + 3], gx[:, :], 1.0 / QMAX, SCALE_FLOOR, ALU.mult, ALU.max))
                chain(v.reciprocal(sc[:, ISX:ISX + 3], sc[:, SX:SX + 3]))
                v.tensor_tensor(sc[:, SXW:SXW + 1], sc[:, SX:SX + 1], sc[:, SX + 1:SX + 2], ALU.mult)
                v.tensor_scalar(big[:, :, :], wf[:, :, :], sc[:, ISX + 1:ISX + 2], ROUND, ALU.mult, ALU.add)
                v.tensor_scalar(bigp[:, :, :], wpf[:, :, :], sc[:, ISX + 2:ISX + 3], ROUND, ALU.mult, ALU.add)
                chain(v.tensor_tensor(sc[:, ISXW:ISXW + 1], sc[:, ISX:ISX + 1], sc[:, ISX + 1:ISX + 2], ALU.mult))
                v.tensor_scalar(wint[:, :, :], big[:, :, :], ROUND, None, ALU.subtract)
                v.tensor_scalar(wpi[:, :, :], bigp[:, :, :], ROUND, None, ALU.subtract)
                chain(v.tensor_scalar(rest[:, 0, :], brow[:, :], sc[0:1, ISXW:ISXW + 1], None, ALU.mult))
                chain(v.tensor_copy(parts[:, 0, :], rest[:, 0, :]))
                chain(v.tensor_tensor(rest[:, 1, :], rest[:, 0, :], parts[:, 0, :], ALU.subtract))
                chain(v.tensor_copy(parts[:, 1, :], rest[:, 1, :]))
                v.tensor_tensor(parts[:, 2, :], rest[:, 1, :], parts[:, 1, :], ALU.subtract).then_inc(parts_ready, 1)
                v.wait_ge(parts_placed, 16)
                v.wait_ge(zeroed, 1)
                chain(v.tensor_copy(wqk[:, :, :, 0:DH], wint[:, :, 0:2 * D].rearrange("p k (h d) -> p k h d", d=DH)))


def quantize_phase(nc, T, C):
    NT = N // 3
    PAD = NT + 1
    sc, wint = C["sc"], C["wint"]
    with ExitStack() as ctx:
        m = Mem(nc, ctx, "qz")
        yt = m.sb("yt", [NT, 2, 3, D])
        big = m.sb("big", [NT, 2, 3, D])
        yq = m.sb("yq", [NT, 2, 3, D], BF16)
        yT = m.sb("yT", [128, 2, 2, NE], BF16)
        tile_max = m.sb("tile_max", [NT, 6, 3])
        run_max = m.sb("run_max", [NT, 6, 3])
        pt = [m.ps(f"pt{s}", [128, 2, 3, PAD], BF16) for s in range(2)]
        pj = m.ps("pj", [128, 6, 512])
        y_loaded = [m.sem(f"y_loaded{s}") for s in range(2)]
        yq_ready = [m.sem(f"yq_ready{s}") for s in range(2)]
        turned = [m.sem(f"turned{s}") for s in range(2)]
        yT_ready = [m.sem(f"yT_ready{s}") for s in range(2)]
        rounded = [m.sem(f"rounded{s}") for s in range(2)]
        stored = [m.sem(f"stored{s}") for s in range(2)]
        product = m.sem("product")
        reduced = m.sem("reduced")
        ones_set = m.sem("ones_set")
        vchain = m.sem("vchain")
        with nc.Block() as block:

            @block.sync
            def _(sp):

                def load(it, s):
                    sp.wait_ge(yq_ready[s], it)
                    sp.dma_start(yt[:, s, :, :].rearrange("p i d -> p (i d)"),
                                 T["Y"].rearrange("(r i) d -> r (i d)", i=3)[bass.ts(it * 2 + s, NT), :]
                                 ).then_inc(y_loaded[s], 16)

                def store(it, s):
                    sp.wait_ge(yT_ready[s], it + 1)
                    sp.dma_start(T["YQ"][bass.ds((it * 2 + s) * D, 128), :], yT[:, s, 0, :]).then_inc(stored[s], 16)
                    sp.dma_start(T["YQ"][bass.ds((it * 2 + s) * D + 128, D2), :], yT[0:D2, s, 1, :]).then_inc(stored[s], 16)

                for s in range(2):
                    load(0, s)
                with sp.Fori(0, B // 2 - 1) as it:
                    for s in range(2):
                        load(it + 1, s)
                    for s in range(2):
                        store(it, s)
                for s in range(2):
                    store(B // 2 - 1, s)
                for s in range(2):
                    sp.wait_ge(stored[s], 16 * B)

            @block.vector
            def _(v):
                chain = Chain(v, vchain)
                v.memset(run_max[:, :, :], 0.0)
                v.memset(yT[:, :, :, :], 0.0)
                chain(v.memset(C["qkvmax"][:, :], 0.0))
                v.memset(yT[D2:D2 + 3, :, 1, :], 1.0).then_inc(ones_set, 1)

                def quantize(it, s):
                    v.wait_ge(y_loaded[s], it * 16 + 16)
                    v.tensor_scalar(big[:, s, :, :], yt[:, s, :, :], sc[0:NT, ISX:ISX + 1], ROUND, ALU.mult, ALU.add
                                    ).then_inc(rounded[s], 1)
                    v.wait_ge(rounded[s], it + 1)
                    v.wait_ge(turned[s], it)
                    v.tensor_scalar(yq[:, s, :, :], big[:, s, :, :], ROUND, None, ALU.subtract).then_inc(yq_ready[s], 1)

                def maxima(it):
                    for t in range(6):
                        v.wait_ge(product, it * 6 + (t + 1))
                        ins = v.tensor_reduce(tile_max[:, t, :], pj[0:NT, 3 * (t % 2):3 * (t % 2) + 3, 0:D], AX.X, ALU.max,
                                              apply_absolute_value=True)
                        ins.then_inc(reduced, 1)
                    v.wait_ge(reduced, it * 6 + 6)
                    chain(v.tensor_tensor(run_max[:, :, :], run_max[:, :, :], tile_max[:, :, :], ALU.max))

                for s in range(2):
                    quantize(0, s)
                with v.Fori(0, B // 2 - 1) as it:
                    chain.loop(it, 1)
                    for s in range(2):
                        quantize(it + 1, s)
                    maxima(it)
                chain.end(B // 2 - 1)
                maxima(B // 2 - 1)
                chain(v.tensor_reduce(C["qkvmax"][0:NT, :], run_max[:, :, :].rearrange("p t c -> p c t"), AX.X, ALU.max))

            @block.scalar
            def _(act):
                act.preload_act_table(ACT.Copy)
                act.wait_ge(ones_set, 1)

                def take(it, s):
                    act.wait_ge(turned[s], it + 1)
                    act.wait_ge(stored[s], it * 32)
                    for k in range(2):
                        K = (128, D2)[k]
                        ins = act.activation(yT[0:K, s, k, 0:N].rearrange("c (p i) -> c i p", i=3),
                                             pt[s][0:K, k, :, 0:NT], ACT.Copy)
                    ins.then_inc(yT_ready[s], 1)

                for s in range(2):
                    take(0, s)
                with act.Fori(0, B // 2 - 1) as it:
                    for s in range(2):
                        act.wait_ge(product, it * 6 + (3 * s + 3))
                        take(it + 1, s)

            @block.tensor
            def _(pe):

                def turn(it, s):
                    pe.wait_ge(yq_ready[s], it + 1)
                    pe.wait_ge(yT_ready[s], it)
                    for k in range(2):
                        K = (128, D2)[k]
                        for i in range(3):
                            ins = pe.transpose(pt[s][0:K, k, i, 0:NT], yq[:, s, i, 128 * k:128 * k + K],
                                               C["identb"][0:NT, 0:NT])
                    ins.then_inc(turned[s], 1)

                def products(it, s):
                    pe.wait_ge(yT_ready[s], it + 1)
                    for i in range(3):
                        t = 3 * s + i
                        if t >= 2:
                            pe.wait_ge(reduced, it * 6 + (t - 1))
                        else:
                            pe.wait_ge(reduced, it * 6)
                        for c in range(3):
                            for k in range(2):
                                K = 128
                                ins = pe.matmul(pj[0:NT, 3 * (t % 2) + c, 0:D], yT[0:K, s, k, i * NT:(i + 1) * NT],
                                                wint[0:K, k, c * D:(c + 1) * D], start=(k == 0), stop=(k == 1))
                        ins.then_inc(product, 1)

                for s in range(2):
                    turn(0, s)
                with pe.Fori(0, B // 2 - 1) as it:
                    for s in range(2):
                        products(it, s)
                        turn(it + 1, s)
                for s in range(2):
                    products(B // 2 - 1, s)


def head_scales(nc, T, C):
    sc = C["sc"]
    with ExitStack() as ctx:
        m = Mem(nc, ctx, "hs")
        gx = m.sb("gx", [128, 3])
        gx_ready = m.sem("gx_ready")
        vchain = m.sem("vchain")
        with nc.Block() as block:

            @block.gpsimd
            def _(pool):
                pool.partition_all_reduce(gx[:, :], C["qkvmax"][:, :], 128, RMAX).then_inc(gx_ready, 1)

            @block.vector
            def _(v):
                chain = Chain(v, vchain)
                one = lambda i: sc[:, i:i + 1]
                three = lambda i: sc[:, i:i + 3]
                v.wait_ge(gx_ready, 1)
                chain(v.tensor_scalar(three(TMP), gx[:, :], one(SXW), None, ALU.mult))
                chain(v.tensor_scalar(three(SQKV), three(TMP), 1.0 / QMAX, SCALE_FLOOR, ALU.mult, ALU.max))
                chain(v.reciprocal(three(IQKV), three(SQKV)))
                v.tensor_scalar(three(AQKV), three(IQKV), one(SXW), None, ALU.mult)
                chain(v.tensor_scalar(one(ALPHA), one(SQKV), one(SQKV + 1), float(DH) ** -0.5, ALU.mult, ALU.mult))
                v.reciprocal(one(IALPHA), one(ALPHA))


def qkv_phase(nc, T, C):
    L = N - 256
    sc, wint, wqk = C["sc"], C["wint"], C["wqkp"]
    with ExitStack() as ctx:
        m = Mem(nc, ctx, "qk")
        yT = m.sb("yT", [128, 2, 2, NE], BF16)
        yL = m.sb("yL", [128, 2, 2, 4, 32], BF16)
        qkb = m.sb("qkb", [128, 2, 2, 3, NE])
        qko = m.sb("qko", [128, 2, 2, 3, NE], BF16)
        vb = m.sb("vb", [128, 2, 3, D])
        vo = m.sb("vo", [128, 2, 3, D], BF16)
        kround = m.sb("kround", [128, 1])
        rounding = m.sb("rounding", [128, 1])
        ps = m.ps("ps", [128, 8, 512])
        loaded = [m.sem(f"loaded{s}") for s in range(2)]
        left_ready = [m.sem(f"left_ready{s}") for s in range(2)]
        q_mm, k_mm = m.sem("q_mm"), m.sem("k_mm")
        v_mm = [m.sem(f"v_mm{s}") for s in range(2)]
        q_out, k_out, v_out = m.sem("q_out"), m.sem("k_out"), m.sem("v_out")
        qk_ready = [m.sem(f"qk_ready{s}") for s in range(2)]
        v_ready = [m.sem(f"v_ready{s}") for s in range(2)]
        qk_stored = [m.sem(f"qk_stored{s}") for s in range(2)]
        v_stored = [m.sem(f"v_stored{s}") for s in range(2)]
        const_set = m.sem("const_set")
        ones_set = m.sem("ones_set")
        k_loaded = m.sem("k_loaded")
        with nc.Block() as block:

            @block.sync
            def _(sp):
                sp.dma_start(kround[:, :], T["kround"]).then_inc(k_loaded, 16)
                sp.wait_ge(ones_set, 1)

                def load(it, s):
                    sp.wait_ge(v_mm[s], it)
                    sp.dma_start(yT[:, s, 0, :], T["YQ"][bass.ds((it * 2 + s) * D, 128), :]).then_inc(loaded[s], 16)
                    sp.dma_start(yT[0:D2, s, 1, :], T["YQ"][bass.ds((it * 2 + s) * D + 128, D2), :]).then_inc(loaded[s], 16)

                def store(it, s):
                    sp.wait_ge(qk_ready[s], it * 2 + 2)
                    sp.dma_start(T["QK"][:, :, bass.ds((it * 2 + s) * (3 * NE), 3 * NE)].rearrange("a p n -> p a n"),
                                 qko[:, s, :, :, :].rearrange("p a g n -> p a (g n)")).then_inc(qk_stored[s], 16)
                    sp.wait_ge(v_ready[s], it + 1)
                    sp.dma_start(T["V"][bass.ts(it * 2 + s, 128), :], vo[:, s, :, :].rearrange("p t d -> p (t d)")
                                 ).then_inc(v_stored[s], 16)

                for s in range(2):
                    load(0, s)
                with sp.Fori(0, B // 2 - 1) as it:
                    for s in range(2):
                        load(it + 1, s)
                        store(it, s)
                for s in range(2):
                    store(B // 2 - 1, s)
                for s in range(2):
                    sp.wait_ge(qk_stored[s], 8 * B)
                    sp.wait_ge(v_stored[s], 8 * B)

            @block.gpsimd
            def _(pool):
                pool.memset(yL[:, :, :, :, :], 0.0).then_inc(const_set, 1)
                pool.wait_ge(const_set, 4)
                with pool.Fori(0, B // 2) as it:
                    for s in range(2):
                        pool.wait_ge(loaded[s], it * 32 + 32)
                        pool.wait_ge(v_mm[s], it)
                        pool_copy(pool, yL[:, s, :, :, 0:L], yT[:, s, :, 256:N].unsqueeze(2).to_broadcast([128, 2, 4, L]), C["one"][:, :]
                                         ).then_inc(left_ready[s], 1)

            @block.scalar
            def _(act):
                aq, ak = act.alloc_register("scale_q"), act.alloc_register("scale_k")
                act.reg_load(aq, sc[0:1, AQKV:AQKV + 1].bitcast(U32))
                act.reg_load(ak, sc[0:1, AQKV + 1:AQKV + 2].bitcast(U32))
                act.preload_act_table(ACT.Identity)
                act.wait_ge(const_set, 4)
                with act.Fori(0, B // 2) as it:
                    for s in range(2):
                        act.wait_ge(qk_ready[s], it * 2)
                        for a, (mm, out, r) in enumerate(((q_mm, q_out, aq), (k_mm, k_out, ak))):
                            act.wait_ge(mm, it * 2 + (s + 1))
                            act.activation(qkb[:, s, a, :, 0:N], ps[:, 3 * a:3 * a + 3, 0:N], ACT.Identity,
                                           scale=r, bias=rounding[:, 0:1]).then_inc(out, 1)

            @block.vector
            def _(v):
                v.memset(rounding[:, :], ROUND).then_inc(const_set, 1)
                v.memset(qko[:, :, :, :, :], 0.0).then_inc(const_set, 1)
                v.memset(yT[:, :, :, :], 0.0).then_inc(const_set, 1)
                v.wait_ge(const_set, 4)
                v.memset(yT[D2:D2 + 3, :, 1, :], 1.0).then_inc(ones_set, 1)
                v.wait_ge(k_loaded, 16)
                with v.Fori(0, B // 2) as it:
                    for s in range(2):
                        v.wait_ge(qk_stored[s], it * 16)
                        v.wait_ge(q_out, it * 2 + (s + 1))
                        v.tensor_scalar(qko[:, s, 0, :, 0:N], qkb[:, s, 0, :, 0:N], ROUND, None, ALU.subtract
                                        ).then_inc(qk_ready[s], 1)
                        v.wait_ge(k_out, it * 2 + (s + 1))
                        v.tensor_scalar(qko[:, s, 1, :, 0:N], qkb[:, s, 1, :, 0:N], kround[:, 0:1], None, ALU.subtract
                                        ).then_inc(qk_ready[s], 1)
                        v.wait_ge(v_mm[s], it + 1)
                        v.tensor_scalar(vb[:, s, 0:2, :], ps[:, 6, 0:2 * D].rearrange("p (t d) -> p t d", t=2),
                                        sc[:, AQKV + 2:AQKV + 3], ROUND, ALU.mult, ALU.add)
                        v.tensor_scalar(vb[:, s, 2, :], ps[:, 7, 0:D], sc[:, AQKV + 2:AQKV + 3], ROUND, ALU.mult, ALU.add
                                        ).then_inc(v_out, 1)
                        v.wait_ge(v_out, it * 2 + (s + 1))
                        v.wait_ge(v_stored[s], it * 16)
                        v.tensor_scalar(vo[:, s, :, :], vb[:, s, :, :], ROUND, None, ALU.subtract).then_inc(v_ready[s], 1)

            @block.tensor
            def _(pe):
                pe.wait_ge(ones_set, 1)
                with pe.Fori(0, B // 2) as it:
                    for s in range(2):
                        pe.wait_ge(loaded[s], it * 32 + 32)
                        for a, (mm, out) in enumerate(((q_mm, q_out), (k_mm, k_out))):
                            pe.wait_ge(out, it * 2 + s)
                            for g in range(3):
                                for k in range(2):
                                    K = 128
                                    ins = pe.matmul(ps[:, 3 * a + g, 0:N],
                                                    wqk[0:K, k, 12 * a + 4 * g:12 * a + 4 * g + 4, :].rearrange("c j n -> c (j n)"),
                                                    yT[0:K, s, k, 0:N], start=(k == 0), stop=(k == 1))
                            ins.then_inc(mm, 1)
                        pe.wait_ge(v_out, it * 2 + s)
                        pe.wait_ge(left_ready[s], it + 1)
                        for t in range(3):
                            for k in range(2):
                                K = 128
                                lhsT = (yT[0:K, s, k, t * 128:(t + 1) * 128] if t < 2 else
                                        yL[0:K, s, k, :, :].rearrange("c j n -> c (j n)"))
                                ins = pe.matmul(ps[:, 6 + t // 2, (t % 2) * D:(t % 2) * D + D], lhsT,
                                                wint[0:K, k, 2 * D:3 * D], start=(k == 0), stop=(k == 1),
                                                skip_group_check=True)
                        ins.then_inc(v_mm[s], 1)


def tiles_of_sample():
    pairs = [[(g, t, j), (g, t, j + 1)] for g in range(3) for t in range(2) for j in (0, 2)]
    return pairs + [[(0, 2, 0), (1, 2, 0)], [(2, 2, 0)]]


def row_phase(nc, T, C):
    L = N - 256
    sc = C["sc"]
    PAIRS = tiles_of_sample()
    NP = len(PAIRS)
    col = lambda g, t, j: g * 9 + t * 4 + j
    with ExitStack() as ctx:
        m = Mem(nc, ctx, "rw")
        qk = m.sb("qk", [128, 2, 2, 3, NE], BF16)
        qL = m.sb("qL", [128, 2, 3, 4, 32], BF16)
        nm = m.sb("nm", [128, 2, 27])
        nb = m.sb("nb", [128, 2, 27])
        zz = m.sb("zz", [128, 2, 27])
        ps = m.ps("ps", [128, 8, 512])
        loaded = [m.sem(f"loaded{s}") for s in range(2)]
        left_ready = [m.sem(f"left_ready{s}") for s in range(2)]
        scored = [m.sem(f"scored{n}") for n in range(4)]
        maxed = m.sem("maxed")
        biased = m.sem("biased")
        summed = [m.sem(f"summed{n}") for n in range(4)]
        pchain = m.sem("pchain")
        kept = [m.sem(f"kept{s}") for s in range(2)]
        zeroed = m.sem("zeroed")
        with nc.Block() as block:

            @block.sync
            def _(sp):
                with sp.Fori(0, B // 2) as it:
                    for s in range(2):
                        sp.wait_ge(kept[s], it * 2)
                        sp.dma_start(qk[:, s, :, :, :].rearrange("p a g n -> p a (g n)"),
                                     T["QK"][:, :, bass.ds((it * 2 + s) * (3 * NE), 3 * NE)].rearrange("a p n -> p a n")
                                     ).then_inc(loaded[s], 16)

            @block.gpsimd
            def _(pool):
                pool.memset(qL[:, :, :, :, :], 0.0).then_inc(zeroed, 1)
                pool.wait_ge(zeroed, 1)
                chain = Chain(pool, pchain)
                with pool.Fori(0, B // 2) as it:
                    chain.loop(it, 6)
                    for s in range(2):
                        pool.wait_ge(loaded[s], it * 16 + 16)
                        for j in range(4):
                            ins = pool_copy(pool, qL[32 * j:32 * j + 32, s, :, j, 0:L], qk[32 * j:32 * j + 32, s, 0, :, 256:N],
                                            C["one"][32 * j:32 * j + 32, :])
                            if j < 3:
                                chain(ins)
                        ins.then_inc(left_ready[s], 1)
                        pool.wait_ge(left_ready[s], it + 1)
                    for s in range(2):
                        n = 14 * s + 13
                        pool.wait_ge(summed[n % 4], it * 7 + (n // 4 + 1))
                        pool_copy(pool, C["nmax"][:, bass.ds((it * 2 + s) * 27, 27)], nm[:, s, :], C["one"][:, :]).then_inc(kept[s], 1)
                        pool_copy(pool, C["zsum"][:, bass.ds((it * 2 + s) * 27, 27)], zz[:, s, :], C["one"][:, :]).then_inc(kept[s], 1)
                chain.end(B // 2)

            @block.tensor
            def _(pe):
                with pe.Fori(0, B // 2) as it:
                    for s in range(2):
                        for p, pair in enumerate(PAIRS):
                            n = NP * s + p
                            bank = 2 * (n % 4)
                            if p == 0:
                                pe.wait_ge(loaded[s], it * 16 + 16)
                            if p == 12:
                                pe.wait_ge(left_ready[s], it + 1)
                            pe.wait_ge(summed[n % 4], it * 7 + n // 4)
                            for c, (g, t, j) in enumerate(pair):
                                if t < 2:
                                    r = slice(32 * j, 32 * j + 32)
                                    ins = pe.matmul(ps[:, bank + c, 0:N], qk[r, s, 0, g, t * 128:(t + 1) * 128],
                                                    qk[r, s, 1, g, 0:N], start=True, stop=True)
                                else:
                                    ins = pe.matmul(ps[:, bank + c, 0:N], qL[:, s, g, :, :].rearrange("p j n -> p (j n)"),
                                                    qk[:, s, 1, g, 0:N], start=True, stop=True)
                            ins.then_inc(scored[n % 4], 1)

            @block.vector
            def _(v):
                with v.Fori(0, B // 2) as it:
                    for s in range(2):
                        v.wait_ge(kept[s], it * 2)
                        for p, pair in enumerate(PAIRS):
                            n = NP * s + p
                            bank = 2 * (n % 4)
                            c0, w = col(*pair[0]), len(pair)
                            at = slice(c0, c0 + 1) if w == 1 else slice(c0, col(*pair[1]) + 1, col(*pair[1]) - c0)
                            v.wait_ge(scored[n % 4], it * 7 + (n // 4 + 1))
                            v.tensor_reduce(nm[:, s, at], ps[:, bank:bank + w, 0:N], AX.X, ALU.max, negate=True
                                            ).then_inc(maxed, 1)
                            v.wait_ge(maxed, it * 28 + (n + 1))
                            v.tensor_scalar(nb[:, s, at], nm[:, s, at], sc[:, ALPHA:ALPHA + 1], None, ALU.mult
                                            ).then_inc(biased, 1)

            @block.scalar
            def _(act):
                alpha = act.alloc_register("alpha1")
                act.reg_load(alpha, sc[0:1, ALPHA:ALPHA + 1].bitcast(U32))
                act.preload_act_table(ACT.Exp)
                with act.Fori(0, B // 2) as it:
                    for s in range(2):
                        act.wait_ge(kept[s], it * 2)
                        for p, pair in enumerate(PAIRS):
                            n = NP * s + p
                            bank = 2 * (n % 4)
                            act.wait_ge(biased, it * 28 + (n + 1))
                            for c, t in enumerate(pair):
                                i = col(*t)
                                ins = act.activation(ps[:, bank + c, 0:N], ps[:, bank + c, 0:N], ACT.Exp,
                                                     bias=nb[:, s, i:i + 1], scale=alpha, accum_out=zz[:, s, i:i + 1])
                            ins.then_inc(summed[n % 4], 1)


def row_offsets(nc, T, C):
    L = N - 256
    GROUP = 108
    NG = B * 27 // GROUP
    sc = C["sc"]
    one = lambda i: sc[:, i:i + 1]
    with ExitStack() as ctx:
        m = Mem(nc, ctx, "ro")
        zmin = m.sb("zmin", [128, 1])
        gx = m.sb("gx", [128, 1])
        lnz = m.sb("lnz", [128, B * 27])
        off = m.sb("off", [128, B * 27])
        rest = m.sb("rest", [GROUP, 2, NG, 128])
        parts = m.sb("parts", [GROUP, NG, 3, 128], BF16)
        ps = m.ps("ps", [128, 2, 4, 128])
        zmin_ready = m.sem("zmin_ready")
        gx_ready = m.sem("gx_ready")
        scale_ready = m.sem("scale_ready")
        ln_ready = m.sem("ln_ready")
        off_ready = m.sem("off_ready")
        turned = m.sem("turned")
        parts_ready = m.sem("parts_ready")
        staged = m.sem("staged")
        placed = m.sem("placed")
        vchain = m.sem("vchain")
        with nc.Block() as block:

            @block.gpsimd
            def _(pool):
                pool.wait_ge(zmin_ready, 1)
                pool.partition_all_reduce(gx[:, :], zmin[:, :], 128, RMAX).then_inc(gx_ready, 1)

            @block.scalar
            def _(act):
                act.activation(lnz[:, :], C["zsum"][:, :], ACT.Ln).then_inc(ln_ready, 1)
                act.wait_ge(scale_ready, 1)
                act.activation(one(LNSP), one(SP_), ACT.Ln).then_inc(ln_ready, 1)

            @block.vector
            def _(v):
                chain = Chain(v, vchain)
                chain(v.tensor_reduce(gx[:, :], C["zsum"][:, :], AX.X, ALU.min))
                v.tensor_scalar(zmin[:, :], gx[:, :], -1.0, None, ALU.mult).then_inc(zmin_ready, 1)
                v.wait_ge(gx_ready, 1)
                chain(v.tensor_scalar(one(TMP), gx[:, :], -1.0, None, ALU.mult))
                chain(v.reciprocal(one(TMP + 1), one(TMP)))
                chain(v.tensor_scalar(one(SP_), one(TMP + 1), 1.0 / QMAX, SCALE_FLOOR, ALU.mult, ALU.max))
                v.tensor_scalar(one(TMP + 2), one(IALPHA), -1.0, None, ALU.mult)
                v.tensor_tensor(one(SO_IN), one(SP_), one(SQKV + 2), ALU.mult).then_inc(scale_ready, 1)
                v.wait_ge(ln_ready, 2)
                v.wait_ge(scale_ready, 1)
                chain(v.tensor_scalar(lnz[:, :], lnz[:, :], one(LNSP), one(TMP + 2), ALU.add, ALU.mult))
                v.tensor_tensor(off[:, :], lnz[:, :], C["nmax"][:, :], ALU.add).then_inc(off_ready, 1)
                v.wait_ge(turned, 1)
                t = ps[0:GROUP, :, :, :].rearrange("p a b n -> p (a b) n")
                chain(v.tensor_copy(parts[:, :, 0, :], t))
                chain(v.tensor_tensor(rest[:, 0, :, :], t, parts[:, :, 0, :], ALU.subtract))
                chain(v.tensor_copy(parts[:, :, 1, :], rest[:, 0, :, :]))
                v.tensor_tensor(parts[:, :, 2, :], rest[:, 0, :, :], parts[:, :, 1, :], ALU.subtract
                                ).then_inc(parts_ready, 1)

            @block.tensor
            def _(pe):
                pe.wait_ge(off_ready, 1)
                for g in range(NG):
                    ins = pe.transpose(ps[0:GROUP, g // 4, g % 4, :], off[:, g * GROUP:(g + 1) * GROUP], C["ident"][:, :])
                ins.then_inc(turned, 1)

            @block.sync
            def _(sp):
                sp.wait_ge(parts_ready, 1)
                sp.dma_start(T["OFF"].rearrange("(g p) r n -> p g (r n)", p=GROUP),
                             parts[:, :, :, :].rearrange("p g r n -> p g (r n)")).then_inc(staged, 16)
                sp.wait_ge(staged, 16)
                src = T["OFF"].rearrange("(m c) r n -> c r m n", c=9)
                for j in range(4):
                    rows = T["QK"][0, 32 * j + DH:32 * j + DH + 3, :].rearrange("r (m n) -> r m n", n=NE)
                    for t in range(2):
                        sp.dma_start(rows[:, :, t * 128:(t + 1) * 128], src[t * 4 + j]).then_inc(placed, 16)
                    sp.dma_start(rows[:, :, 256:N], src[8, :, :, 32 * j:32 * j + L]).then_inc(placed, 16)
                sp.wait_ge(placed, 16 * 12)


def product_phase(nc, T, C):
    L = N - 256
    sc = C["sc"]
    tiles = [(g, t, j) for g in range(3) for t in (0, 1, 2) for j in (range(4) if t < 2 else [0])]
    UNITS = len(tiles) // 3
    A_LAST = UNITS * 2 // 3 - 1
    LAST = B // 2 - 1
    with ExitStack() as ctx:
        m = Mem(nc, ctx, "pr")
        q = m.sb("q", [128, 2, 3, NE], BF16)
        k = m.sb("k", [128, 2, 4, 3, NE], BF16)
        kL = m.sb("kL", [128, 2, 3, 4, 32], BF16)
        vt = m.sb("vt", [128, 2, 3, D], BF16)
        va = m.sb("va", [128, 2, 2, 8 * (128 + DH)], BF16)
        vb = m.sb("vb", [128, 2, 2, 4 * (64 + DH)], BF16)
        vL = m.sb("vL", [128, 2, 3 * 192], BF16)
        e = m.sb("e", [128, 3, 3, NE])
        p = m.sb("p", [128, 3, 3, NE], BF16)
        o = m.sb("o", [128, 2, 2, N])
        mx = m.sb("mx", [128, 2, 2])
        ps = m.ps("ps", [128, 8, 512])
        qk_loaded = [m.sem(f"qk_loaded{s}") for s in range(2)]
        v_loaded = [m.sem(f"v_loaded{s}") for s in range(2)]
        kL_ready = [m.sem(f"kL_ready{s}") for s in range(2)]
        v_ready = [m.sem(f"v_ready{s}") for s in range(2)]
        scored = [m.sem(f"scored{n}") for n in range(2)]
        exp_done = [m.sem(f"exp_done{n}") for n in range(2)]
        rounded = [m.sem(f"rounded{n}") for n in range(3)]
        used = [m.sem(f"used{n}") for n in range(3)]
        a_taken = m.sem("a_taken")
        b_taken = [m.sem(f"b_taken{s}") for s in range(2)]
        cls_kept = [m.sem(f"cls_kept{s}") for s in range(2)]
        o_stored = [m.sem(f"o_stored{s}") for s in range(2)]
        zeroed = m.sem("zeroed")
        k_zeroed = m.sem("k_zeroed")
        pchain, vchain = m.sem("pchain"), m.sem("vchain")
        before = lambda it, w: it * UNITS + w // 2
        before3 = lambda it, w: it * (UNITS * 2 // 3) + w // 3
        with nc.Block() as block:

            @block.sync
            def _(sp):

                def load(it, s):
                    at = bass.ds((it * 2 + s) * (3 * NE), 3 * NE)
                    for j in range(4):
                        r = slice(32 * j, 32 * j + 32)
                        sp.dma_start(k[r, s, j, :, :].rearrange("p g n -> p (g n)"), T["QK"][1, r, at]
                                     ).then_inc(qk_loaded[s], 16)
                    sp.dma_start(q[:, s, :, :].rearrange("p g n -> p (g n)"), T["QK"][0, :, at]).then_inc(qk_loaded[s], 16)
                    sp.dma_start(vt[:, s, :, :].rearrange("p t d -> p (t d)"), T["V"][bass.ts(it * 2 + s, 128), :]
                                 ).then_inc(v_loaded[s], 16)

                def store(it, s):
                    sp.wait_ge(b_taken[s], it + 1)
                    sp.dma_start(T["OT"][0:128, bass.ts(it * 2 + s, N)], o[:, s, 0, :]).then_inc(o_stored[s], 16)
                    sp.dma_start(T["OT"][128:D, bass.ts(it * 2 + s, N)], o[0:D2, s, 1, :]).then_inc(o_stored[s], 16)

                sp.wait_ge(k_zeroed, 1)
                for s in range(2):
                    load(0, s)
                with sp.Fori(0, LAST) as it:
                    for s in range(2):
                        w = UNITS * s + UNITS - 1
                        sp.wait_ge(scored[w % 2], before(it, w) + 1)
                        load(it + 1, s)
                        store(it, s)
                for s in range(2):
                    store(LAST, s)
                for s in range(2):
                    sp.wait_ge(o_stored[s], 16 * B)

            @block.gpsimd
            def _(pool):
                chain = Chain(pool, pchain)
                pool.memset(k[:, :, :, :, :], 0.0).then_inc(k_zeroed, 1)
                pool.wait_ge(k_zeroed, 1)
                chain(pool.memset(kL[:, :, :, :, :], 0.0))
                chain(pool.memset(va[:, :, :, :], 0.0))
                chain(pool.memset(vb[:, :, :, :], 0.0))
                pool.memset(vL[:, :, :], 0.0).then_inc(zeroed, 1)
                pool.wait_ge(zeroed, 1)

                def build(it, s):
                    pool.wait_ge(qk_loaded[s], it * 80 + 80)
                    for j in range(4):
                        r = slice(32 * j, 32 * j + 32)
                        ins = pool_copy(pool, kL[r, s, :, j, 0:L], k[r, s, j, :, 256:N], C["one"][r, :])
                        if j < 3:
                            chain(ins)
                    ins.then_inc(kL_ready[s], 1)
                    pool.wait_ge(kL_ready[s], it + 1)
                    pool.wait_ge(v_loaded[s], it * 16 + 16)
                    if not isinstance(it, int):
                        w = UNITS * s + UNITS - 1
                        pool.wait_ge(used[w % 3], before3(it - 1, w) + 1)
                    chain(pool_copy(pool, va[:, s, :, :].rearrange("p t (h c) -> p t h c", h=8)[:, :, :, 0:DH],
                                           vt[:, s, 0:2, 0:128].rearrange("p t (h d) -> p t h d", d=DH), C["one"][:, :]))
                    chain(pool_copy(pool, vb[:, s, :, :].rearrange("p t (h c) -> p t h c", h=4)[:, :, :, 0:DH],
                                           vt[:, s, 0:2, 128:D].rearrange("p t (h d) -> p t h d", d=DH), C["one"][:, :]))
                    for j in range(4):
                        r = slice(32 * j, 32 * j + 32)
                        ins = pool_copy(pool, vL[r, s, :].rearrange("p (g c) -> p g c", g=3)[:, :, 16 * j:16 * j + DH],
                                               vt[r, s, 2, :].rearrange("p (g j d) -> p g j d", g=3, j=4)[:, :, j, :], C["one"][r, :])
                        if j < 3:
                            chain(ins)
                    ins.then_inc(v_ready[s], 1)
                    pool.wait_ge(v_ready[s], it + 1)

                def keep_cls(it, s):
                    pool.wait_ge(b_taken[s], it + 1)
                    pool_copy(pool, C["ocls"][:, :, :, bass.ds(it * 2 + s, 1)], o[:, s, :, 0:NCLS].unsqueeze(3), C["one"][:, :]
                                     ).then_inc(cls_kept[s], 1)
                    pool.wait_ge(cls_kept[s], it + 1)

                for s in range(2):
                    build(0, s)
                with pool.Fori(0, LAST) as it:
                    chain.loop(it, 2 * 8)
                    for s in range(2):
                        build(it + 1, s)
                        keep_cls(it, s)
                chain.end(LAST)
                for s in range(2):
                    keep_cls(LAST, s)

            @block.tensor
            def _(pe):

                def score(it, w):
                    if w >= 2 * UNITS:
                        it, w = it + 1, w - 2 * UNITS
                    s, u = w // UNITS, w % UNITS
                    if u == 0:
                        pe.wait_ge(qk_loaded[s], it * 80 + 80)
                    if u == 2:
                        pe.wait_ge(kL_ready[s], it + 1)
                    if not (isinstance(it, int) and it == 0 and w < 2):
                        pe.wait_ge(exp_done[w % 2], before(it, w))
                    for c in range(3):
                        g, t, j = tiles[3 * u + c]
                        out = ps[:, 3 * (w % 2) + c, 0:N]
                        keys = k[:, s, j, g, t * 128:(t + 1) * 128] if t < 2 else kL[:, s, g, :, :].rearrange("p j n -> p (j n)")
                        ins = pe.matmul(out, keys, q[:, s, g, 0:N], start=True, stop=True)
                    ins.then_inc(scored[w % 2], 1)

                def times_v(it, w):
                    s, u = w // UNITS, w % UNITS
                    if u == 0:
                        pe.wait_ge(v_ready[s], it + 1)
                        pe.wait_ge(a_taken, it * 2 + s)
                    if u == A_LAST + 1:
                        pe.wait_ge(b_taken[1 - s], it + s)
                    pe.wait_ge(rounded[w % 3], before3(it, w) + 1)
                    for c in range(3):
                        n = 3 * u + c
                        g, t, j = tiles[n]
                        probs = p[:, w % 3, c, 0:N]
                        if g < 2:
                            h = 4 * g + j
                            v = va[:, s, t, 128 * h:128 * h + 128] if t < 2 else vL[:, s, 128 * g:128 * g + 128]
                            ins = pe.matmul(ps[:, 6, 0:N], v, probs, start=(n == 0), stop=(n == 3 * A_LAST + 2))
                        else:
                            v = vb[:, s, t, 64 * j:64 * j + 64] if t < 2 else vL[:, s, 384:448]
                            ins = pe.matmul(ps[0:64, 7, 0:N], v, probs, start=(n == 3 * A_LAST + 3),
                                            stop=(n == len(tiles) - 1))
                    ins.then_inc(used[w % 3], 1)

                def step(it, last):
                    for w in range(2 * UNITS):
                        if not (last and w + 3 >= 2 * UNITS):
                            score(it, w + 3)
                        times_v(it, w)

                for w in range(3):
                    score(0, w)
                with pe.Fori(0, LAST) as it:
                    step(it, False)
                step(LAST, True)

            @block.scalar
            def _(act):
                alpha = act.alloc_register("alpha2")
                act.reg_load(alpha, sc[0:1, ALPHA:ALPHA + 1].bitcast(U32))
                act.preload_act_table(ACT.Exp)
                with act.Fori(0, B // 2) as it:
                    for w in range(2 * UNITS):
                        at = w % 2
                        act.wait_ge(scored[at], before(it, w) + 1)
                        act.wait_ge(rounded[w % 3], before3(it, w))
                        act.activation(e[:, w % 3, :, 0:N], ps[:, 3 * at:3 * at + 3, 0:N], ACT.Exp, scale=alpha
                                       ).then_inc(exp_done[at], 1)

            @block.vector
            def _(v):
                chain = Chain(v, vchain)
                chain(v.memset(o[D2:128, :, 1, :], 0.0))
                chain(v.memset(mx[:, :, :], 0.0))
                chain(v.memset(C["omax"][:, :], 0.0))

                def round_unit(it, w):
                    if w >= 2 * UNITS:
                        it, w = it + 1, w - 2 * UNITS
                    at = w % 3
                    v.wait_ge(exp_done[w % 2], before(it, w) + 1)
                    v.wait_ge(used[at], before3(it, w))
                    v.tensor_scalar(p[:, at, :, 0:N], e[:, at, :, 0:N], ROUND, ROUND, ALU.add, ALU.subtract
                                    ).then_inc(rounded[at], 1)

                def take_a(it, s):
                    w = UNITS * s + A_LAST
                    v.wait_ge(used[w % 3], before3(it, w) + 1)
                    v.wait_ge(o_stored[s], it * 32)
                    v.wait_ge(cls_kept[s], it)
                    v.tensor_reduce(mx[:, s, 0:1], ps[:, 6, 0:N], AX.X, ALU.max, apply_absolute_value=True)
                    v.tensor_copy(o[:, s, 0, :], ps[:, 6, 0:N]).then_inc(a_taken, 1)

                def take_b(it, s):
                    w = UNITS * s + UNITS - 1
                    v.wait_ge(used[w % 3], before3(it, w) + 1)
                    v.tensor_reduce(mx[0:64, s, 1:2], ps[0:64, 7, 0:N], AX.X, ALU.max, apply_absolute_value=True)
                    v.tensor_copy(o[0:64, s, 1, :], ps[0:64, 7, 0:N]).then_inc(b_taken[s], 1)
                    v.wait_ge(b_taken[s], it + 1)
                    chain(v.tensor_tensor(C["omax"][:, :], C["omax"][:, :], mx[:, s, :], ALU.max))

                def step(it, last):
                    for w in range(2, 2 * UNITS + (0 if last else 2)):
                        round_unit(it, w)
                        if w % UNITS == A_LAST + 2:
                            take_a(it, w // UNITS)
                        if w % UNITS == 1:
                            take_b(it, w // UNITS - 1)

                round_unit(0, 0)
                round_unit(0, 1)
                with v.Fori(0, LAST) as it:
                    chain.loop(it, 2)
                    step(it, False)
                chain.end(LAST)
                step(LAST, True)
                take_b(LAST, 1)


GROUP_TOKENS = 336
GP = GROUP_TOKENS // 3
GROUPS = TOKENS // GROUP_TOKENS


def output_scales(nc, T, C):
    sc = C["sc"]
    one = lambda i: sc[:, i:i + 1]
    with ExitStack() as ctx:
        m = Mem(nc, ctx, "os")
        w1 = m.sb("w1", [128, 2, F])
        w2 = m.sb("w2", [128, FT, D])
        scaled1 = m.sb("scaled1", [128, 2, F])
        scaled2 = m.sb("scaled2", [128, FT, D])
        mx = m.sb("mx", [128, 4])
        gx = m.sb("gx", [128, 4])
        loaded = m.sem("loaded")
        mx_ready = m.sem("mx_ready")
        gx_ready = m.sem("gx_ready")
        vchain = m.sem("vchain")
        with nc.Block() as block:

            @block.sync
            def _(sp):
                sp.dma_start(w1[:, :, :], T["mw1"]).then_inc(loaded, 16)
                sp.dma_start(w2[:, :, :], T["mw2"].rearrange("(k p) d -> p k d", p=128)).then_inc(loaded, 16)
                sp.dma_start(C["b1"][:, :], T["mb1"]).then_inc(loaded, 16)
                sp.wait_ge(loaded, 48)

            @block.gpsimd
            def _(pool):
                pool.wait_ge(mx_ready, 1)
                pool.partition_all_reduce(gx[:, :], mx[:, :], 128, RMAX).then_inc(gx_ready, 1)

            @block.vector
            def _(v):
                chain = Chain(v, vchain)
                v.tensor_reduce(mx[:, 0:1], C["omax"][:, :], AX.X, ALU.max)
                v.wait_ge(loaded, 48)
                v.tensor_reduce(mx[:, 1:2], w1[:, :, :], AX.XY, ALU.max, apply_absolute_value=True)
                v.tensor_reduce(mx[:, 2:3], w2[:, :, :], AX.XY, ALU.max, apply_absolute_value=True)
                v.tensor_reduce(mx[:, 3:4], C["b1"][:, :], AX.X, ALU.max, apply_absolute_value=True).then_inc(mx_ready, 1)
                v.wait_ge(gx_ready, 1)
                chain(v.tensor_scalar(one(TMP), gx[:, 0:1], one(SO_IN), None, ALU.mult))
                chain(v.tensor_scalar(one(SOUT), one(TMP), 1.0 / QMAX, SCALE_FLOOR, ALU.mult, ALU.max))
                chain(v.reciprocal(one(ISOUT), one(SOUT)))
                v.tensor_tensor(one(HOUT), one(SOUT), one(SX + 2), ALU.mult)
                v.tensor_tensor(one(AOUT), one(ISOUT), one(SO_IN), ALU.mult)
                v.tensor_scalar(one(UW1), gx[:, 1:2], 1.0 / 1024.0, 1e-30, ALU.mult, ALU.max)
                v.tensor_scalar(one(UW2), gx[:, 2:3], 1.0 / 1024.0, 1e-30, ALU.mult, ALU.max)
                chain(v.scalar_tensor_tensor(out=one(TMP), in0=gx[:, 1:2], scalar=float(D), in1=gx[:, 3:4],
                                             op0=ALU.mult, op1=ALU.add))
                chain(v.tensor_scalar(one(TMP + 1), one(TMP), 1.0 / 32768.0, 1e-30, ALU.mult, ALU.max))
                v.reciprocal(one(SW1), one(UW1))
                v.reciprocal(one(SW2), one(UW2))
                chain(v.reciprocal(one(SHID), one(TMP + 1)))
                chain(v.tensor_tensor(one(UW2), one(UW2), one(TMP + 1), ALU.mult))
                v.tensor_scalar(scaled1[:, :, :], w1[:, :, :], one(SW1), None, ALU.mult)
                chain(v.tensor_scalar(scaled2[:, :, :], w2[:, :, :], one(SW2), None, ALU.mult))
                v.tensor_copy(C["w1h"][:, :, :], scaled1[:, :, :])
                chain(v.tensor_copy(C["w2h"][:, :, :], scaled2[:, :, :]))
                v.tensor_tensor(C["w1l"][:, :, :], scaled1[:, :, :], C["w1h"][:, :, :], ALU.subtract)
                chain(v.tensor_tensor(C["w2l"][:, :, :], scaled2[:, :, :], C["w2h"][:, :, :], ALU.subtract))


def output_phase(nc, T, C):
    sc = C["sc"]
    G = GROUP_TOKENS
    LOOP = (GROUPS - 4) // 2
    with ExitStack() as ctx:
        m = Mem(nc, ctx, "out")
        rows = m.sb("rows", [GP, 2, D])
        rounding = m.sb("rounding", [128, 1])
        ot = m.sb("ot", [128, 2, 2, G])
        big = m.sb("big", [128, 2, 3, GP])
        oq = m.sb("oq", [128, 2, 2, 3, GP], BF16)
        hin = m.sb("hin", [GP, 2, 3, D])
        hb = m.sb("hb", [GP, 2, 3, D])
        h2 = m.sb("h2", [GP, 2, 3, D])
        h2b = m.sb("h2b", [GP, 2, 3, D])
        bn = m.sb("bn", [GP, 3, 6])
        mv = m.sb("mv", [GP, 3, 2])
        var = m.sb("var", [GP, 3])
        rstd = m.sb("rstd", [GP, 3])
        y = m.sb("y", [GP, 3, 256])
        yh = m.sb("yh", [128, 2, G], F16)
        yl = m.sb("yl", [128, G], F16)
        act_out = m.sb("act_out", [128, FT, G])
        hh = m.sb("hh", [128, FT, G], F16)
        hl = m.sb("hl", [128, FT, G], F16)
        gap = m.sb("gap", [1, 1])
        out = m.sb("out", [GP, 2, 3, D])
        ps = m.ps("ps", [128, 8, 512])
        w_loaded = m.sem("w_loaded")
        ot_loaded = [m.sem(f"ot_loaded{s}") for s in range(2)]
        hin_loaded = [m.sem(f"hin_loaded{s}") for s in range(2)]
        const_set = m.sem("const_set")
        big_done = m.sem("big_done")
        oq_ready = m.sem("oq_ready")
        proj_mm = m.sem("proj_mm")
        hb_ready = m.sem("hb_ready")
        h2_done = m.sem("h2_done")
        h2b_ready = m.sem("h2b_ready")
        var_ready = m.sem("var_ready")
        rstd_ready = m.sem("rstd_ready")
        y_ready = m.sem("y_ready")
        turned = m.sem("turned")
        yT_ready = m.sem("yT_ready")
        fc1_mm = m.sem("fc1_mm")
        gelu_done = m.sem("gelu_done")
        split_done = m.sem("split_done")
        highs = m.sem("highs")
        high_ready = m.sem("high_ready")
        fc2_mm = m.sem("fc2_mm")
        out_done = m.sem("out_done")
        stored = [m.sem(f"stored{s}") for s in range(2)]
        vchain = m.sem("vchain")

        def exists(it, s, k):
            return not isinstance(it, int) or 2 * it + s + k < GROUPS

        def steps(eng, body):
            with eng.Fori(0, LOOP) as it:
                for s in range(2):
                    body(it, s)
            for it in range(LOOP, GROUPS // 2):
                for s in range(2):
                    body(it, s)

        with nc.Block() as block:

            @block.sync
            def _(sp):
                sp.dma_start(rows[:, :, :].rearrange("p r d -> p (r d)"),
                             T["rows"][0, 8 * D:10 * D].partition_broadcast(GP)).then_inc(w_loaded, 16)

                def load(it, s, k):
                    q, m = (s + k) % 2, it * 2 + (s + k)
                    if not (isinstance(m, int) and m < 2):
                        sp.wait_ge(big_done, m - 1)
                        sp.wait_ge(hb_ready, m - 1)
                    sp.dma_start(ot[:, q, 0, :], T["OT"][0:128, bass.ts(m, G)]).then_inc(ot_loaded[q], 16)
                    sp.dma_start(ot[0:D2, q, 1, :], T["OT"][128:D, bass.ts(m, G)]).then_inc(ot_loaded[q], 16)
                    sp.dma_start(hin[:, q, :, :].rearrange("p i d -> p (i d)"),
                                 T["H"].rearrange("(r i) d -> r (i d)", i=3)[bass.ts(m, GP), :]).then_inc(hin_loaded[q], 16)

                sp.wait_ge(const_set, 2)
                for k in range(2):
                    load(0, 0, k)
                sp.dma_start(C["a1"][:, :, :], T["a1"]).then_inc(C["experts_loaded"], 16)
                sp.dma_start(C["a2"][:, :, :], T["a2"].rearrange("(k p) d -> p k d", p=128)).then_inc(C["experts_loaded"], 16)
                for k in range(2, 4):
                    load(0, 0, k)

                def body(it, s):
                    if exists(it, s, 4):
                        load(it, s, 4)
                    sp.wait_ge(out_done, it * 2 + (s + 1))
                    sp.dma_start(T["out"].rearrange("(r i) d -> r (i d)", i=3)[bass.ts(it * 2 + s, GP), :],
                                 out[:, s, :, :].rearrange("p i d -> p (i d)")).then_inc(stored[s], 16)

                steps(sp, body)
                for s in range(2):
                    sp.wait_ge(stored[s], 8 * GROUPS)
                sp.wait_ge(C["experts_loaded"], 32)

            @block.gpsimd
            def _(pool):
                pool.wait_ge(w_loaded, 16)

                def with_bias(it, s, k):
                    q, m = (s + k) % 2, it * 2 + (s + k)
                    pool.wait_ge(hin_loaded[q], it * 16 + (s + k) // 2 * 16 + 16)
                    if not (isinstance(m, int) and m < 2):
                        pool.wait_ge(h2_done, m - 1)
                    pool.tensor_tensor(hb[:, q, :, :], hin[:, q, :, :],
                                       rows[:, 0:1, :].to_broadcast([GP, 3, D]), ALU.add).then_inc(hb_ready, 1)

                def norm(it, s, k):
                    q, m = (s + k) % 2, it * 2 + (s + k)
                    pool.wait_ge(var_ready, m + 1)
                    pool.tensor_tensor(rstd[:, :], var[:, :], C["nhalf"][0:GP, 0:3], ALU.pow).then_inc(rstd_ready, 1)
                    if not (isinstance(m, int) and m < 2):
                        pool.wait_ge(out_done, m - 1)
                    pool.tensor_tensor(h2b[:, q, :, :], h2[:, q, :, :], rows[:, 1:2, :].to_broadcast([GP, 3, D]), ALU.add
                                       ).then_inc(h2b_ready, 1)

                with_bias(0, 0, 0)
                with_bias(0, 0, 1)
                norm(0, 0, 0)

                def body(it, s):
                    if exists(it, s, 1):
                        norm(it, s, 1)
                    if exists(it, s, 2):
                        with_bias(it, s, 2)

                steps(pool, body)

            @block.scalar
            def _(act):
                aout = act.alloc_register("scale_out")
                act.reg_load(aout, sc[0:1, AOUT:AOUT + 1].bitcast(U32))
                uw1 = act.alloc_register("undo_w1")
                act.reg_load(uw1, sc[0:1, UW1:UW1 + 1].bitcast(U32))
                shid = act.alloc_register("scale_hidden")
                act.reg_load(shid, sc[0:1, SHID:SHID + 1].bitcast(U32))
                act.preload_act_table(ACT.Gelu)
                act.wait_ge(w_loaded, 16)
                act.wait_ge(const_set, 2)

                def enlarge(it, s, k):
                    q, m = (s + k) % 2, it * 2 + (s + k)
                    act.wait_ge(ot_loaded[q], it * 32 + (s + k) // 2 * 32 + 32)
                    if not (isinstance(m, int) and m < 1):
                        act.wait_ge(oq_ready, m)
                    for kk in range(2):
                        ins = act.activation(big[:, kk, :, :], ot[:, q, kk, :].rearrange("c (p i) -> c i p", i=3),
                                             ACT.Identity, scale=aout, bias=rounding[:, 0:1])
                    ins.then_inc(big_done, 1)

                def take_turned(it, s, k):
                    act.wait_ge(turned, it * 2 + (s + k + 1))
                    act.activation(yh[:, 0, :], ps[:, 2, 0:G], ACT.Copy)
                    act.activation(yh[:, 1, :], ps[:, 3, 0:G], ACT.Copy).then_inc(high_ready, 1)

                enlarge(0, 0, 0)
                enlarge(0, 0, 1)
                take_turned(0, 0, 0)

                def body(it, s):
                    if exists(it, s, 2):
                        enlarge(it, s, 2)
                    act.wait_ge(split_done, it * (2 * FT) + s * FT)
                    for f in range(FT):
                        act.wait_ge(fc1_mm, it * (2 * FT) + (s * FT + f + 1))
                        act.activation(act_out[:, f, :], ps[:, 4 + f % 2, 0:G], ACT.Gelu, bias=C["b1"][:, f:f + 1],
                                       scale=uw1).then_inc(gelu_done, 1)
                        if f == 0:
                            act.wait_ge(fc2_mm, it * 2 + s)
                        act.wait_ge(gelu_done, it * (2 * FT) + (s * FT + f + 1))
                        act.activation(hh[:, f, :], act_out[:, f, :], ACT.Copy, scale=shid).then_inc(highs, 1)
                    if exists(it, s, 1):
                        take_turned(it, s, 1)

                steps(act, body)

            @block.tensor
            def _(pe):
                pe.wait_ge(w_loaded, 16)
                place = lambda first, i: ps[0:GP, first + i // 2, (i % 2) * D:(i % 2) * D + D]

                def project(it, s, k):
                    q, m = (s + k) % 2, it * 2 + (s + k)
                    pe.wait_ge(oq_ready, m + 1)
                    if not (isinstance(m, int) and m < 1):
                        pe.wait_ge(h2_done, m)
                    for i in range(3):
                        for kk in range(2):
                            K = (128, D2)[kk]
                            ins = pe.matmul(place(0, i), oq[0:K, q, kk, i, :], C["wpint"][0:K, kk, :],
                                            start=(kk == 0), stop=(kk == 1), skip_group_check=True)
                    ins.then_inc(proj_mm, 1)

                def turn(it, s, k):
                    m = it * 2 + (s + k)
                    pe.wait_ge(y_ready, m + 1)
                    if not (isinstance(m, int) and m < 1):
                        pe.wait_ge(yT_ready, m)
                    for kk in range(2):
                        for i in range(3):
                            ins = pe.transpose(ps[:, 2 + kk, i * GP:(i + 1) * GP], y[:, i, 128 * kk:128 * kk + 128],
                                               C["ident"][0:GP, 0:GP])
                    ins.then_inc(turned, 1)

                project(0, 0, 0)
                turn(0, 0, 0)

                def body(it, s):
                    n = it * 2 + s
                    if exists(it, s, 1):
                        project(it, s, 1)
                    pe.wait_ge(yT_ready, n + 1)
                    for f in range(FT):
                        if f >= 2:
                            pe.wait_ge(gelu_done, it * (2 * FT) + (s * FT + f - 1))
                        at = slice(f * 128, (f + 1) * 128)
                        pairs = [(C["w1h"][:, 0, at], yh[:, 0, :]), (C["w1h"][:, 0, at], yl[:, :]),
                                 (C["w1h"][:, 1, at], yh[:, 1, :]), (C["w1l"][:, 0, at], yh[:, 0, :]),
                                 (C["w1l"][0:D2, 1, at], yh[0:D2, 1, :])]
                        for n5, (w, src) in enumerate(pairs):
                            ins = pe.matmul(ps[:, 4 + f % 2, 0:G], w, src, start=(n5 == 0), stop=(n5 == len(pairs) - 1))
                        ins.then_inc(fc1_mm, 1)
                    if exists(it, s, 1):
                        turn(it, s, 1)
                    pe.wait_ge(out_done, n)
                    for f in range(FT):
                        pe.wait_ge(split_done, it * (2 * FT) + (s * FT + f + 1))
                        for i in range(3):
                            at = slice(i * GP, (i + 1) * GP)
                            for part, (h, w) in enumerate(((hh, "w2h"), (hl, "w2h"), (hh, "w2l"))):
                                ins = pe.matmul(place(6, i), h[:, f, at], C[w][:, f, :],
                                                start=(f == 0 and part == 0 and i != 1),
                                                stop=(f == FT - 1 and part == 2), skip_group_check=True)
                    ins.then_inc(fc2_mm, 1)

                steps(pe, body)

            @block.vector
            def _(v):
                chain = Chain(v, vchain)
                v.memset(rounding[:, :], ROUND).then_inc(const_set, 1)
                v.memset(ot[:, :, :, :], 0.0).then_inc(const_set, 1)
                v.wait_ge(w_loaded, 16)

                def quantize(it, s, k):
                    q, m = (s + k) % 2, it * 2 + (s + k)
                    v.wait_ge(big_done, m + 1)
                    if not (isinstance(m, int) and m < 2):
                        v.wait_ge(proj_mm, m - 1)
                    v.tensor_scalar(oq[:, q, :, :, :], big[:, :, :, :], ROUND, None, ALU.subtract).then_inc(oq_ready, 1)

                def both(first, t, q):
                    two = ps[0:GP, first, 0:2 * D].rearrange("p (i d) -> p i d", i=2)
                    return (two, t[:, q, 0:2, :]), (ps[0:GP, first + 1:first + 2, 0:D], t[:, q, 2:3, :])

                def norm(it, s, k):
                    q, m = (s + k) % 2, it * 2 + (s + k)
                    v.wait_ge(proj_mm, m + 1)
                    v.wait_ge(hb_ready, m + 1)
                    if not (isinstance(m, int) and m < 2):
                        v.wait_ge(h2b_ready, m - 1)
                    for (src, dst), (_, add) in zip(both(0, h2, q), both(0, hb, q)):
                        ins = v.scalar_tensor_tensor(out=dst, in0=src, scalar=sc[0:GP, HOUT:HOUT + 1], in1=add,
                                                     op0=ALU.mult, op1=ALU.add)
                    ins.then_inc(h2_done, 1)
                    v.wait_ge(h2_done, m + 1)
                    for i in range(3):
                        ins = v.bn_stats(bn[:, i, :], h2[:, q, i, :])
                    chain(ins)
                    v.memset(gap[:, :], 0.0)
                    for i in range(3):
                        ins = v.bn_aggr(mv[:, i, :], bn[:, i, :])
                    chain(ins)
                    v.tensor_scalar(var[:, :], mv[:, :, 1], EPS, None, ALU.add).then_inc(var_ready, 1)

                def scale_norm(it, s, k):
                    q, m = (s + k) % 2, it * 2 + (s + k)
                    if not (isinstance(m, int) and m < 1):
                        v.wait_ge(turned, m)
                    v.wait_ge(rstd_ready, m + 1)
                    for i in range(3):
                        for dst, src in ((slice(0, D), slice(0, D)), (slice(D, 256), slice(128, D))):
                            ins = v.tensor_scalar(y[:, i, dst], h2[:, q, i, src], mv[:, i, 0:1], rstd[:, i:i + 1],
                                                  ALU.subtract, ALU.mult)
                    ins.then_inc(y_ready, 1)

                def low_parts(it, s, k):
                    v.wait_ge(high_ready, it * 2 + (s + k + 1))
                    v.tensor_tensor(yl[:, :], ps[:, 2, 0:G], yh[:, 0, :], ALU.subtract)
                    v.tensor_tensor(yh[D2:128, 1, :], ps[D2:128, 3, 0:G], yh[D2:128, 1, :], ALU.subtract
                                    ).then_inc(yT_ready, 1)

                def split(it, s, fs):
                    for f in fs:
                        v.wait_ge(highs, it * (2 * FT) + (s * FT + f + 1))
                        v.scalar_tensor_tensor(out=hl[:, f, :], in0=act_out[:, f, :], scalar=sc[:, SHID:SHID + 1],
                                               in1=hh[:, f, :], op0=ALU.mult, op1=ALU.subtract).then_inc(split_done, 1)

                quantize(0, 0, 0)
                quantize(0, 0, 1)
                norm(0, 0, 0)
                scale_norm(0, 0, 0)
                low_parts(0, 0, 0)

                def body(it, s):
                    if exists(it, s, 1):
                        norm(it, s, 1)
                    split(it, s, range(1))
                    if exists(it, s, 1):
                        scale_norm(it, s, 1)
                    split(it, s, range(1, FT))
                    if exists(it, s, 1):
                        low_parts(it, s, 1)
                    if exists(it, s, 2):
                        quantize(it, s, 2)
                    n = it * 2 + s
                    v.wait_ge(fc2_mm, n + 1)
                    v.wait_ge(h2b_ready, n + 1)
                    v.wait_ge(stored[s], it * 16)
                    for (src, dst), (_, add) in zip(both(6, out, s), both(6, h2b, s)):
                        ins = v.scalar_tensor_tensor(out=dst, in0=src, scalar=sc[0:GP, UW2:UW2 + 1], in1=add,
                                                     op0=ALU.mult, op1=ALU.add)
                    ins.then_inc(out_done, 1)

                with v.Fori(0, LOOP) as it:
                    chain.loop(it, 4)
                    for s in range(2):
                        body(it, s)
                chain.end(LOOP)
                for it in range(LOOP, GROUPS // 2):
                    for s in range(2):
                        body(it, s)


def class_phase(nc, T, C):
    sc = C["sc"]
    P, E, A = 3 * B, 2, 3
    with ExitStack() as ctx:
        m = Mem(nc, ctx, "cl")
        b1 = m.sb("b1", [128, 5 * FT])
        gw = m.sb("gw", [128, 2, 2 * NCLS])
        a2b = m.sb("a2b", [P, 2, E, D])
        bp = m.sb("bp", [P, D])
        hin = m.sb("hin", [P, E, D])
        hb = m.sb("hb", [P, E, D])
        rounding = m.sb("rounding", [128, 1])
        big = m.sb("big", [128, 2, E * P])
        oq = m.sb("oq", [128, 2, E * P], BF16)
        h2 = m.sb("h2", [P, E, D])
        bn = m.sb("bn", [P, E, 6])
        mv = m.sb("mv", [P, E, 2])
        var = m.sb("var", [P, E])
        rstd = m.sb("rstd", [P, E])
        y = m.sb("y", [P, E, D])
        yT = m.sb("yT", [128, 2, E * P])
        hid = m.sb("hid", [128, 2, FT, E * P])
        lg = m.sb("lg", [P, E, 2])
        lx = m.sb("lx", [P, E, 2])
        le = m.sb("le", [P, E, 2])
        gate = m.sb("gate", [P, E, 2])
        kept = m.sb("kept", [P, E, 2])
        final = m.sb("final", [P, E, 2])
        mask = m.sb("mask", [P, E, 2])
        r1 = m.sb("r1", [P, 4, E])
        res = m.sb("res", [P, 2, E, D])
        out = m.sb("out", [P, 2, E, D])
        ps = m.ps("ps", [128, 8, 512])
        loaded = m.sem("loaded")
        const_set = m.sem("const_set")
        big_done = m.sem("big_done")
        oq_ready = m.sem("oq_ready")
        proj_mm = m.sem("proj_mm")
        var_ready = m.sem("var_ready")
        rstd_ready = m.sem("rstd_ready")
        y_ready = m.sem("y_ready")
        turned = m.sem("turned")
        yT_ready = m.sem("yT_ready")
        gates_mm = m.sem("gates_mm")
        gates_out = m.sem("gates_out")
        less_max = m.sem("less_max")
        gate_exp = m.sem("gate_exp")
        fc1_mm = m.sem("fc1_mm")
        gelu_done = m.sem("gelu_done")
        fc2_mm = m.sem("fc2_mm")
        out_ready = m.sem("out_ready")
        stored = m.sem("stored")
        vchain = m.sem("vchain")
        by_sample = lambda t: t.rearrange("(b n) d -> b n d", b=B)
        NLOAD = 3 + 2 + 3 * E + NCLS
        with nc.Block() as block:

            @block.sync
            def _(sp):
                for a in range(A):
                    for e in range(E):
                        sp.dma_start(hin[B * a:B * a + B, e, :], by_sample(T["H"])[:, 2 * a + e, :]).then_inc(loaded, 16)
                sp.dma_start(b1[:, :], T["a1b"]).then_inc(loaded, 16)
                sp.dma_start(gw[:, :, :], T["gw"]).then_inc(loaded, 16)
                sp.dma_start(bp[:, :], T["rows"][0, 8 * D:9 * D].partition_broadcast(P)).then_inc(loaded, 16)
                for e in range(E):
                    sp.dma_start(a2b[:, 0, e, :], T["a2b"][3 + e, :].partition_broadcast(P)).then_inc(loaded, 16)
                    for a in range(A):
                        sp.dma_start(a2b[B * a:B * a + B, 1, e, :], T["a2b"][a, :].partition_broadcast(B)).then_inc(loaded, 16)
                sp.wait_ge(out_ready, 1)
                for a in range(A):
                    for e in range(E):
                        sp.dma_start(by_sample(T["out"])[:, 2 * a + e, :], out[B * a:B * a + B, 1, e, :]).then_inc(stored, 16)
                sp.wait_ge(stored, 16 * NCLS)

            @block.gpsimd
            def _(pool):
                pool.wait_ge(var_ready, 1)
                pool.tensor_tensor(rstd[:, :], var[:, :], C["nhalf"][0:P, 0:E], ALU.pow).then_inc(rstd_ready, 1)

            @block.scalar
            def _(act):
                aout = act.alloc_register("scale_out_c")
                act.reg_load(aout, sc[0:1, AOUT:AOUT + 1].bitcast(U32))
                act.preload_act_table(ACT.Gelu)
                act.wait_ge(const_set, 1)
                act.wait_ge(loaded, 16 * NLOAD)
                for e in range(E):
                    ins = act.activation(big[:, :, e * P:(e + 1) * P].rearrange("p k (a b) -> p k a b", a=A),
                                         C["ocls"][:, :, :, :].rearrange("p k (a e) b -> p k e a b", e=E)[:, :, e, :, :],
                                         ACT.Identity, scale=aout, bias=rounding[:, 0:1])
                ins.then_inc(big_done, 1)
                act.wait_ge(turned, 1)
                act.activation(yT[:, 0, :], ps[:, 2, 0:E * P], ACT.Copy)
                act.activation(yT[0:D2, 1, :], ps[0:D2, 3, 0:E * P], ACT.Copy).then_inc(yT_ready, 1)
                act.wait_ge(less_max, 1)
                act.activation(le[:, :, :], lx[:, :, :], ACT.Exp).then_inc(gate_exp, 1)
                act.preload_act_table(ACT.Gelu)
                for f in range(FT):
                    for pair in range(2):
                        n = 2 * f + pair
                        act.wait_ge(fc1_mm, n + 1)
                        src, dst = ps[:, 4 + n % 4, 0:E * P], hid[:, pair, f, :]
                        if pair == 0:
                            split = lambda t: t.rearrange("p (e a b) -> p a e b", e=E, a=A)
                            for a in range(A):
                                ins = act.activation(split(dst)[:, a, :, :], split(src)[:, a, :, :], ACT.Gelu,
                                                     bias=b1[:, a * FT + f:a * FT + f + 1])
                        else:
                            for e in range(E):
                                x = (3 + e) * FT + f
                                ins = act.activation(dst[:, e * P:(e + 1) * P], src[:, e * P:(e + 1) * P], ACT.Gelu,
                                                     bias=b1[:, x:x + 1])
                        ins.then_inc(gelu_done, 1)

            @block.tensor
            def _(pe):
                pe.wait_ge(loaded, 16 * NLOAD)
                pe.wait_ge(oq_ready, 1)
                for e in range(E):
                    for k in range(2):
                        K = (128, D2)[k]
                        ins = pe.matmul(ps[0:P, 0, e * D:(e + 1) * D], oq[0:K, k, e * P:(e + 1) * P], C["wpint"][0:K, k, :],
                                        start=(k == 0), stop=(k == 1), skip_group_check=True)
                ins.then_inc(proj_mm, 1)
                pe.wait_ge(y_ready, 1)
                for k in range(2):
                    K = (128, D2)[k]
                    for e in range(E):
                        ins = pe.transpose(ps[0:K, 2 + k, e * P:(e + 1) * P], y[:, e, 128 * k:128 * k + K], C["ident"][0:P, 0:P])
                ins.then_inc(turned, 1)
                pe.wait_ge(yT_ready, 1)
                for e in range(E):
                    for k in range(2):
                        K = (128, D2)[k]
                        ins = pe.matmul(ps[0:P, 1, 16 * e:16 * e + 2 * NCLS], yT[0:K, k, e * P:(e + 1) * P], gw[0:K, k, :],
                                        start=(k == 0), stop=(k == 1), skip_group_check=True)
                ins.then_inc(gates_mm, 1)
                for f in range(FT):
                    for pair in range(2):
                        n = 2 * f + pair
                        if n >= 4:
                            pe.wait_ge(gelu_done, n - 3)
                        out4 = ps[:, 4 + n % 4, 0:E * P]
                        split = lambda t: t.rearrange("p (e a b) -> p a e b", e=E, a=A)
                        for x in range(A if pair == 0 else E):
                            ex = x if pair == 0 else 3 + x
                            for k in range(2):
                                K = (128, D2)[k]
                                w = C["a1"][0:K, k, ex * F + f * 128:ex * F + (f + 1) * 128]
                                if pair == 0:
                                    dst, src = split(out4)[:, x, :, :], split(yT[0:K, k, :])[:, x, :, :]
                                else:
                                    dst, src = out4[:, x * P:(x + 1) * P], yT[0:K, k, x * P:(x + 1) * P]
                                ins = pe.matmul(dst, w, src, start=(k == 0), stop=(k == 1), skip_group_check=True)
                        ins.then_inc(fc1_mm, 1)
                pe.wait_ge(gelu_done, 2 * FT)
                pe.wait_ge(gates_out, 1)
                for e in range(E):
                    for f in range(FT):
                        ins = pe.matmul(ps[0:P, 0, e * D:(e + 1) * D], hid[:, 0, f, e * P:(e + 1) * P],
                                        C["a2"][:, (3 + e) * FT + f, :], start=(f == 0), stop=(f == FT - 1), skip_group_check=True)
                for a in range(A):
                    for e in range(E):
                        for f in range(FT):
                            ins = pe.matmul(ps[0:P, 1 + a, e * D:(e + 1) * D], hid[:, 1, f, e * P:(e + 1) * P],
                                            C["a2"][:, a * FT + f, :], start=(f == 0), stop=(f == FT - 1), skip_group_check=True)
                ins.then_inc(fc2_mm, 1)

            @block.vector
            def _(v):
                chain = Chain(v, vchain)
                v.memset(rounding[:, :], ROUND).then_inc(const_set, 1)
                v.wait_ge(loaded, 16 * NLOAD)
                two = ps[0:P, 0, 0:E * D].rearrange("p (e d) -> p e d", e=E)
                chain(v.tensor_tensor(hb[:, :, :], hin[:, :, :], bp[:, :].unsqueeze(1).to_broadcast([P, E, D]), ALU.add))
                v.wait_ge(big_done, 1)
                v.tensor_scalar(oq[:, :, :], big[:, :, :], ROUND, None, ALU.subtract).then_inc(oq_ready, 1)
                v.wait_ge(proj_mm, 1)
                chain(v.scalar_tensor_tensor(out=h2[:, :, :], in0=two, scalar=sc[0:P, HOUT:HOUT + 1], in1=hb[:, :, :],
                                             op0=ALU.mult, op1=ALU.add))
                for e in range(E):
                    ins = v.bn_stats(bn[:, e, :], h2[:, e, :])
                chain(ins)
                for e in range(E):
                    ins = v.bn_aggr(mv[:, e, :], bn[:, e, :])
                chain(ins)
                v.tensor_scalar(var[:, :], mv[:, :, 1], EPS, None, ALU.add).then_inc(var_ready, 1)
                v.wait_ge(rstd_ready, 1)
                for e in range(E):
                    ins = v.tensor_scalar(y[:, e, :], h2[:, e, :], mv[:, e, 0:1], rstd[:, e:e + 1], ALU.subtract, ALU.mult)
                ins.then_inc(y_ready, 1)
                v.wait_ge(gates_mm, 1)
                for a in range(A):
                    r = slice(B * a, B * a + B)
                    ins = v.tensor_copy(lg[r, :, :], ps[r, 1, 0:36].rearrange("p (e x) -> p e x", x=18)[:, :, 4 * a:4 * a + 2])
                ins.then_inc(gates_out, 1)
                v.wait_ge(gates_out, 1)
                wide = lambda i: r1[:, i, :].unsqueeze(2).to_broadcast([P, E, 2])
                chain(v.tensor_reduce(r1[:, 0, :], lg[:, :, :], AX.X, ALU.max))
                v.tensor_tensor(lx[:, :, :], lg[:, :, :], wide(0), ALU.subtract).then_inc(less_max, 1)
                v.wait_ge(gate_exp, 1)
                chain(v.tensor_reduce(r1[:, 1, :], le[:, :, :], AX.X, ALU.add))
                chain(v.reciprocal(r1[:, 2, :], r1[:, 1, :]))
                chain(v.tensor_tensor(gate[:, :, :], le[:, :, :], wide(2), ALU.mult))
                chain(v.tensor_reduce(r1[:, 3, :], gate[:, :, :], AX.X, ALU.min))
                chain(v.tensor_tensor(mask[:, :, :], gate[:, :, :], wide(3), ALU.is_gt))
                chain(v.tensor_tensor(kept[:, :, :], gate[:, :, :], mask[:, :, :], ALU.mult))
                chain(v.tensor_reduce(r1[:, 0, :], kept[:, :, :], AX.X, ALU.add))
                chain(v.tensor_scalar(r1[:, 1, :], r1[:, 0, :], 1e-6, None, ALU.max))
                chain(v.reciprocal(r1[:, 2, :], r1[:, 1, :]))
                chain(v.tensor_tensor(final[:, :, :], kept[:, :, :], wide(2), ALU.mult))
                v.wait_ge(fc2_mm, 1)
                v.tensor_tensor(res[:, 0, :, :], two, a2b[:, 0, :, :], ALU.add)
                for a in range(A):
                    r = slice(B * a, B * a + B)
                    ins = v.tensor_tensor(res[r, 1, :, :], ps[r, 1 + a, 0:E * D].rearrange("p (e d) -> p e d", e=E),
                                          a2b[r, 1, :, :], ALU.add)
                chain(ins)
                for pair in range(2):
                    for e in range(E):
                        add = h2[:, e, :] if pair == 0 else out[:, 0, e, :]
                        ins = v.scalar_tensor_tensor(out=out[:, pair, e, :], in0=res[:, pair, e, :],
                                                     scalar=final[:, e, pair:pair + 1], in1=add, op0=ALU.mult, op1=ALU.add)
                    if pair == 0:
                        chain(ins)
                ins.then_inc(out_ready, 1)


def final_phases(nc, T, C):
    with ExitStack() as ctx:
        m = Mem(nc, ctx, "fin")
        C["a1"] = m.sb("a1", [128, 2, 5 * F])
        C["a2"] = m.sb("a2", [128, 5 * FT, D])
        C["b1"] = m.sb("b1", [128, FT])
        C["w1h"], C["w1l"] = m.sb("w1h", [128, 2, F], F16), m.sb("w1l", [128, 2, F], F16)
        C["w2h"], C["w2l"] = m.sb("w2h", [128, FT, D], F16), m.sb("w2l", [128, FT, D], F16)
        C["experts_loaded"] = m.sem("experts_loaded")
        output_scales(nc, T, C)
        output_phase(nc, T, C)
        class_phase(nc, T, C)


def setup(nc, T, C):
    with ExitStack() as ctx:
        m = Mem(nc, ctx, "se")
        tok = m.sb("tok", [NTXT, B], I32)
        tf = m.sb("tf", [NTXT, B])
        below = m.sb("below", [NTXT, B])
        tw = m.sb("tw", [NTXT, B])
        loaded = m.sem("loaded")
        vchain = m.sem("vchain")
        with nc.Block() as block:

            @block.sync
            def _(sp):
                sp.dma_start(tok[:, :], T["tok"]).then_inc(loaded, 16)
                sp.dma_start(C["ident"][:, :], T["ident"]).then_inc(loaded, 16)
                sp.wait_ge(loaded, 32)

            @block.vector
            def _(v):
                chain = Chain(v, vchain)
                v.memset(C["nhalf"][:, :], -0.5)
                v.memset(C["one"][:, :], 1.0)
                v.memset(C["half"][:, :], 0.5)
                v.memset(C["ymax_txt"][:, :], 0.0)
                v.wait_ge(loaded, 32)
                v.tensor_copy(C["identb"][:, :], C["ident"][:, :])
                chain(v.tensor_copy(tf[:, :], tok[:, :]))
                chain(v.tensor_scalar(below[:, :], tf[:, :], 0.0, float(VOCAB), ALU.is_lt, ALU.mult))
                chain(v.tensor_tensor(tw[:, :], tf[:, :], below[:, :], ALU.add))
                chain(v.tensor_scalar(tf[:, :], tw[:, :], 0.0, float(VOCAB - 1), ALU.max, ALU.min))
                chain(v.tensor_copy(C["idx"][:, :], tf[:, :]))


def program(nc, T):
    with ExitStack() as ctx:
        m = Mem(nc, ctx, "c")
        C = {}
        C["nhalf"], C["half"] = m.sb("nhalf", [128, 96]), m.sb("half", [128, 96])
        C["one"] = m.sb("one", [128, 1])
        C["ident"], C["identb"] = m.sb("ident", [128, 128]), m.sb("identb", [128, 128], BF16)
        C["ymax_img"], C["ymax_txt"] = m.sb("ymax_img", [128, 1]), m.sb("ymax_txt", [128, 1])
        C["sc"] = m.sb("sc", [128, NSC])
        C["qkvmax"], C["omax"] = m.sb("qkvmax", [128, 3]), m.sb("omax", [128, 2])
        C["wint"], C["wpint"] = m.sb("wint", [128, 2, 3 * D], BF16), m.sb("wpint", [128, 2, D], BF16)
        C["wqkp"] = m.sb("wqkp", [128, 2, 2 * HEADS, 32], BF16)
        C["nmax"], C["zsum"] = m.sb("nmax", [128, B * 27]), m.sb("zsum", [128, B * 27])
        C["ocls"] = m.sb("ocls", [128, 2, NCLS, B])
        with ExitStack() as first:
            C["idx"] = first.enter_context(nc.sbuf_tensor("c_idx", [NTXT, B], I32))
            C["emb"] = first.enter_context(nc.sbuf_tensor("c_emb", [NTXT, B, D], F32))
            setup(nc, T, C)
            image_phase(nc, T, C)
            text_phase(nc, T, C)
        scales(nc, T, C)
        quantize_phase(nc, T, C)
        head_scales(nc, T, C)
        qkv_phase(nc, T, C)
        row_phase(nc, T, C)
        row_offsets(nc, T, C)
        product_phase(nc, T, C)
        final_phases(nc, T, C)


SCRATCH = {"H": ((TOKENS, D), F32),
           "Y": ((TOKENS, D), F32),
           "YQ": ((B * D, NE), BF16),
           "QK": ((2, 128, B * 3 * NE), BF16),
           "V": ((B * 128, 3 * D), BF16),
           "OFF": ((B * 27, 3, 128), BF16),
           "OT": ((D, TOKENS), F32)}


def lay_out(np, inputs):
    take = lambda n: np.asarray(inputs[n])
    out = {}
    x = take("x")
    pix = counts()
    npix = len(pix)
    ys, xs = np.array([p[1] for p in pix]), np.array([p[2] for p in pix])
    xp = np.zeros((B, CH, IMG + 2, IMG + 2), x.dtype)
    xp[:, :, 1:-1, 1:-1] = x
    at = np.arange(GRID) * PATCH + 1
    cols = xp[:, :, at[:, None, None] + ys, at[None, :, None] + xs]
    cols = cols.reshape(B, CH, STEPS, IPT, TILES, npix).transpose(2, 4, 5, 1, 0, 3)
    cols = cols.reshape(STEPS * TILES, KT, KP, 128).transpose(0, 2, 1, 3)
    out["xcol"] = np.ascontiguousarray(cols).reshape(STEPS * TILES * KP, KT * 128)
    src = np.array([p[3] for p in pix])
    feat = np.where(src[:, None, :] >= 0, src[:, None, :] * 15 + np.arange(5) * CH + np.arange(CH)[:, None], FEAT)
    feat = feat.reshape(KT, KP, 5).transpose(1, 0, 2)
    pad = lambda a: np.concatenate([a, np.zeros((1,) + a.shape[1:], a.dtype)])
    out["wsh"] = pad(take("L0_tok_W"))[feat]
    out["gsh"] = pad(take("L0_tok_gamma"))[feat]
    out["bsh"] = pad(take("L0_tok_beta"))[feat]
    cnt = np.repeat([p[0] for p in pix], CH).reshape(KT, KP).T
    out["cntw"] = (cnt / FEAT).astype(np.float32)
    out["rootw"] = np.sqrt(cnt / FEAT).astype(np.float32)
    rows = ["L0_tok_b", "L0_txt_bv", "L0_txt_bo", "L0_txt_gamma1", "L0_txt_beta1", "L0_txt_b2", "L0_txt_gamma2",
            "L0_txt_beta2", "L0_attn_b_proj", "L0_ffn_moe0_b2"]
    out["rows"] = np.concatenate([take(r) for r in rows])[None, :]
    def two(a):
        t = np.zeros((2, 128, a.shape[1]), a.dtype)
        t[0], t[1, :D2] = a[:128], a[128:]
        return t.transpose(1, 0, 2)

    def spread(a):
        t = np.zeros(a.shape[:-1] + (3, 4, 32), a.dtype)
        t[..., :DH] = a.reshape(a.shape[:-1] + (3, 4, DH))
        return t.reshape(a.shape[:-1] + (384,))

    out["tok"] = take("x_txt").T
    out["emb"] = take("L0_txt_emb")
    wqk = np.stack([two(spread(take("L0_txt_wq"))), two(spread(take("L0_txt_wk")))], axis=2)
    out["wqk"] = wqk
    out["bqk"] = np.concatenate([spread(take("L0_txt_bq")).reshape(3, 128), spread(take("L0_txt_bk")).reshape(3, 128)]).T
    out["wv"], out["wo"], out["w1"] = two(take("L0_txt_wv")), two(take("L0_txt_wo")), two(take("L0_txt_w1"))
    out["b1"] = take("L0_txt_b1").reshape(FT, 128).T
    out["w2"] = take("L0_txt_w2")
    out["wqkv"], out["wproj"] = two(take("L0_attn_w_qkv")), two(take("L0_attn_w_proj"))
    out["bqkv"] = take("L0_attn_b_qkv")[None, :]
    t = np.full((4, 32), ROUND, np.float32)
    t[:, DH:DH + 3] -= 1.0
    out["kround"] = t.reshape(128, 1)
    place = np.arange(NTXT, dtype=np.float32)[:, None]
    i = np.arange(D, dtype=np.float32)[None, :]
    power = np.power(10000.0, (np.float32(2.0) * i / np.float32(D)).astype(np.float64)).astype(np.float32)
    ang = (place / power).astype(np.float64)
    out["pos"] = np.where(np.arange(D)[None, :] % 2 == 0, np.cos(ang), np.sin(ang)).astype(np.float32)
    out["ident"] = np.eye(128, dtype=np.float32)
    w1 = take("L0_ffn_moe0_W1")
    out["mw1"] = np.stack([w1[:128], np.concatenate([w1[128:], w1[128:]])], axis=1)
    out["mw2"] = take("L0_ffn_moe0_W2")
    out["mb1"] = take("L0_ffn_moe0_b1").reshape(FT, 128).T
    out["a1"] = two(take("L0_ffn_A1_W").transpose(1, 0, 2).reshape(D, 5 * F))
    out["a1b"] = take("L0_ffn_A1_b").reshape(5 * FT, 128).T
    out["a2"], out["a2b"] = take("L0_ffn_A2_W").reshape(5 * F, D), take("L0_ffn_A2_b")
    out["gw"] = two(take("L0_ffn_G_W").transpose(1, 0, 2).reshape(D, 2 * NCLS))
    return {k: np.ascontiguousarray(a) for k, a in out.items()}


def kernel(**inputs):
    import numpy as np
    import concourse.bacc as bacc
    from concourse import mybir
    from concourse.bass_utils import run_bass_kernel_spmd

    nc = bacc.Bacc("TRN2", target_bir_lowering=False, num_devices=1)
    T, arrays = {}, {}
    for name, a in lay_out(np, inputs).items():
        arrays["in_" + name] = a
        T[name] = nc.dram_tensor("in_" + name, a.shape, mybir.dt.from_np(a.dtype), kind="ExternalInput").ap()
    for name, (shape, dtype) in SCRATCH.items():
        T[name] = nc.dram_tensor("kept_" + name, shape, dtype).ap()
    T["out"] = nc.dram_tensor("out_0", (TOKENS, D), F32, kind="ExternalOutput").ap()
    program(nc, T)
    r = run_bass_kernel_spmd(nc, [arrays], core_ids=[0])
    return r.results[0]["out_0"].reshape(B, N, D)
```
